# Optimizing a Trainium2 kernel written in Bass

```python
import numpy as np
import jax
import jax.numpy as jnp

def _softmax(x, axis=-1):
    return jax.nn.softmax(x, axis=axis)

def _gelu(x):
    return jax.nn.gelu(x, approximate=True)

def _silu(x):
    return jax.nn.silu(x)

def _sigmoid(x):
    return jax.nn.sigmoid(x)

def _layernorm(x, axis=-1, eps=1e-05):
    m = jnp.mean(x, axis=axis, keepdims=True)
    v = jnp.var(x, axis=axis, keepdims=True)
    return (x - m) / jnp.sqrt(v + eps)

def _scatter_add(tgt, idx, src, axis=0):
    return tgt.at[idx].add(src)

def _segment_sum(src, seg, n):
    return jax.ops.segment_sum(src, seg, n)
kernel_name = 'mk_gnn_resnorm_d4_gnn_r8_4d13f4'

def setup_inputs(seed: int=0):
    np.random.seed(seed)
    _w = jnp.asarray

    def _rec_inputs():
        import jax
        import jax.numpy as jnp
        _gk = jax.random.key(seed)
        x = -0.000202 + 1 * jax.random.normal(jax.random.fold_in(_gk, 1), (6250, 128), jnp.float32)
        src = jax.random.randint(jax.random.fold_in(_gk, 2), (100000,), 0, 6250, jnp.int32)
        dst = jax.random.randint(jax.random.fold_in(_gk, 3), (100000,), 0, 6250, jnp.int32)
        _o = jnp.argsort(dst, stable=True)
        src = src[_o]
        dst = dst[_o]
        edge_attr_128 = 2.93046e-05 + 1.00006 * jax.random.normal(jax.random.fold_in(_gk, 12), (100000, 128), jnp.float32)
        edge_type_4 = jax.random.randint(jax.random.fold_in(_gk, 14), (100000,), 0, 4, jnp.int32)
        return (x, src, dst, edge_attr_128, edge_type_4)
    x, src, dst, edge_attr_128, edge_type_4 = _rec_inputs()

    def _L0_gnn_setup():
        import jax, jax.numpy as jnp
        import numpy as np
        N_NODES = 6250
        N_EDGES = 100000
        IN_CH = 128
        OUT_CH = 32
        HEADS = 4
        N_TYPES = 4
        N_CONF = 5
        key = jax.random.key(seed)
        ks = jax.random.split(key, 8)
        x = jax.random.normal(ks[0], (N_NODES, IN_CH), dtype=jnp.float32)
        edge_index = jax.random.randint(ks[1], (2, N_EDGES), 0, N_NODES, dtype=jnp.int32)
        edge_types = jax.random.randint(ks[2], (N_EDGES,), 0, N_TYPES, dtype=jnp.int32)
        D = OUT_CH * HEADS
        W = jax.random.normal(ks[3], (N_TYPES, IN_CH, D), dtype=jnp.float32) * (1.0 / np.sqrt(IN_CH))
        att_vectors = jax.random.normal(ks[4], (N_CONF, HEADS, 2 * OUT_CH), dtype=jnp.float32) * 0.1
        confounder_probs = jax.random.uniform(ks[5], (N_CONF,), dtype=jnp.float32)
        edge_importance = jnp.array([2.0, 1.5, 1.0, 0.5], dtype=jnp.float32)
        bias = jnp.zeros((D,), dtype=jnp.float32)
        return {'x': x, 'edge_index': edge_index, 'edge_types': edge_types, 'W': W, 'att_vectors': att_vectors, 'confounder_probs': confounder_probs, 'edge_importance': edge_importance, 'bias': bias}
    _L0_gnn_all = _L0_gnn_setup()
    _L0_gnn_in = {k: v for k, v in _L0_gnn_all.items() if k in ('W', 'att_vectors', 'confounder_probs', 'edge_importance', 'bias')}
    del _L0_gnn_all

    def _L1_gnn_setup():
        import jax, jax.numpy as jnp
        import numpy as np
        NEG_SLOPE = 0.2
        EPS = 1e-16
        N_NODES = 12500
        N_EDGES = 200000
        D = 128
        H = 4
        C = 32
        L = 3

        def _gat_layer(h, src, dst, Ws, Wd, a_s, a_d, bias):
            N = h.shape[0]
            xs = (h @ Ws).reshape(N, H, C)
            xd = (h @ Wd).reshape(N, H, C)
            alpha_s = jnp.sum(xs * a_s, axis=-1)
            alpha_d = jnp.sum(xd * a_d, axis=-1)
            e = alpha_s[src] + alpha_d[dst]
            e = jax.nn.leaky_relu(e, NEG_SLOPE)
            emax = jax.ops.segment_max(e, dst, num_segments=N)
            ex = jnp.exp(e - emax[dst])
            denom = jax.ops.segment_sum(ex, dst, num_segments=N)
            alpha = ex / (denom[dst] + EPS)
            msg = xs[src] * alpha[:, :, None]
            out = jax.ops.segment_sum(msg, dst, num_segments=N)
            return out.reshape(N, H * C) + bias
        key = jax.random.key(seed)
        ks = jax.random.split(key, 7)
        x = jax.random.normal(ks[0], (N_NODES, D), dtype=jnp.float32)
        edge_index = jax.random.randint(ks[1], (2, N_EDGES), 0, N_NODES, dtype=jnp.int32)
        scale = 1.0 / np.sqrt(D)
        Ws = jax.random.normal(ks[2], (L, D, H * C), dtype=jnp.float32) * scale
        Wd = jax.random.normal(ks[3], (L, D, H * C), dtype=jnp.float32) * scale
        att_s = jax.random.normal(ks[4], (L, H, C), dtype=jnp.float32) * scale
        att_d = jax.random.normal(ks[5], (L, H, C), dtype=jnp.float32) * scale
        b = jnp.zeros((L, H * C), dtype=jnp.float32)
        return {'x': x, 'edge_index': edge_index, 'Ws': Ws, 'Wd': Wd, 'att_s': att_s, 'att_d': att_d, 'b': b}
    _L1_gnn_all = _L1_gnn_setup()
    _L1_gnn_in = {k: v for k, v in _L1_gnn_all.items() if k in ('Ws', 'Wd', 'att_s', 'att_d', 'b')}
    del _L1_gnn_all

    def _L2_gnn_setup():
        import jax, jax.numpy as jnp
        import numpy as np
        N_NODES = 5000
        N_EDGES = 80000
        D_NODE = 128
        D_EDGE = 128
        HID = 256
        D_OUT = 128

        def _lin_params(key, d_in, d_out):
            k1, k2 = jax.random.split(key)
            bound = 1.0 / np.sqrt(d_in)
            W = jax.random.uniform(k1, (d_in, d_out), jnp.float32, -bound, bound)
            b = jax.random.uniform(k2, (d_out,), jnp.float32, -bound, bound)
            return (W, b)
        key = jax.random.key(seed)
        ks = jax.random.split(key, 10)
        x = jax.random.normal(ks[0], (N_NODES, D_NODE), jnp.float32)
        edge_index = jax.random.randint(ks[1], (2, N_EDGES), 0, N_NODES, jnp.int64)
        edge_attr = jax.random.normal(ks[2], (N_EDGES, D_EDGE), jnp.float32)
        u = jax.random.normal(ks[3], (1, 64), jnp.float32)
        batch = jnp.zeros((N_NODES,), jnp.int64)
        w1a, b1a = _lin_params(ks[4], D_NODE + D_EDGE, HID)
        w1b, b1b = _lin_params(ks[5], HID, HID)
        w1c, b1c = _lin_params(ks[6], HID, HID)
        w2a, b2a = _lin_params(ks[7], D_NODE + HID, HID)
        w2b, b2b = _lin_params(ks[8], HID, D_OUT)
        return {'x': x, 'edge_index': edge_index, 'edge_attr': edge_attr, 'u': u, 'batch': batch, 'w1a': w1a, 'b1a': b1a, 'w1b': w1b, 'b1b': b1b, 'w1c': w1c, 'b1c': b1c, 'w2a': w2a, 'b2a': b2a, 'w2b': w2b, 'b2b': b2b}
    _L2_gnn_all = _L2_gnn_setup()
    _L2_gnn_in = {k: v for k, v in _L2_gnn_all.items() if k in ('u', 'w1a', 'b1a', 'w1b', 'b1b', 'w1c', 'b1c', 'w2a', 'b2a', 'w2b', 'b2b')}
    del _L2_gnn_all

    def _L3_gnn_setup():
        import jax, jax.numpy as jnp
        import numpy as np
        N_N = 12500
        N_E = 200000
        IN_DIM = 128
        OUT_DIM = 128
        key = jax.random.key(seed)
        k1, k2, k3, k4 = jax.random.split(key, 4)
        feats_n = jax.random.normal(k1, (N_N, IN_DIM), dtype=jnp.float32)
        hs = jnp.concatenate([jnp.arange(N_N, dtype=jnp.int64), jax.random.randint(k2, (N_E - N_N,), 0, N_N, dtype=jnp.int64)])
        ts = jax.random.randint(k3, (N_E,), 0, N_N, dtype=jnp.int64)
        edges = jnp.stack([hs, ts], axis=0)
        weight = jax.random.normal(k4, (OUT_DIM, IN_DIM), dtype=jnp.float32) / np.sqrt(OUT_DIM)
        return {'feats_n': feats_n, 'edges': edges, 'weight': weight}
    _L3_gnn_all = _L3_gnn_setup()
    _L3_gnn_in = {k: v for k, v in _L3_gnn_all.items() if k in ('weight',)}
    del _L3_gnn_all
    return {'x': x, 'src': src, 'dst': dst, 'edge_attr_128': edge_attr_128, 'edge_type_4': edge_type_4, 'L0_gnn_W': _L0_gnn_in['W'], 'L0_gnn_att_vectors': _L0_gnn_in['att_vectors'], 'L0_gnn_confounder_probs': _L0_gnn_in['confounder_probs'], 'L0_gnn_edge_importance': _L0_gnn_in['edge_importance'], 'L0_gnn_bias': _L0_gnn_in['bias'], 'L1_gnn_Ws': _L1_gnn_in['Ws'], 'L1_gnn_Wd': _L1_gnn_in['Wd'], 'L1_gnn_att_s': _L1_gnn_in['att_s'], 'L1_gnn_att_d': _L1_gnn_in['att_d'], 'L1_gnn_b': _L1_gnn_in['b'], 'L2_gnn_u': _L2_gnn_in['u'], 'L2_gnn_w1a': _L2_gnn_in['w1a'], 'L2_gnn_b1a': _L2_gnn_in['b1a'], 'L2_gnn_w1b': _L2_gnn_in['w1b'], 'L2_gnn_b1b': _L2_gnn_in['b1b'], 'L2_gnn_w1c': _L2_gnn_in['w1c'], 'L2_gnn_b1c': _L2_gnn_in['b1c'], 'L2_gnn_w2a': _L2_gnn_in['w2a'], 'L2_gnn_b2a': _L2_gnn_in['b2a'], 'L2_gnn_w2b': _L2_gnn_in['w2b'], 'L2_gnn_b2b': _L2_gnn_in['b2b'], 'L3_gnn_weight': _L3_gnn_in['weight']}

def reference(x, src, dst, edge_attr_128, edge_type_4, L0_gnn_W, L0_gnn_att_vectors, L0_gnn_confounder_probs, L0_gnn_edge_importance, L0_gnn_bias, L1_gnn_Ws, L1_gnn_Wd, L1_gnn_att_s, L1_gnn_att_d, L1_gnn_b, L2_gnn_u, L2_gnn_w1a, L2_gnn_b1a, L2_gnn_w1b, L2_gnn_b1b, L2_gnn_w1c, L2_gnn_b1c, L2_gnn_w2a, L2_gnn_b2a, L2_gnn_w2b, L2_gnn_b2b, L3_gnn_weight):
    import jax
    import jax.numpy as jnp

    def _L0_gnn_ref(x, edge_index, edge_types, W, att_vectors, confounder_probs, edge_importance, bias):
        import jax, jax.numpy as jnp
        import numpy as np
        N_NODES = 6250
        N_EDGES = 100000
        IN_CH = 128
        OUT_CH = 32
        HEADS = 4
        N_TYPES = 4
        N_CONF = 5
        N = x.shape[0]
        T = W.shape[0]
        K, H, C2 = att_vectors.shape
        C = C2 // 2
        src = edge_index[0]
        dst = edge_index[1]
        et = edge_types.astype(jnp.int32)
        xt = jnp.einsum('ni,tio->tno', x, W)
        xj = xt[et, src].reshape(-1, H, C)
        xi = xt[et, dst].reshape(-1, H, C)
        x_cat = jnp.concatenate([xi, xj], axis=-1)
        scores = jnp.einsum('ehd,khd->ehk', x_cat, att_vectors)
        scores = jax.nn.leaky_relu(scores, negative_slope=0.2)
        pk = jax.nn.softmax(confounder_probs)
        alpha = jnp.einsum('ehk,k->eh', scores, pk)
        seg = et * N + dst
        n_seg = T * N
        m = jax.ops.segment_max(alpha, seg, num_segments=n_seg)
        a = jnp.exp(alpha - m[seg])
        denom = jax.ops.segment_sum(a, seg, num_segments=n_seg)
        alpha_n = a / denom[seg]
        msg = (xj * alpha_n[..., None]).reshape(-1, H * C)
        msg = msg * edge_importance[et][:, None]
        out = jax.ops.segment_sum(msg, dst, num_segments=N)
        out = out + x @ W[0] + bias
        return out

    def _L1_gnn_ref(x, edge_index, Ws, Wd, att_s, att_d, b):
        import jax, jax.numpy as jnp
        import numpy as np
        NEG_SLOPE = 0.2
        EPS = 1e-16
        N_NODES = 12500
        N_EDGES = 200000
        D = 128
        H = 4
        C = 32
        L = 3

        def _gat_layer(h, src, dst, Ws, Wd, a_s, a_d, bias):
            N = h.shape[0]
            xs = (h @ Ws).reshape(N, H, C)
            xd = (h @ Wd).reshape(N, H, C)
            alpha_s = jnp.sum(xs * a_s, axis=-1)
            alpha_d = jnp.sum(xd * a_d, axis=-1)
            e = alpha_s[src] + alpha_d[dst]
            e = jax.nn.leaky_relu(e, NEG_SLOPE)
            emax = jax.ops.segment_max(e, dst, num_segments=N)
            ex = jnp.exp(e - emax[dst])
            denom = jax.ops.segment_sum(ex, dst, num_segments=N)
            alpha = ex / (denom[dst] + EPS)
            msg = xs[src] * alpha[:, :, None]
            out = jax.ops.segment_sum(msg, dst, num_segments=N)
            return out.reshape(N, H * C) + bias
        src = edge_index[0]
        dst = edge_index[1]
        h = x
        for i in range(L):
            h = _gat_layer(h, src, dst, Ws[i], Wd[i], att_s[i], att_d[i], b[i])
            if i < L - 1:
                h = jax.nn.relu(h)
        return h

    def _L2_gnn_ref(x, edge_index, edge_attr, u, batch, w1a, b1a, w1b, b1b, w1c, b1c, w2a, b2a, w2b, b2b):
        import jax, jax.numpy as jnp
        import numpy as np
        N_NODES = 5000
        N_EDGES = 80000
        D_NODE = 128
        D_EDGE = 128
        HID = 256
        D_OUT = 128

        def _lin_params(key, d_in, d_out):
            k1, k2 = jax.random.split(key)
            bound = 1.0 / np.sqrt(d_in)
            W = jax.random.uniform(k1, (d_in, d_out), jnp.float32, -bound, bound)
            b = jax.random.uniform(k2, (d_out,), jnp.float32, -bound, bound)
            return (W, b)
        row, col = (edge_index[0], edge_index[1])
        h = jnp.concatenate([x[row], edge_attr], axis=1)
        h = jax.nn.relu(h @ w1a + b1a)
        h = jax.nn.relu(h @ w1b + b1b)
        h = h @ w1c + b1c
        n = x.shape[0]
        summed = jax.ops.segment_sum(h, col, num_segments=n)
        counts = jax.ops.segment_sum(jnp.ones((h.shape[0],), h.dtype), col, num_segments=n)
        agg = summed / jnp.maximum(counts, 1.0)[:, None]
        z = jnp.concatenate([x, agg], axis=1)
        z = jax.nn.relu(z @ w2a + b2a)
        return z @ w2b + b2b

    def _L3_gnn_ref(feats_n, edges, weight):
        import jax, jax.numpy as jnp
        import numpy as np
        N_N = 12500
        N_E = 200000
        IN_DIM = 128
        OUT_DIM = 128
        hs, ts = (edges[0], edges[1])
        n = feats_n.shape[0]
        deg = jax.ops.segment_sum(jnp.ones_like(hs, dtype=feats_n.dtype), hs, num_segments=n)
        sqrt_d_inv = deg ** (-0.5)
        scaled = sqrt_d_inv[:, None] * feats_n
        agg = jax.ops.segment_sum(scaled[ts], hs, num_segments=n)
        msg = sqrt_d_inv[:, None] * agg
        out = msg @ weight.T
        return jax.nn.relu(out)
    edge_index = jnp.stack([src, dst])
    batch0 = jnp.zeros((6250,), jnp.int32)
    x = _layernorm(x + _L0_gnn_ref(x, edge_index, edge_type_4, L0_gnn_W, L0_gnn_att_vectors, L0_gnn_confounder_probs, L0_gnn_edge_importance, L0_gnn_bias), axis=-1)
    x = _layernorm(x + _L1_gnn_ref(x, edge_index, L1_gnn_Ws, L1_gnn_Wd, L1_gnn_att_s, L1_gnn_att_d, L1_gnn_b), axis=-1)
    x = _layernorm(x + _L2_gnn_ref(x, edge_index, edge_attr_128, L2_gnn_u, batch0, L2_gnn_w1a, L2_gnn_b1a, L2_gnn_w1b, L2_gnn_b1b, L2_gnn_w1c, L2_gnn_b1c, L2_gnn_w2a, L2_gnn_b2a, L2_gnn_w2b, L2_gnn_b2b), axis=-1)
    x = _layernorm(x + _L3_gnn_ref(x, edge_index, L3_gnn_weight), axis=-1)
    return x

_drawn_inputs = setup_inputs


def setup_inputs(seed=0):
    import zlib

    import numpy as np

    out = dict(_drawn_inputs(seed))
    spreads = {'L0_gnn_bias': (0.0, 0.8), 'L1_gnn_b': (0.0, 0.472)}
    factors = {'edge_attr_128': 8.0,
     'L0_gnn_confounder_probs': 28.704,
     'L1_gnn_Wd': 64.0,
     'L1_gnn_att_d': 64.0,
     'L2_gnn_w1a': 8.0,
     'L2_gnn_b1a': 47.227,
     'L2_gnn_w1b': 5.735,
     'L2_gnn_b1b': 64.0,
     'L2_gnn_w1c': 4.421,
     'L2_gnn_b1c': 57.816,
     'L2_gnn_b2a': 33.56,
     'L0_gnn_att_vectors': 5.885,
     'L1_gnn_Ws': 4.218,
     'L1_gnn_att_s': 8.0,
     'L2_gnn_b2b': 21.92}
    for name, (base, spread) in spreads.items():
        noise = np.random.default_rng([zlib.crc32(name.encode()), seed]).standard_normal(out[name].shape)
        drawn = base * np.exp(spread * noise) if base else spread * noise
        out[name] = jnp.asarray(drawn.astype(out[name].dtype))
    for name, factor in factors.items():
        out[name] = (out[name] * factor).astype(out[name].dtype)
    return out
```

```python
import concourse.bass as bass
from concourse import mybir
from contextlib import ExitStack

P = 128
N, E, D = 6250, 100000, 128
NT = -(-N // P)
NTP = NT + 1
NPAD = NTP * P
EC = -(-E // P)
EPAD = EC * P
H, C, K5, T4 = 4, 32, 5, 4
S = 4
U = 4
GC = -(-(int(E * 1.04) // S + NTP + 2 * U) // P)
GMAX = GC * P
ROWS = NPAD + P
REC = 20
R_SRC, R_EID, R_SUM, R_ANY, R_J, R_IDX, R_TYPE = 0, S, 2 * S, 3 * S, 4 * S, REC, REC + S
BIG = 2e30
LOW = -1e30
DEGCAP = 2000
HALF = 17
A0, A1 = D + H * K5, D + H
HID = 256


def gnn(nc, x, src, dst, windows, edge_attr, W0, W0T, attI, attJ, probs, importance, bias0,
        Ws, WsT, Wd, WdT, attS, attD, bias1, w1a, b1a, w1b, b1b, w1c, b1c, w2a, b2a, w2b, b2b,
        w3T, out):
    fp32, bf16, i32, u32 = mybir.dt.float32, mybir.dt.bfloat16, mybir.dt.int32, mybir.dt.uint32
    ALU, ACT, AX = mybir.AluOpType, mybir.ActivationFunctionType, mybir.AxisListType
    ds = bass.ds
    V, A, PE, G = nc.vector, nc.scalar, nc.tensor, nc.gpsimd

    def dram(name, shape, dt):
        return nc.dram_tensor(name, shape, dt).ap()

    key_d = dram("keys", [P, NT], fp32)
    perm_d = dram("nodes_by_degree", [NT * P, 4], i32)
    item_d = dram("item_table", [GMAX, 2], i32)
    rec_d = dram("item_records", [GMAX, P, REC], i32)
    rec0_d = dram("item_records_layer0", [GMAX, P, REC], i32)
    tab0_d = dram("table_layer0", [NPAD, T4 * A0], fp32)
    tab1_d = [dram(f"table_layer1_{i}", [NPAD, A1], fp32) for i in range(3)]
    tab2_d = dram("table_layer2", [NPAD, HID], fp32)
    x3_d = dram("x_before_layer3", [NPAD, D], fp32)
    sum_d = [dram(f"sums_by_source_{s}", [ROWS, D], fp32) for s in range(S)]

    top = ExitStack()
    with top:
        def sb(name, shape, dt=fp32, ctx=top):
            return ctx.enter_context(nc.sbuf_tensor(name, shape, dt))

        def pb(name, shape, dt=fp32, ctx=top):
            return ctx.enter_context(nc.psum_tensor(name, shape, dt))

        live = []

        def sem(name):
            live.append(nc.alloc_semaphore(name=name))
            return live[-1]

        def fresh_semaphores():
            nc.clear_and_free_semaphores(live)
            nc.all_engine_barrier()
            live.clear()


        def bc(ap, axis, n):
            v = ap.unsqueeze(axis)
            shape = list(v.shape)
            shape[axis] = n
            return v.to_broadcast(shape)

        xr = sb("xr", [P, NTP, D])
        ident = sb("ident", [P, P])
        identb = sb("identb", [P, P], bf16)
        nid = sb("nid", [P, NTP], i32)
        degI = sb("degI", [P, NTP])
        degO = sb("degO", [P, NTP])
        degOn = sb("degOn", [P, NT])
        rowst = sb("rowst", [P, NTP])
        trips = sb("trips", [1, 1], i32)
        iotaS = sb("iotaS", [P, S])
        iotaT = sb("iotaT", [P, T4])
        place = sb("place", [P, 1])
        strict = sb("strict", [P, P])
        lower = sb("lower", [P, P])

        with ExitStack() as ph:
            e32 = [sb(f"e32_{w}", [P, EC], i32, ph) for w in "ds"]
            part = [[sb(f"part_{w}{q}", [P, EC], i32, ph) for q in "lh"] for w in "ds"]
            lo = [sb(f"lo_{w}", [P, EC], bf16, ph) for w in "ds"]
            hi = [sb(f"hi_{w}", [P, EC], bf16, ph) for w in "ds"]
            row128 = sb("row128", [P, P], bf16, ph)
            oneL = [sb(f"oneL{i}", [P, HALF, P], bf16, ph) for i in range(2)]
            oneH = [sb(f"oneH{i}", [P, HALF, NT], bf16, ph) for i in range(2)]
            ones = sb("ones", [P, P], fp32, ph)
            zeros = sb("zeros", [P, D * 2], fp32, ph)
            zerob = sb("zerob", [P, P], bf16, ph)
            nrev = sb("nrev", [P, NT], fp32, ph)
            nnum = sb("nnum", [P, NT], i32, ph)
            degIn = sb("degIn", [P, NT], fp32, ph)
            rsn = sb("rsn", [P, NT], fp32, ph)
            key = sb("key", [P, NT], fp32, ph)
            keyrow = sb("keyrow", [P, NT * P], fp32, ph)
            above = sb("above", [P, NT * P], bf16, ph)
            rank = sb("rank", [P, NT], fp32, ph)
            ranki = sb("ranki", [P, NT], u32, ph)
            tot = sb("tot", [P, NT], fp32, ph)
            incl = sb("incl", [P, NT], fp32, ph)
            noderec = sb("noderec", [P, NT, 4], i32, ph)
            permrec = sb("permrec", [P, NTP, 4], i32, ph)
            dmax = sb("dmax", [P, NTP], fp32, ph)
            nci = sb("nci", [P, NTP], i32, ph)
            ncf = sb("ncf", [P, NTP], fp32, ph)
            ends = sb("ends", [P, NTP], fp32, ph)
            tripf = sb("tripf", [1, 1], i32, ph)
            gnum = sb("gnum", [P, GC], fp32, ph)
            jof = sb("jof", [P, 2, GC], fp32, ph)
            start = sb("start", [P, 2, GC], fp32, ph)
            hit = sb("hit", [P, GC], fp32, ph)
            items = sb("items", [P, GC, 2], i32, ph)
            hist = [pb(f"hist_{w}", [P, 512], fp32, ph) for w in "ds"]
            pre = pb("pre", [P, 512], fp32, ph)
            edges_in = [sem("edges_in_d"), sem("edges_in_s")]
            consts = sem("consts")
            cst2 = sem("consts_first")
            zeroed = sem("zeroed")
            onehot = [sem("onehot0"), sem("onehot1")]
            counted = [sem("counted0"), sem("counted1")]
            hist_done = sem("hist_done")
            degs = sem("degrees_ready")
            prefix = sem("prefix_done")
            keys = sem("keys_ready")
            key_out = sem("keys_stored")
            key_in = sem("keyrow_in")
            ranks = sem("ranks_ready")
            perm_out = sem("perm_stored")
            perm_in = sem("perm_in")
            perm_ok = sem("perm_unpacked")
            dmax_ok = sem("dmax_ready")
            items_ok = sem("items_ready")
            items_out = sem("items_stored")
            STEPS = EC // (2 * HALF)

            block = ph.enter_context(nc.Block())

            @block.sync
            def _(sp):
                for w, e in enumerate((dst, src)):
                    sp.dma_start(e32[w][:, :], e).then_inc(edges_in[w], 16)
                sp.wait_ge(consts, 1)
                for s in range(S):
                    for r in range(NPAD // P):
                        sp.dma_start(sum_d[s][r * P:(r + 1) * P, :], zeros[:, 0:D]).then_inc(zeroed, 16)
                sp.wait_ge(keys, 1)
                sp.dma_start(key_d, key[:, :]).then_inc(key_out, 16)
                sp.wait_ge(key_out, 16)
                sp.dma_start(keyrow[:, :], key_d.rearrange("p j -> (p j)").partition_broadcast(P)
                             ).then_inc(key_in, 16)
                sp.wait_ge(perm_out, 16 * NT)
                sp.dma_start(permrec[:, 0:NT, :],
                             perm_d[0:NT * P, :].rearrange("(j p) w -> p j w", p=P)).then_inc(perm_in, 16)
                sp.wait_ge(items_ok, 1)
                sp.dma_start(item_d.rearrange("(p c) w -> p c w", p=P), items[:, :, :]).then_inc(items_out, 16)
                sp.wait_ge(items_out, 16)
                sp.wait_ge(zeroed, 16 * S * (NPAD // P))

            @block.gpsimd
            def _(pool):
                G.memset(zeros[:, :], 0.0).then_inc(consts, 1)
                G.memset(zerob[:, :], 0.0).then_inc(cst2, 1)
                G.memset(ones[:, :], 1.0).then_inc(cst2, 1)
                G.memset(ident[:, :], 0.0).then_inc(cst2, 1)
                G.memset(strict[:, :], 0.0).then_inc(cst2, 1)
                G.memset(lower[:, :], 1.0).then_inc(cst2, 1)
                G.iota(row128[:, :], [[1, P]], base=0, channel_multiplier=0,
                       allow_small_or_imprecise_dtypes=True).then_inc(cst2, 1)
                pool.wait_ge(cst2, 6)
                G.affine_select(out=ident[:, :], in_=ident[:, :], compare_op=ALU.not_equal, fill=1.0,
                                base=0, pattern=[[-1, P]], channel_multiplier=1).then_inc(cst2, 1)
                G.affine_select(out=strict[:, :], in_=strict[:, :], compare_op=ALU.is_ge, fill=1.0,
                                base=0, pattern=[[-1, P]], channel_multiplier=1).then_inc(cst2, 1)
                G.affine_select(out=lower[:, :], in_=lower[:, :], compare_op=ALU.is_gt, fill=0.0,
                                base=0, pattern=[[-1, P]], channel_multiplier=1).then_inc(cst2, 1)
                G.iota(nnum[:, :], [[P, NT]], base=0, channel_multiplier=1).then_inc(cst2, 1)
                G.iota(nrev[:, :], [[-P, NT]], base=8191, channel_multiplier=-1,
                       allow_small_or_imprecise_dtypes=True).then_inc(cst2, 1)
                G.iota(iotaS[:, :], [[1, S]], base=0, channel_multiplier=0,
                       allow_small_or_imprecise_dtypes=True).then_inc(cst2, 1)
                G.iota(iotaT[:, :], [[1, T4]], base=0, channel_multiplier=0,
                       allow_small_or_imprecise_dtypes=True).then_inc(cst2, 1)
                G.iota(place[:, :], [[1, 1]], base=0, channel_multiplier=1,
                       allow_small_or_imprecise_dtypes=True).then_inc(cst2, 1)
                G.iota(gnum[:, :], [[1, GC]], base=0, channel_multiplier=GC,
                       allow_small_or_imprecise_dtypes=True).then_inc(cst2, 1)
                pool.wait_ge(ranks, 1)
                for j in range(NT):
                    G.indirect_dma_start(out=perm_d, out_offset=bass.IndirectOffsetOnAxis(ap=ranki[:, j:j + 1], axis=0),
                                         in_=noderec[:, j, :], in_offset=None).then_inc(perm_out, 16)
                pool.wait_ge(perm_ok, 1)
                G.partition_all_reduce(dmax[:, :], degI[:, :], P, bass.bass_isa.ReduceOp.max).then_inc(dmax_ok, 1)

            @block.vector
            def _(dve):
                for w in range(2):
                    dve.wait_ge(edges_in[w], 16)
                    V.tensor_scalar(part[w][0][:, :], e32[w][:, :], P - 1, None, ALU.bitwise_and)
                    V.tensor_scalar(part[w][1][:, :], e32[w][:, :], 7, None, ALU.arith_shift_right)
                dve.drain()
                for w in range(2):
                    V.tensor_copy(lo[w][:, :], part[w][0][:, :])
                    V.tensor_copy(hi[w][:, :], part[w][1][:, :])
                dve.drain()
                dve.wait_ge(cst2, 15)
                for w in range(2):
                    with dve.Fori(0, STEPS) as i:
                        for v in range(2):
                            dve.wait_ge(counted[v], i + w * STEPS + 1)
                            at = (i * 2 + v) * HALF
                            V.tensor_tensor(oneL[v][:, :, :], bc(lo[w][:, ds(at, HALF)], 2, P),
                                            bc(row128[:, :], 1, HALF), ALU.is_equal)
                            V.tensor_tensor(oneH[v][:, :, :], bc(hi[w][:, ds(at, HALF)], 2, NT),
                                            bc(row128[:, 0:NT], 1, HALF), ALU.is_equal).then_inc(onehot[v], 1)
                dve.wait_ge(hist_done, 1)
                V.tensor_copy(degIn[:, :], hist[0][:, 0:NT])
                V.tensor_copy(degOn[:, :], hist[1][:, 0:NT])
                V.tensor_copy(identb[:, :], ident[:, :])
                dve.drain()
                V.tensor_scalar(key[:, :], degIn[:, :], float(DEGCAP), 8192.0, ALU.min, ALU.mult).then_inc(degs, 1)
                dve.drain()
                V.tensor_tensor(key[:, :], key[:, :], nrev[:, :], ALU.add).then_inc(keys, 1)
                dve.wait_ge(prefix, 1)
                V.tensor_copy(tot[:, :], pre[:, NT:2 * NT])
                dve.drain()
                V.tensor_tensor_scan(incl[:, :], ones[:, 0:NT], tot[:, :], 0.0, ALU.mult, ALU.add)
                dve.drain()
                V.tensor_tensor(incl[:, :], incl[:, :], tot[:, :], ALU.subtract)
                dve.drain()
                V.tensor_tensor(rsn[:, :], incl[:, :], pre[:, 0:NT], ALU.add)
                dve.drain()
                V.tensor_copy(noderec[:, :, 0], nnum[:, :])
                V.tensor_copy(noderec[:, :, 1], rsn[:, :])
                V.tensor_copy(noderec[:, :, 2], degIn[:, :])
                V.tensor_copy(noderec[:, :, 3], degOn[:, :])
                V.tensor_scalar(incl[:, :], nrev[:, :], float(8191 - N) + 0.5, None, ALU.is_lt)
                dve.drain()
                V.tensor_tensor(degOn[:, :], degOn[:, :], incl[:, :], ALU.max)
                dve.wait_ge(key_in, 16)
                with dve.Fori(0, NT) as j:
                    V.tensor_scalar(above[:, :], keyrow[:, :], key[:, ds(j, 1)], 0.0, ALU.is_gt, ALU.add,
                                    accum_out=rank[:, ds(j, 1)])
                    dve.drain()
                V.tensor_copy(ranki[:, :], rank[:, :]).then_inc(ranks, 1)
                dve.wait_ge(perm_in, 16)
                V.tensor_copy(nid[:, 0:NT], permrec[:, 0:NT, 0])
                V.tensor_scalar(nid[:, NT:NTP], place[:, :], float(NT * P), None, ALU.add)
                V.memset(rowst[:, NT:NTP], 0.0)
                V.memset(degI[:, NT:NTP], 0.0)
                V.memset(degO[:, NT:NTP], 0.0)
                V.tensor_copy(rowst[:, 0:NT], permrec[:, 0:NT, 1])
                V.tensor_copy(degO[:, 0:NT], permrec[:, 0:NT, 3])
                V.tensor_copy(degI[:, 0:NT], permrec[:, 0:NT, 2]).then_inc(perm_ok, 1)
                dve.wait_ge(dmax_ok, 1)
                V.tensor_scalar(nci[:, :], dmax[:, :], float(S - 1), None, ALU.add)
                dve.drain()
                V.tensor_scalar(nci[:, :], nci[:, :], S.bit_length() - 1, None, ALU.arith_shift_right)
                dve.drain()
                V.tensor_copy(ncf[:, :], nci[:, :])
                dve.drain()
                V.tensor_tensor_scan(ends[:, :], ones[:, 0:NTP], ncf[:, :], 0.0, ALU.mult, ALU.add)
                dve.drain()
                V.tensor_scalar(tripf[:, :], ends[0:1, NT - 1:NT], float(U - 1), None, ALU.add)
                dve.drain()
                V.tensor_scalar(trips[:, :], tripf[:, :], U.bit_length() - 1, None, ALU.arith_shift_right)
                V.memset(jof[:, :, :], 0.0)
                V.memset(start[:, :, :], 0.0)
                dve.drain()
                for j in range(NT):
                    a, b = j % 2, (j + 1) % 2
                    V.scalar_tensor_tensor(jof[:, b, :], gnum[:, :], ends[:, j:j + 1], jof[:, a, :], ALU.is_ge, ALU.add)
                    V.tensor_scalar(hit[:, :], gnum[:, :], ends[:, j:j + 1], ends[:, j:j + 1], ALU.is_ge, ALU.mult)
                    dve.drain()
                    V.tensor_tensor(start[:, b, :], hit[:, :], start[:, a, :], ALU.max)
                    dve.drain()
                b = NT % 2
                V.tensor_tensor(hit[:, :], gnum[:, :], start[:, b, :], ALU.subtract)
                V.tensor_copy(items[:, :, 0], jof[:, b, :])
                dve.drain()
                V.tensor_scalar(items[:, :, 1], hit[:, :], float(S), None, ALU.mult).then_inc(items_ok, 1)

            @block.tensor
            def _(pe):
                for c in counted:
                    pe.sem_inc(c, 1)
                pe.wait_ge(cst2, 15)
                for w in range(2):
                    PE.matmul(hist[w][:, 0:NT], zerob[:, :], zerob[:, 0:NT], start=True, stop=False)
                    with pe.Fori(0, STEPS) as i:
                        for v in range(2):
                            pe.wait_ge(onehot[v], i + 1 + w * STEPS)
                            for t in range(HALF):
                                last = PE.matmul(hist[w][:, 0:NT], oneL[v][:, t, :], oneH[v][:, t, :],
                                                 start=False, stop=False)
                            last.then_inc(counted[v], 1)
                    last = PE.matmul(hist[w][:, 0:NT], zerob[:, :], zerob[:, 0:NT], start=False, stop=True)
                last.then_inc(hist_done, 1)
                pe.wait_ge(degs, 1)
                PE.matmul(pre[:, 0:NT], strict[:, :], degIn[:, :], start=True, stop=True)
                PE.matmul(pre[:, NT:2 * NT], ones[:, :], degIn[:, :], start=True, stop=True).then_inc(prefix, 1)

        with ExitStack() as ph:
            jk = [sb(f"jk{u}", [P, 2], i32, ph) for u in range(U)]
            kb = sb("kb", [P, U], fp32, ph)
            rs = sb("rs", [P, U], fp32, ph)
            dg = sb("dg", [P, U], fp32, ph)
            kk = sb("kk", [P, U, S], fp32, ph)
            ee = sb("ee", [P, U, S], fp32, ph)
            ok = sb("ok", [P, U, S], fp32, ph)
            t1 = sb("t1", [P, U, S], fp32, ph)
            t2 = sb("t2", [P, U, S], fp32, ph)
            trash = sb("trash", [P, U, S], fp32, ph)
            eq = sb("eq", [P, U, S, T4], fp32, ph)
            win = sb("win", [P, U], u32, ph)
            we = sb("we", [P, U, 2 * S], i32, ph)
            wf = sb("wf", [P, U, 2 * S], fp32, ph)
            rec = sb("rec", [P, U, 2 * REC], i32, ph)
            recf = rec[:, :, :].bitcast(fp32)
            jk_in = [sem(f"jk_in{u}") for u in range(U)]
            jk_used = sem("jk_used")
            win_ok = sem("window_index_ready")
            gate = sem("pool_gate_records")
            gate2 = sem("act_gate_records")
            gate3 = sem("dve_gate_records")
            win_in = sem("windows_in")
            rec_ok = sem("record_ready")
            rec_out = sem("record_stored")
            rec_blank = sem("record_blank")

            block = ph.enter_context(nc.Block())

            @block.sync
            def _(sp):
                n = sp.value_load(trips[0:1, 0:1], min_val=1, max_val=GMAX // U)
                with sp.Fori(0, n) as i:
                    sp.wait_ge(jk_used, i + 1)
                    for u in range(U):
                        sp.dma_start(jk[u][:, :], item_d[ds(i * U + u, 1), :].rearrange("a w -> (a w)")
                                     .partition_broadcast(P)).then_inc(jk_in[u], 16)

            @block.gpsimd
            def _(pool):
                n = pool.value_load(trips[0:1, 0:1], min_val=1, max_val=GMAX // U)
                with pool.Fori(0, n) as i:
                    pool.wait_ge(win_ok, i + 1)
                    pool.sem_inc(gate, 1)
                    for u in range(U):
                        G.indirect_dma_start(out=we[:, u, :], out_offset=None, in_=windows,
                                             in_offset=bass.IndirectOffsetOnAxis(ap=win[:, u:u + 1], axis=0)
                                             ).then_inc(win_in, 16)

            @block.scalar
            def _(act):
                n = act.value_load(trips[0:1, 0:1], min_val=1, max_val=GMAX // U)
                act.wait_ge(rec_blank, 1)
                for half, to in enumerate((rec_d, rec0_d)):
                    act.dma_start(to[GMAX - U:GMAX, :, :].rearrange("u p w -> p u w"),
                                  rec[:, :, half * REC:(half + 1) * REC]).then_inc(rec_out, 16)
                with act.Fori(0, n) as i:
                    act.wait_ge(rec_ok, i + 1)
                    for half, to in enumerate((rec_d, rec0_d)):
                        act.dma_start(to[ds(i * U, U), :, :].rearrange("u p w -> p u w"),
                                      rec[:, :, half * REC:(half + 1) * REC]).then_inc(rec_out, 16)
                act.wait_ge(rec_out, n * 32 + 32)
                act.sem_inc(gate2, 1)

            @block.vector
            def _(dve):
                n = dve.value_load(trips[0:1, 0:1], min_val=1, max_val=GMAX // U)
                for u in range(U):
                    V.tensor_scalar(trash[:, u, :], place[:, :].to_broadcast([P, S]), float(NPAD), None, ALU.add)
                V.memset(rec[:, :, :], 0).then_inc(rec_blank, 1)
                dve.drain()
                dve.sem_inc(jk_used, 1)
                with dve.Fori(0, n) as i:
                    for u in range(U):
                        dve.wait_ge(jk_in[u], (i + 1) * 16)
                        dve.sem_inc(gate3, 1)
                        j = dve.value_load(jk[u][0:1, 0:1], min_val=0, max_val=NT)
                        V.tensor_copy(rs[:, u:u + 1], rowst[:, ds(j, 1)])
                        V.tensor_copy(dg[:, u:u + 1], degI[:, ds(j, 1)])
                        V.tensor_copy(kb[:, u:u + 1], jk[u][:, 1:2])
                        if u == 0:
                            dve.wait_ge(rec_out, i * 32 + 32)
                        V.tensor_copy(rec[:, u, R_J:R_J + 1], jk[u][:, 0:1])
                    dve.drain()
                    V.tensor_tensor(rs[:, :], rs[:, :], kb[:, :], ALU.add)
                    V.tensor_tensor(kk[:, :, :], bc(kb[:, :], 2, S), bc(iotaS[:, :], 1, U), ALU.add).then_inc(jk_used, 1)
                    dve.drain()
                    V.tensor_scalar(win[:, :], rs[:, :], float(E), None, ALU.min).then_inc(win_ok, 1)
                    V.tensor_tensor(ok[:, :, :], kk[:, :, :], bc(dg[:, :], 2, S), ALU.is_lt)
                    V.tensor_tensor(ee[:, :, :], bc(rs[:, :], 2, S), bc(iotaS[:, :], 1, U), ALU.add)
                    dve.drain()
                    V.tensor_tensor(rec[:, :, R_EID:R_EID + S], ee[:, :, :], ok[:, :, :], ALU.mult)
                    V.tensor_scalar(recf[:, :, R_ANY:R_ANY + S], ok[:, :, :], 1.0, BIG, ALU.subtract, ALU.mult)
                    dve.wait_ge(win_in, (i + 1) * 16 * U)
                    V.tensor_copy(wf[:, :, :], we[:, :, :])
                    dve.drain()
                    V.tensor_tensor(t1[:, :, :], wf[:, :, 0:S], ok[:, :, :], ALU.mult)
                    V.scalar_tensor_tensor(t2[:, :, :], wf[:, :, S:2 * S], 1.0, ok[:, :, :], ALU.add, ALU.mult)
                    V.tensor_tensor(ee[:, :, :], wf[:, :, 0:S], trash[:, :, :], ALU.subtract)
                    dve.drain()
                    V.tensor_tensor(ee[:, :, :], ee[:, :, :], ok[:, :, :], ALU.mult)
                    V.tensor_copy(rec[:, :, R_SRC:R_SRC + S], t1[:, :, :])
                    V.scalar_tensor_tensor(kk[:, :, :], t1[:, :, :], float(T4), t2[:, :, :], ALU.mult, ALU.add)
                    V.tensor_scalar(t2[:, :, :], t2[:, :, :], 1.0, None, ALU.subtract)
                    dve.drain()
                    V.tensor_tensor(rec[:, :, R_IDX:R_IDX + S], kk[:, :, :], ok[:, :, :], ALU.subtract)
                    V.tensor_tensor(recf[:, :, R_SUM:R_SUM + S], ee[:, :, :], trash[:, :, :], ALU.add)
                    for u in range(U):
                        V.tensor_tensor(eq[:, u, :, :], bc(t2[:, u, :], 2, T4), bc(iotaT[:, :], 1, S), ALU.is_equal)
                    dve.drain()
                    V.tensor_scalar(recf[:, :, R_TYPE:R_TYPE + S * T4],
                                    eq[:, :, :, :].rearrange("p u s t -> p u (s t)"),
                                    1.0, BIG, ALU.subtract, ALU.mult).then_inc(rec_ok, 1)

        fresh_semaphores()

        h = sb("h", [P, NTP, D])
        own = sb("own", [P, NTP, T4 * H * K5])
        rhs0 = sb("rhs0", [P, T4, A0])
        rhs0i = sb("rhs0i", [P, T4, H * K5])
        rhs1 = sb("rhs1", [P, 3, D + 2 * H])
        soft = sb("soft", [P, K5])
        impt = sb("impt", [P, T4])
        bias = sb("bias", [P, 4, D])
        with ExitStack() as ph:
            wT = sb("wT", [P, T4, D], fp32, ph)
            wsT = sb("wsT", [P, 3, D], fp32, ph)
            wdT = sb("wdT", [P, 3, D], fp32, ph)
            aI = sb("aI", [P, H * K5], fp32, ph)
            aJ = sb("aJ", [P, H * K5], fp32, ph)
            aS = sb("aS", [P, 3, H], fp32, ph)
            aD = sb("aD", [P, 3, H], fp32, ph)
            pk = sb("pk", [P, K5], fp32, ph)
            sm = sb("sm", [P, 2], fp32, ph)
            wps = pb("wps", [P, 512], fp32, ph)
            w_in = sem("weights_in")
            probs_in = sem("probs_in")
            x_in = sem("x_in")
            wp = sem("score_weights_done")
            mx = sem("probs_max_ready")
            ex = sem("probs_exp_ready")

            block = ph.enter_context(nc.Block())

            @block.sync
            def _(sp):
                sp.dma_start(pk[:, :], probs.partition_broadcast(P)).then_inc(probs_in, 16)
                for to, frm in ((wT[:, :, :], W0T), (wsT[:, :, :], WsT), (wdT[:, :, :], WdT),
                                (aI[:, :], attI), (aJ[:, :], attJ), (aS[:, :, :], attS), (aD[:, :, :], attD),
                                (rhs0[:, :, 0:D], W0), (rhs1[:, :, 0:D], Ws),
                                (impt[:, :], importance.partition_broadcast(P)),
                                (bias[:, 0, :], bias0.partition_broadcast(P)),
                                (bias[:, 1:4, :], bias1.partition_broadcast(P))):
                    sp.dma_start(to, frm).then_inc(w_in, 16)
                sp.wait_ge(w_in, 16 * 12)

            @block.gpsimd
            def _(pool):
                for j in range(NTP):
                    G.indirect_dma_start(out=xr[:, j, :], out_offset=None, in_=x,
                                         in_offset=bass.IndirectOffsetOnAxis(ap=nid[:, j:j + 1].bitcast(u32), axis=0)
                                         ).then_inc(x_in, 16)
                pool.wait_ge(x_in, 16 * NTP)

            @block.tensor
            def _(pe):
                pe.wait_ge(w_in, 16 * 12)
                for t in range(T4):
                    PE.matmul(wps[:, t * 40:t * 40 + 20], wT[:, t, :], aJ[:, :], start=True, stop=True)
                    PE.matmul(wps[:, t * 40 + 20:t * 40 + 40], wT[:, t, :], aI[:, :], start=True, stop=True)
                for l in range(3):
                    PE.matmul(wps[:, 160 + 8 * l:164 + 8 * l], wsT[:, l, :], aS[:, l, :], start=True, stop=True)
                    last = PE.matmul(wps[:, 164 + 8 * l:168 + 8 * l], wdT[:, l, :], aD[:, l, :], start=True, stop=True)
                last.then_inc(wp, 1)

            @block.scalar
            def _(act):
                act.wait_ge(mx, 1)
                A.activation(soft[:, :], pk[:, :], ACT.Exp).then_inc(ex, 1)

            @block.vector
            def _(dve):
                dve.wait_ge(probs_in, 16)
                V.tensor_reduce(sm[:, 0:1], pk[:, :], AX.X, ALU.max)
                dve.drain()
                V.tensor_scalar(pk[:, :], pk[:, :], sm[:, 0:1], None, ALU.subtract).then_inc(mx, 1)
                dve.wait_ge(ex, 1)
                V.tensor_reduce(sm[:, 0:1], soft[:, :], AX.X, ALU.add)
                dve.drain()
                V.reciprocal(sm[:, 1:2], sm[:, 0:1])
                dve.drain()
                V.tensor_scalar(soft[:, :], soft[:, :], sm[:, 1:2], None, ALU.mult)
                dve.wait_ge(wp, 1)
                v = wps[:, 0:160].rearrange("p (t w) -> p t w", t=T4)
                V.tensor_copy(rhs0[:, :, D:A0], v[:, :, 0:20])
                V.tensor_copy(rhs0i[:, :, :], v[:, :, 20:40])
                V.tensor_copy(rhs1[:, :, D:D + 2 * H], wps[:, 160:184].rearrange("p (l w) -> p l w", l=3))

        def node_table(tag, frm, rhs, pieces, stage, table):
            with ExitStack() as ph:
                ht = [sb(f"ht_{tag}{v}", [P, P], fp32, ph) for v in range(2)]
                hc = [sb(f"hc_{tag}{v}", [P, P], fp32, ph) for v in range(2)]
                tps = [pb(f"tps_{tag}{v}", [P, 512], fp32, ph) for v in range(2)]
                banks = max(p[0] for p in pieces) + 1
                mps = [[pb(f"mps_{tag}{v}{b}", [P, 512], fp32, ph) for b in range(banks)] for v in range(2)]
                fetched = sem(f"tile_copied_{tag}")
                turned = sem(f"tile_transposed_{tag}")
                stored = sem(f"transpose_stored_{tag}")
                mult = sem(f"tile_multiplied_{tag}")
                staged = sem(f"tile_staged_{tag}")
                rows_out = sem(f"rows_out_{tag}")
                block = ph.enter_context(nc.Block())

                @block.scalar
                def _(act):
                    for c in (stored,):
                        act.sem_inc(c, 1)
                    with act.Fori(0, NTP // 2) as i:
                        for v in range(2):
                            act.wait_ge(turned, (i * 2 + v - 1 if v else i * 2) + 1)
                            A.activation(hc[v][:, :], frm[:, ds(i * 2 + v, 1), :].rearrange("p a c -> p (a c)"),
                                         ACT.Copy).then_inc(fetched, 1)
                        for v in range(2):
                            act.wait_ge(turned, i * 2 + v + 2)
                            act.wait_ge(mult, i * 2 + 1)
                            A.activation(ht[v][:, :], tps[v][:, 0:P], ACT.Copy).then_inc(stored, 1)

                @block.tensor
                def _(pe):
                    for c in (turned, mult):
                        pe.sem_inc(c, 1)
                    with pe.Fori(0, NTP // 2) as i:
                        for v in range(2):
                            pe.wait_ge(fetched, i * 2 + v + 1)
                            pe.wait_ge(stored, i * 2 + 1)
                            PE.transpose(tps[v][:, 0:P], hc[v][:, :], ident[:, :]).then_inc(turned, 1)
                        for v in range(2):
                            pe.wait_ge(stored, i * 2 + v + 2)
                            pe.wait_ge(staged, i * 2 + 1)
                            for b, a, z, op, _ in pieces:
                                last = PE.matmul(mps[v][b][:, a:z], ht[v][:, :], op, start=True, stop=True)
                            last.then_inc(mult, 1)

                @block.vector
                def _(dve):
                    for c in (staged,):
                        dve.sem_inc(c, 1)
                    with dve.Fori(0, NTP // 2) as i:
                        for v in range(2):
                            dve.wait_ge(mult, i * 2 + v + 2)
                            for b, a, z, _, to in pieces:
                                for lo_, hi_, dest in to:
                                    last = V.tensor_copy(dest(i * 2 + v), mps[v][b][:, lo_:hi_])
                            last.then_inc(staged, 1)

                @block.gpsimd
                def _(pool):
                    for j in range(NTP):
                        pool.wait_ge(staged, j + 2)
                        G.indirect_dma_start(out=table, out_offset=bass.IndirectOffsetOnAxis(
                            ap=nid[:, j:j + 1].bitcast(u32), axis=0), in_=stage[:, j, :], in_offset=None
                        ).then_inc(rows_out, 16)
                    pool.wait_ge(rows_out, 16 * NTP)

        def flat(ap):
            return ap.rearrange("p a c -> p (a c)")

        def attention(tag, T, table, width, recs, acc, mrun, srun, prod, big, SUMS):
            L = T * H
            with ExitStack() as ph:
                rec = [sb(f"rec_{tag}{u}", [P, 2, REC], i32, ph) for u in range(U)]
                g = [big[:, SUMS + u * S * width:SUMS + (u + 1) * S * width].rearrange("p (s w) -> p s w", s=S)
                     for u in range(U)]
                sc = [sb(f"sc_{tag}{u}", [P, S + 1, L], fp32, ph) for u in range(U)]
                w = [sb(f"w_{tag}{u}", [P, S + 1, L], fp32, ph) for u in range(U)]
                mi = [sb(f"mi_{tag}{u}", [P, L], fp32, ph) for u in range(U)]
                si = [sb(f"si_{tag}{u}", [P, L], fp32, ph) for u in range(U)]
                ZW = H * K5 if T > 1 else H
                z = [sb(f"z_{tag}{u}", [P, S, ZW], fp32, ph) for u in range(U)]
                if T > 1:
                    zt = [sb(f"zt_{tag}{v}", [P, S, T, ZW], fp32, ph) for v in range(2)]
                al = [sb(f"al_{tag}{u}", [P, S, H], fp32, ph) for u in range(U)]
                sums = [pb(f"sums_{tag}{u}", [P, 512], fp32, ph) for u in range(U)]
                rec_in = [sem(f"rec_in_{tag}{u}") for u in range(U)]
                rec_free = [sem(f"rec_free_{tag}{u}") for u in range(U)]
                gathered = [sem(f"gathered_{tag}{u}") for u in range(U)]
                g_free = [sem(f"rows_used_{tag}{u}") for u in range(U)]
                gate = sem(f"gate_{tag}")
                scored = sem(f"scores_ready_{tag}")
                weighed = sem(f"weights_ready_{tag}")
                prods = sem(f"products_ready_{tag}")
                summed = sem(f"products_summed_{tag}")

                block = ph.enter_context(nc.Block())
                NREC = 2 if T > 1 else 1

                def turns(eng):
                    return eng.value_load(trips[0:1, 0:1], min_val=1, max_val=GMAX // U)

                @block.sync
                def _(sp):
                    n = turns(sp)
                    with sp.Fori(0, n) as i:
                        for u in range(U):
                            sp.wait_ge(rec_free[u], i + 1)
                            for half in range(NREC):
                                sp.dma_start(rec[u][:, half, :], recs[half][ds(i * U + u, 1), :, :]
                                             .rearrange("a p w -> (a p) w")).then_inc(rec_in[u], 16)

                @block.gpsimd
                def _(pool):
                    n = turns(pool)
                    ix = (1, 0) if T > 1 else (0, R_SRC)
                    with pool.Fori(0, n) as i:
                        for u in range(U):
                            pool.wait_ge(rec_in[u], (i + 1) * 16 * NREC)
                            pool.wait_ge(g_free[u], i + 1)
                            pool.sem_inc(gate, 1)
                            for s in range(S):
                                G.indirect_dma_start(
                                    out=g[u][:, s, :], out_offset=None, in_=table,
                                    in_offset=bass.IndirectOffsetOnAxis(
                                        ap=rec[u][:, ix[0], ix[1] + s:ix[1] + s + 1].bitcast(u32), axis=0)
                                ).then_inc(gathered[u], 16)

                @block.scalar
                def _(act):
                    n = turns(act)
                    with act.Fori(0, n) as i:
                        for u in range(U):
                            act.wait_ge(scored, i * U + u + 1)
                            A.activation(w[u][:, :, :], sc[u][:, :, :], ACT.Exp).then_inc(weighed, 1)

                @block.tensor
                def _(pe):
                    for c in (summed,):
                        pe.sem_inc(c, 1)
                    n = turns(pe)
                    with pe.Fori(0, n) as i:
                        for u in range(U):
                            pe.wait_ge(prods, i * U + u + 1)
                            for s in range(S):
                                last = PE.matmul(sums[u][:, 0:T * D], ident[:, :], prod[u % 2][:, s, :],
                                                 start=(s == 0), stop=(s == S - 1))
                            last.then_inc(summed, 1)

                @block.vector
                def _(dve):
                    for c in (*rec_free, *g_free):
                        dve.sem_inc(c, 1)
                    n = turns(dve)
                    V.memset(mrun[:, :, :], LOW)
                    V.memset(srun[:, :, :], 0.0)
                    V.memset(acc[:, :, :], 0.0)
                    dve.drain()
                    with dve.Fori(0, n) as i:
                        tile = []
                        for pair in ((0, 1), (2, 3)):
                            js = []
                            for u in pair:
                                dve.wait_ge(gathered[u], (i + 1) * 16 * S)
                                dve.sem_inc(gate, 1)
                                j = dve.value_load(rec[u][0:1, 0, R_J:R_J + 1], min_val=0, max_val=NT)
                                js.append(j)
                            tile += js
                            for u, j in zip(pair, js):
                                if T > 1:
                                    mask = rec[u][:, 1, S:S + S * T].bitcast(fp32).rearrange("p (s t) -> p s t", s=S)
                                    V.tensor_tensor(zt[u % 2][:, :, :, :],
                                                    bc(own[:, ds(j, 1), :].rearrange("p a (t w) -> p (a t) w", t=T), 1, S),
                                                    bc(mask, 3, ZW), ALU.add)
                                else:
                                    V.tensor_tensor(z[u][:, :, :], g[u][:, :, D:D + H],
                                                    own[:, ds(j, 1), 0:H].to_broadcast([P, S, H]), ALU.add)
                            dve.drain()
                            if T > 1:
                                for u in pair:
                                    V.tensor_reduce(z[u][:, :, :], zt[u % 2][:, :, :, :].rearrange("p s t w -> p s w t"),
                                                    AX.X, ALU.max)
                                dve.drain()
                                for u in pair:
                                    V.tensor_tensor(z[u][:, :, :], z[u][:, :, :], g[u][:, :, D:D + ZW], ALU.add)
                                dve.drain()
                            for u in pair:
                                V.scalar_tensor_tensor(z[u][:, :, :], z[u][:, :, :], 0.2, z[u][:, :, :], ALU.mult, ALU.max)
                            dve.drain()
                            if T > 1:
                                for u in pair:
                                    zz = z[u][:, :, :].rearrange("p s (h k) -> p (s h) k", k=K5)
                                    V.tensor_tensor(zz, zz, bc(soft[:, :], 1, S * H), ALU.mult)
                                dve.drain()
                                for u in pair:
                                    zz = z[u][:, :, :].rearrange("p s (h k) -> p s h k", k=K5)
                                    V.tensor_reduce(al[u][:, :, :], zz, AX.X, ALU.add)
                                dve.drain()
                                for u in pair:
                                    mask = rec[u][:, 1, S:S + S * T].bitcast(fp32).rearrange("p (s t) -> p s t", s=S)
                                    V.tensor_tensor(sc[u][:, 0:S, :].rearrange("p s (t h) -> p s t h", t=T),
                                                    bc(al[u][:, :, :], 2, T), bc(mask, 3, H), ALU.add)
                            else:
                                for u in pair:
                                    V.tensor_tensor(sc[u][:, 0:S, :], z[u][:, :, :],
                                                    bc(rec[u][:, 0, R_ANY:R_ANY + S].bitcast(fp32), 2, H), ALU.add)
                            dve.drain()
                            for u in pair:
                                V.tensor_reduce(mi[u][:, :], sc[u][:, 0:S, :].rearrange("p s l -> p l s"), AX.X, ALU.max)
                            dve.drain()
                            for u, j in zip(pair, js):
                                V.tensor_tensor(mi[u][:, :], mi[u][:, :], flat(mrun[:, ds(j, 1), :]), ALU.max)
                                dve.drain()
                                V.tensor_tensor(sc[u][:, S, :], flat(mrun[:, ds(j, 1), :]), mi[u][:, :], ALU.subtract)
                                V.tensor_tensor(sc[u][:, 0:S, :], sc[u][:, 0:S, :], bc(mi[u][:, :], 1, S),
                                                ALU.subtract).then_inc(scored, 1)
                                dve.drain()
                                V.tensor_copy(flat(mrun[:, ds(j, 1), :]), mi[u][:, :])
                                dve.drain()
                        for pair in ((0, 1), (2, 3)):
                            for u in pair:
                                dve.wait_ge(weighed, i * U + u + 1)
                                dve.wait_ge(summed, (i * U + (u - 1 if u >= 2 else 0)) + 1)
                                if T > 1:
                                    for s in range(S):
                                        V.tensor_tensor(
                                            prod[u % 2][:, s, :].rearrange("p (t h c) -> p t h c", t=T, h=H),
                                            bc(w[u][:, s, :].rearrange("p (t h) -> p t h", t=T), 3, C),
                                            bc(g[u][:, s, 0:D].rearrange("p (h c) -> p h c", h=H), 1, T), ALU.mult)
                                else:
                                    V.tensor_tensor(prod[u % 2][:, :, :].rearrange("p s (h c) -> p s h c", h=H),
                                                    bc(w[u][:, 0:S, :], 3, C),
                                                    g[u][:, :, 0:D].rearrange("p s (h c) -> p s h c", h=H), ALU.mult)
                                V.tensor_reduce(si[u][:, :], w[u][:, 0:S, :].rearrange("p s l -> p l s"), AX.X, ALU.add
                                                ).then_inc(prods, 1)
                                V.drain().then_inc(g_free[u], 1)
                        for u in range(U):
                            j = tile[u]
                            a = acc[:, ds(j, 1), :]
                            V.tensor_tensor(flat(srun[:, ds(j, 1), :]), flat(srun[:, ds(j, 1), :]), w[u][:, S, :], ALU.mult)
                            av = a.rearrange("p a (l c) -> p (a l) c", c=C)
                            V.tensor_tensor(av, av, bc(w[u][:, S, :], 2, C), ALU.mult)
                            dve.drain()
                            dve.wait_ge(summed, i * U + u + 2)
                            V.tensor_tensor(flat(srun[:, ds(j, 1), :]), flat(srun[:, ds(j, 1), :]), si[u][:, :], ALU.add)
                            V.tensor_tensor(flat(a), flat(a), sums[u][:, 0:T * D], ALU.add).then_inc(rec_free[u], 1)
                            dve.drain()

        def normalised(v, t, mean, var, tag):
            half = sem(f"variance_{tag}")
            root = sem(f"root_{tag}")

            def vector(dve):
                V.tensor_reduce(mean, v, AX.X, ALU.add)
                dve.drain()
                V.tensor_scalar(mean, mean, 1.0 / D, None, ALU.mult)
                dve.drain()
                V.tensor_tensor(v, v, bc(mean, 2, D), ALU.subtract)
                dve.drain()
                V.tensor_tensor(t, v, v, ALU.mult)
                dve.drain()
                V.tensor_reduce(var, t, AX.X, ALU.add)
                dve.drain()
                V.tensor_scalar(var, var, 1.0 / D, 1e-5, ALU.mult, ALU.add).then_inc(half, 1)
                dve.wait_ge(root, 1)
                V.reciprocal(var, var)
                dve.drain()
                V.tensor_tensor(v, v, bc(var, 2, D), ALU.mult)
                dve.drain()

            def scalar(act):
                act.wait_ge(half, 1)
                A.activation(var, var, ACT.Sqrt).then_inc(root, 1)
            return vector, scalar

        with ExitStack() as att:
            big = sb("big", [P, NTP * T4 * A0], fp32, att)
            mrun = sb("mrun", [P, NTP, T4 * H], fp32, att)
            srun = sb("srun", [P, NTP, T4 * H], fp32, att)
            mean = sb("mean", [P, NTP], fp32, att)
            var = sb("var", [P, NTP], fp32, att)
            W2 = 2 * A0
            SUMS = NTP * T4 * D
            stage0 = big[:, 0:NTP * T4 * A0].rearrange("p (j w) -> p j w", j=NTP)
            acc0 = big[:, 0:NTP * T4 * D].rearrange("p (j w) -> p j w", j=NTP)

            def products(T):
                return [h[:, v * S * T:(v + 1) * S * T, :].rearrange("p (s t) c -> p s (t c)", s=S)
                        for v in range(2)]

            def at0(a, z):
                return lambda t: flat(stage0[:, ds(t, 1), a:z])

            r0 = flat(rhs0[:, :, :])
            node_table("L0", xr, rhs0,
                       [(0, 0, W2, r0[:, 0:W2], [(0, W2, at0(0, W2))]),
                        (1, 0, W2, r0[:, W2:2 * W2], [(0, W2, at0(W2, 2 * W2))]),
                        (2, 0, T4 * 20, flat(rhs0i[:, :, :]),
                         [(0, T4 * 20, lambda t: flat(own[:, ds(t, 1), :]))])],
                       stage0, tab0_d)
            with nc.Block() as block:
                @block.vector
                def _(dve):
                    V.tensor_tensor(xr[:, :, :], xr[:, :, :], bc(bias[:, 0, :], 1, NTP), ALU.add)
                    dve.drain()
                    V.tensor_tensor(xr[:, :, :], xr[:, :, :], stage0[:, :, 0:D], ALU.add)
            attention("L0", T4, tab0_d.rearrange("n (t w) -> (n t) w", t=T4), A0, (rec_d, rec0_d), acc0, mrun, srun,
                      products(T4), big, SUMS)
            ln_v, ln_s = normalised(xr[:, :, :], h[:, :, :], mean[:, :], var[:, :], "L0")
            with nc.Block() as block:
                @block.vector
                def _(dve):
                    V.tensor_scalar(srun[:, :, :], srun[:, :, :], 1e-30, None, ALU.max)
                    dve.drain()
                    V.reciprocal(srun[:, :, :], srun[:, :, :])
                    dve.drain()
                    for t in range(T4):
                        V.tensor_scalar(srun[:, :, t * H:(t + 1) * H], srun[:, :, t * H:(t + 1) * H],
                                        impt[:, t:t + 1], None, ALU.mult)
                    dve.drain()
                    for t in range(T4):
                        for k in range(H):
                            a = t * D + k * C
                            V.tensor_tensor(h[:, :, k * C:(k + 1) * C], acc0[:, :, a:a + C],
                                            bc(srun[:, :, t * H + k], 2, C), ALU.mult)
                        dve.drain()
                        V.tensor_tensor(xr[:, :, :], xr[:, :, :], h[:, :, :], ALU.add)
                        dve.drain()
                    ln_v(dve)
                    V.tensor_copy(h[:, :, :], xr[:, :, :])

                @block.scalar
                def _(act):
                    ln_s(act)

            fresh_semaphores()
            stage1 = big[:, 0:NTP * A1].rearrange("p (j w) -> p j w", j=NTP)
            acc1 = big[:, NTP * A1:NTP * (A1 + D)].rearrange("p (j w) -> p j w", j=NTP)
            m1 = mrun[:, :, 0:H]
            s1 = srun[:, :, 0:H]
            for l in range(3):
                node_table(f"L1{l}", h, rhs1,
                           [(0, 0, D + 2 * H, rhs1[:, l, :],
                             [(0, A1, lambda t: flat(stage1[:, ds(t, 1), :])),
                              (A1, A1 + H, lambda t: flat(own[:, ds(t, 1), 0:H]))])],
                           stage1, tab1_d[l])
                attention(f"L1{l}", 1, tab1_d[l], A1, (rec_d,), acc1, m1, s1, products(1),
                          big, SUMS)
                if l == 2:
                    ln_v, ln_s = normalised(xr[:, :, :], h[:, :, :], mean[:, :], var[:, :], "L1")
                with nc.Block() as block:
                    @block.vector
                    def _(dve):
                        V.tensor_scalar(s1, s1, 1e-16, None, ALU.add)
                        dve.drain()
                        V.reciprocal(s1, s1)
                        dve.drain()
                        for k in range(H):
                            V.tensor_tensor(h[:, :, k * C:(k + 1) * C], acc1[:, :, k * C:(k + 1) * C],
                                            bc(s1[:, :, k], 2, C), ALU.mult)
                        dve.drain()
                        V.tensor_tensor(h[:, :, :], h[:, :, :], bc(bias[:, l + 1, :], 1, NTP), ALU.add)
                        dve.drain()
                        if l < 2:
                            V.tensor_scalar(h[:, :, :], h[:, :, :], 0.0, None, ALU.max)
                        else:
                            V.tensor_tensor(xr[:, :, :], xr[:, :, :], h[:, :, :], ALU.add)
                            dve.drain()
                            ln_v(dve)

                    if l == 2:
                        @block.scalar
                        def _(act):
                            ln_s(act)
                fresh_semaphores()

        with ExitStack() as mlp:
            big = sb("big2", [P, NTP * HID], fp32, mlp)
            w1 = sb("w1", [P, 2, HID], fp32, mlp)
            w2 = sb("w2", [P, 2, HID], fp32, mlp)
            w3 = sb("w3", [P, 2, HID], fp32, mlp)
            w4 = sb("w4", [P, 3, HID], fp32, mlp)
            w5 = sb("w5", [P, 2, D], fp32, mlp)
            ba = sb("ba", [P, 2], fp32, mlp)
            bb = sb("bb", [P, 2], fp32, mlp)
            bcr = sb("bcr", [P, HID], fp32, mlp)
            b4 = sb("b4", [P, HID], fp32, mlp)
            b5 = sb("b5", [P, D], fp32, mlp)
            wm_in = sem("mlp_weights_in")
            with nc.Block() as block:
                @block.sync
                def _(sp):
                    for to, frm in ((w1[:, :, :], w1a), (w2[:, :, :], w1b), (w3[:, :, :], w1c), (w4[:, :, :], w2a),
                                    (w5[:, :, :], w2b), (ba[:, :], b1a), (bb[:, :], b1b),
                                    (bcr[:, :], b1c.partition_broadcast(P)), (b4[:, :], b2a.partition_broadcast(P)),
                                    (b5[:, :], b2b.partition_broadcast(P))):
                        sp.dma_start(to, frm).then_inc(wm_in, 16)
                    sp.wait_ge(wm_in, 160)
            stage2 = big[:, :].rearrange("p (j w) -> p j w", j=NTP)
            node_table("L2", xr, w1,
                       [(0, 0, HID, w1[:, 0, :], [(0, HID, lambda t: flat(stage2[:, ds(t, 1), :]))])],
                       stage2, tab2_d)

            with ExitStack() as ph:
                total = big[:, :].rearrange("p (j f n) -> p j f n", j=NTP, f=2)
                rec = [sb(f"rec_m{u}", [P, REC], i32, ph) for u in range(U)]
                gx = [sb(f"gx{u}", [P, S, HID], fp32, ph) for u in range(U)]
                ge = [sb(f"ge{u}", [P, S, D], fp32, ph) for u in range(U)]
                off = [sb(f"off{u}", [P, S], bf16, ph) for u in range(U)]
                eT = [sb(f"eT{v}", [P, S * P], fp32, ph) for v in range(2)]
                h1 = [sb(f"h1_{f}", [P, S * P], fp32, ph) for f in range(2)]
                h2 = [sb(f"h2_{f}", [P, S, P], fp32, ph) for f in range(2)]
                part = [sb(f"partial{f}", [P, P], fp32, ph) for f in range(2)]
                psT = [pb(f"psT{v}", [P, 512], fp32, ph) for v in range(2)]
                ps1 = [pb(f"ps1_{f}", [P, 512], fp32, ph) for f in range(2)]
                ps2 = [pb(f"ps2_{f}", [P, 512], fp32, ph) for f in range(2)]
                rec_in = [sem(f"rec_in_m{u}") for u in range(U)]
                rec_free = [sem(f"rec_free_m{u}") for u in range(U)]
                gathered = [sem(f"gathered_m{u}") for u in range(U)]
                rows_used = [sem(f"rows_used_m{u}") for u in range(U)]
                gate = sem("gate_m")
                gate_v = sem("gate_mv")
                masks = sem("masks_ready_m")
                turned = sem("edges_transposed_m")
                eT_ok = sem("edges_stored_m")
                lin1 = sem("hidden1_linear_m")
                act1 = sem("hidden1_ready_m")
                lin2 = sem("hidden2_linear_m")
                act2 = sem("hidden2_ready_m")
                summed = sem("hidden2_summed_m")
                block = ph.enter_context(nc.Block())

                def turns(eng):
                    return eng.value_load(trips[0:1, 0:1], min_val=1, max_val=GMAX // U)

                @block.sync
                def _(sp):
                    n = turns(sp)
                    with sp.Fori(0, n) as i:
                        for u in range(U):
                            sp.wait_ge(rec_free[u], i + 1)
                            sp.dma_start(rec[u][:, :], rec_d[ds(i * U + u, 1), :, :]
                                         .rearrange("a p w -> (a p) w")).then_inc(rec_in[u], 16)

                @block.gpsimd
                def _(pool):
                    n = turns(pool)
                    with pool.Fori(0, n) as i:
                        for u in range(U):
                            pool.wait_ge(rec_in[u], (i + 1) * 16)
                            pool.wait_ge(rows_used[u], i + 1)
                            pool.sem_inc(gate, 1)
                            for s in range(S):
                                G.indirect_dma_start(out=ge[u][:, s, :], out_offset=None, in_=edge_attr,
                                                     in_offset=bass.IndirectOffsetOnAxis(
                                                         ap=rec[u][:, R_EID + s:R_EID + s + 1].bitcast(u32), axis=0)
                                                     ).then_inc(gathered[u], 16)
                            for s in range(S):
                                G.indirect_dma_start(out=gx[u][:, s, :], out_offset=None, in_=tab2_d,
                                                     in_offset=bass.IndirectOffsetOnAxis(
                                                         ap=rec[u][:, R_SRC + s:R_SRC + s + 1].bitcast(u32), axis=0)
                                                     ).then_inc(gathered[u], 16)

                @block.tensor
                def _(pe):
                    for c in (lin2, *rows_used):
                        pe.sem_inc(c, 1)
                    n = turns(pe)
                    with pe.Fori(0, n) as i:
                        for u in range(U):
                            g = i * U + u
                            pe.wait_ge(gathered[u], (i + 1) * 32 * S)
                            pe.wait_ge(eT_ok, (g - 1 if u else g) + 1)
                            for s in range(S):
                                last = PE.transpose(psT[u % 2][:, s * P:(s + 1) * P], ge[u][:, s, :], ident[:, :])
                            last.then_inc(turned, 1)
                            pe.wait_ge(act1, g * 2 + 1)
                            for f in range(2):
                                for s in range(S):
                                    last = PE.matmul(ps1[f][:, s * P:(s + 1) * P], gx[u][:, s, f * P:(f + 1) * P],
                                              ident[:, :], start=(s == 0), stop=False, skip_group_check=True)
                            last.then_inc(rows_used[u], 1)
                            pe.wait_ge(eT_ok, g + 2)
                            for f in range(2):
                                last = PE.matmul(ps1[f][:, :], w1[:, 1, f * P:(f + 1) * P], eT[u % 2][:, :],
                                                 start=False, stop=True, skip_group_check=True)
                                last.then_inc(lin1, 1)
                            pe.wait_ge(act2, g * 2 + 1)
                            pe.wait_ge(masks, g + 1)
                            for f in range(2):
                                for s in range(S):
                                    PE.matmul(ps2[f][:, s * P:(s + 1) * P],
                                              off[u][:, s:s + 1].to_broadcast([P, P]), identb[:, :],
                                              start=(s == 0), stop=False, skip_group_check=True)
                            pe.wait_ge(act1, g * 2 + 2 + 1)
                            for f in range(2):
                                for k in range(2):
                                    last = PE.matmul(ps2[f][:, :], w2[:, k, f * P:(f + 1) * P], h1[k][:, :],
                                                     start=False, stop=(k == 1), skip_group_check=True)
                                last.then_inc(lin2, 1)

                @block.scalar
                def _(act):
                    for c in (eT_ok, act1, act2):
                        act.sem_inc(c, 1)
                    n = turns(act)
                    with act.Fori(0, n) as i:
                        for u in range(U):
                            g = i * U + u
                            act.wait_ge(turned, g + 1)
                            A.activation(eT[u % 2][:, :], psT[u % 2][:, :], ACT.Copy).then_inc(eT_ok, 1)
                            act.wait_ge(lin2, g * 2 + 1)
                            for f in range(2):
                                act.wait_ge(lin1, g * 2 + f + 1)
                                A.activation(h1[f][:, :], ps1[f][:, :], ACT.Relu, bias=ba[:, f:f + 1]).then_inc(act1, 1)
                            act.wait_ge(summed, g * 2 + 1)
                            for f in range(2):
                                act.wait_ge(lin2, g * 2 + f + 2)
                                A.activation(flat(h2[f][:, :, :]), ps2[f][:, :], ACT.Relu, bias=bb[:, f:f + 1]
                                             ).then_inc(act2, 1)

                @block.vector
                def _(dve):
                    for c in (*rec_free, summed):
                        dve.sem_inc(c, 1)
                    n = turns(dve)
                    V.memset(big[:, :], 0.0)
                    dve.drain()
                    with dve.Fori(0, n) as i:
                        for u in range(U):
                            g = i * U + u
                            dve.wait_ge(rec_in[u], (i + 1) * 16)
                            dve.sem_inc(gate_v, 1)
                            j = dve.value_load(rec[u][0:1, R_J:R_J + 1], min_val=0, max_val=NT)
                            V.tensor_copy(off[u][:, :], rec[u][:, R_ANY:R_ANY + S].bitcast(fp32)).then_inc(masks, 1)
                            for f in range(2):
                                dve.wait_ge(act2, g * 2 + f + 2)
                                V.tensor_reduce(part[f][:, :], h2[f][:, :, :].rearrange("p s n -> p n s"), AX.X, ALU.add
                                                ).then_inc(summed, 1)
                            dve.drain()
                            for f in range(2):
                                t = total[:, ds(j, 1), f, :].rearrange("p a n -> p (a n)")
                                last = V.tensor_tensor(t, t, part[f][:, :], ALU.add)
                            dve.wait_ge(gathered[u], (i + 1) * 32 * S)
                            dve.sem_inc(gate_v, 1)
                            V.drain().then_inc(rec_free[u], 1)

            with ExitStack() as ph:
                inv = sb("inv", [P, NTP], fp32, ph)
                has = sb("has", [P, NTP], fp32, ph)
                fx = sb("fx", [P, 2, P], fp32, ph)
                su = [sb(f"su{v}", [P, 2, P], fp32, ph) for v in range(2)]
                xc = [sb(f"xc{v}", [P, P], fp32, ph) for v in range(2)]
                ag = [sb(f"ag{v}", [P, HID], fp32, ph) for v in range(2)]
                kT = [sb(f"kT{v}", [P, 3, P], fp32, ph) for v in range(2)]
                zz = [sb(f"zz{v}", [P, HID], fp32, ph) for v in range(2)]
                zT = [sb(f"zT{v}", [P, 2, P], fp32, ph) for v in range(2)]
                pA = [pb(f"pA{v}", [P, 512], fp32, ph) for v in range(2)]
                pT = [pb(f"pT{v}", [P, 512], fp32, ph) for v in range(2)]
                pZ = [pb(f"pZ{v}", [P, 512], fp32, ph) for v in range(2)]
                pO = [pb(f"pO{v}", [P, 512], fp32, ph) for v in range(2)]
                total = big[:, :].rearrange("p (j f n) -> p j f n", j=NTP, f=2)
                fetched = sem("sums_fetched_n")
                aggp = sem("agg_product_n")
                agg = sem("agg_ready_n")
                tr1 = sem("inputs_transposed_n")
                st1 = sem("inputs_stored_n")
                lin = sem("hidden_linear_n")
                hid = sem("hidden_ready_n")
                tr2 = sem("hidden_transposed_n")
                st2 = sem("hidden_stored_n")
                fin = sem("mlp_output_n")
                added = sem("mlp_output_added_n")
                block = ph.enter_context(nc.Block())

                @block.scalar
                def _(act):
                    with act.Fori(0, NTP // 2) as i:
                        for v in range(2):
                            t = i * 2 + v
                            act.wait_ge(fin, i * 2 + 1)
                            A.activation(su[v][:, :, :], total[:, ds(t, 1), :, :].rearrange("p a f n -> p (a f) n"),
                                         ACT.Copy)
                            A.activation(xc[v][:, :], flat(xr[:, ds(t, 1), :]), ACT.Copy).then_inc(fetched, 1)
                        for v in range(2):
                            act.wait_ge(tr1, i * 2 + v + 1)
                            A.activation(kT[v][:, :, :], pT[v][:, 0:3 * P].rearrange("p (a n) -> p a n", a=3),
                                         ACT.Copy).then_inc(st1, 1)
                        for v in range(2):
                            act.wait_ge(tr2, i * 2 + v + 1)
                            A.activation(zT[v][:, :, :], pT[v][:, 0:2 * P].rearrange("p (a n) -> p a n", a=2),
                                         ACT.Copy).then_inc(st2, 1)

                @block.tensor
                def _(pe):
                    for c in (fin,):
                        pe.sem_inc(c, 1)
                    with pe.Fori(0, NTP // 2) as i:
                        for v in range(2):
                            pe.wait_ge(fetched, i * 2 + v + 1)
                            for k in range(2):
                                last = PE.matmul(pA[v][:, 0:HID], su[v][:, k, :], w3[:, k, :], start=(k == 0), stop=(k == 1))
                            last.then_inc(aggp, 1)
                        for v in range(2):
                            pe.wait_ge(agg, i * 2 + v + 1)
                            PE.transpose(pT[v][:, 0:P], xc[v][:, :], ident[:, :])
                            for k in range(2):
                                last = PE.transpose(pT[v][:, (k + 1) * P:(k + 2) * P], ag[v][:, k * P:(k + 1) * P],
                                                    ident[:, :])
                            last.then_inc(tr1, 1)
                        for v in range(2):
                            pe.wait_ge(st1, i * 2 + v + 1)
                            for k in range(3):
                                last = PE.matmul(pZ[v][:, 0:HID], kT[v][:, k, :], w4[:, k, :], start=(k == 0), stop=(k == 2))
                            last.then_inc(lin, 1)
                        for v in range(2):
                            pe.wait_ge(hid, i * 2 + v + 1)
                            for k in range(2):
                                last = PE.transpose(pT[v][:, k * P:(k + 1) * P], zz[v][:, k * P:(k + 1) * P], ident[:, :])
                            last.then_inc(tr2, 1)
                        for v in range(2):
                            pe.wait_ge(st2, i * 2 + v + 1)
                            pe.wait_ge(added, i * 2 + 1)
                            for k in range(2):
                                last = PE.matmul(pO[v][:, 0:D], zT[v][:, k, :], w5[:, k, :], start=(k == 0), stop=(k == 1))
                            last.then_inc(fin, 1)

                @block.vector
                def _(dve):
                    for c in (added,):
                        dve.sem_inc(c, 1)
                    V.tensor_scalar(inv[:, :], degI[:, :], 1.0, None, ALU.max)
                    V.tensor_scalar(has[:, :], degI[:, :], 1.0, None, ALU.min)
                    dve.drain()
                    V.reciprocal(inv[:, :], inv[:, :])
                    dve.drain()
                    with dve.Fori(0, NTP // 2) as i:
                        for v in range(2):
                            t = i * 2 + v
                            dve.wait_ge(aggp, i * 2 + v + 1)
                            V.tensor_scalar(ag[v][:, :], pA[v][:, 0:HID], inv[:, ds(t, 1)], None, ALU.mult)
                            V.drain()
                            V.scalar_tensor_tensor(ag[v][:, :], bcr[:, :], has[:, ds(t, 1)], ag[v][:, :],
                                                   ALU.mult, ALU.add).then_inc(agg, 1)
                        for v in range(2):
                            dve.wait_ge(lin, i * 2 + v + 1)
                            V.tensor_tensor(zz[v][:, :], pZ[v][:, 0:HID], b4[:, :], ALU.add)
                            V.drain()
                            V.tensor_scalar(zz[v][:, :], zz[v][:, :], 0.0, None, ALU.max).then_inc(hid, 1)
                        for v in range(2):
                            t = i * 2 + v
                            dve.wait_ge(fin, i * 2 + v + 2)
                            x_ = flat(xr[:, ds(t, 1), :])
                            V.tensor_tensor(x_, x_, pO[v][:, 0:D], ALU.add).then_inc(added, 1)

            with ExitStack() as ph:
                mean = sb("mean2", [P, NTP], fp32, ph)
                var = sb("var2", [P, NTP], fp32, ph)
                ln_v, ln_s = normalised(xr[:, :, :], h[:, :, :], mean[:, :], var[:, :], "L2")
                block = ph.enter_context(nc.Block())

                @block.vector
                def _(dve):
                    V.tensor_tensor(xr[:, :, :], xr[:, :, :], bc(b5[:, :], 1, NTP), ALU.add)
                    dve.drain()
                    ln_v(dve)

                @block.scalar
                def _(act):
                    ln_s(act)

        fresh_semaphores()

        with ExitStack() as ph:
            w3 = sb("w3T_", [P, D], fp32, ph)
            iso = sb("iso", [P, NTP], fp32, ph)
            rec = [sb(f"rec_s{u}", [P, REC], i32, ph) for u in range(U)]
            spread = [sb(f"spread{v}", [P, S, P], fp32, ph) for v in range(2)]
            same = [sb(f"same{v}", [P, S, P], fp32, ph) for v in range(2)]
            before = [sb(f"before{v}", [P, S, P], fp32, ph) for v in range(2)]
            dup = [sb(f"dup{v}", [P, S], fp32, ph) for v in range(2)]
            away = [sb(f"away{v}", [P, S], fp32, ph) for v in range(2)]
            to = [sb(f"to{u}", [P, S], u32, ph) for u in range(U)]
            msg = [sb(f"msg{u}", [P, S, D], fp32, ph) for u in range(U)]
            spare = sb("spare", [P, 1], fp32, ph)
            blank = sb("blank", [P, D], fp32, ph)
            blank_ok = sem("blank_ready")
            scaled = [sb(f"scaled{v}", [P, D], fp32, ph) for v in range(2)]
            psR = [pb(f"psR{v}", [P, 512], fp32, ph) for v in range(2)]
            psM = [pb(f"psM{v}", [P, 512], fp32, ph) for v in range(2)]
            w_in = sem("w3_in")
            root = sem("root_s")
            deg_ok = sem("deg_clamped_s")
            x_out = sem("x3_stored")
            rec_in = [sem(f"rec_in_s{u}") for u in range(U)]
            spr_ok = sem("sources_spread")
            rows_ok = sem("sources_in_rows")
            same_ok = sem("equality_ready")
            to_ok = sem("targets_ready")
            msg_ps = sem("messages_summed")
            msg_ok = sem("messages_stored")
            sc_ok = sem("scaled_ready")
            used = sem("slots_used_s")
            added = [sem(f"added_{s}") for s in range(S)]
            gate = sem("gate_s")
            gate_v = sem("gate_sv")

            with nc.Block() as block:
                @block.sync
                def _(sp):
                    sp.dma_start(w3[:, :], w3T).then_inc(w_in, 16)
                    sp.wait_ge(w_in, 16)

                @block.gpsimd
                def _(pool):
                    for j in range(NTP):
                        G.indirect_dma_start(out=x3_d, out_offset=bass.IndirectOffsetOnAxis(
                            ap=nid[:, j:j + 1].bitcast(u32), axis=0), in_=xr[:, j, :], in_offset=None).then_inc(x_out, 16)
                    pool.wait_ge(blank_ok, 1)
                    for s in range(S):
                        pool.dma_start(sum_d[s][NPAD:ROWS, :], blank[:, :]).then_inc(added[s], 16)
                    pool.wait_ge(x_out, 16 * NTP)
                    for s in range(S):
                        pool.wait_ge(added[s], 16)

                @block.vector
                def _(dve):
                    V.memset(blank[:, :], 0.0).then_inc(blank_ok, 1)
                    V.tensor_scalar(iso[:, :], degO[:, :], 1.0, None, ALU.max).then_inc(deg_ok, 1)
                    V.tensor_scalar(spare[:, :], place[:, :], float(NT * P), None, ALU.add)
                    dve.wait_ge(root, 1)
                    V.reciprocal(iso[:, :], iso[:, :])
                    dve.drain()
                    V.tensor_tensor(h[:, :, :], xr[:, :, :], bc(iso[:, :], 2, D), ALU.mult)

                @block.scalar
                def _(act):
                    act.wait_ge(deg_ok, 1)
                    A.activation(iso[:, :], iso[:, :], ACT.Sqrt).then_inc(root, 1)

            with nc.Block() as block:
                def turns(eng):
                    return eng.value_load(trips[0:1, 0:1], min_val=1, max_val=GMAX // U)

                @block.sync
                def _(sp):
                    n = turns(sp)
                    with sp.Fori(0, n) as i:
                        for u in range(U):
                            sp.wait_ge(used, i * U + 1)
                            sp.dma_start(rec[u][:, :], rec_d[ds(i * U + u, 1), :, :]
                                         .rearrange("a p w -> (a p) w")).then_inc(rec_in[u], 16)

                @block.tensor
                def _(pe):
                    for c in (msg_ps,):
                        pe.sem_inc(c, 1)
                    n = turns(pe)
                    with pe.Fori(0, n) as i:
                        for u in range(U):
                            g, v = i * U + u, u % 2
                            pe.wait_ge(spr_ok, g + 1)
                            for s in range(S):
                                last = PE.transpose(psR[v][:, s * P:(s + 1) * P], spread[v][:, s, :], ident[:, :])
                            last.then_inc(rows_ok, 1)
                            pe.wait_ge(same_ok, g + 1)
                            pe.wait_ge(sc_ok, g + 1)
                            pe.wait_ge(msg_ok, (g - 1 if u else g) + 1)
                            for s in range(S):
                                last = PE.matmul(psM[v][:, s * P:(s + 1) * P], same[v][:, s, :], scaled[v][:, :],
                                                 start=True, stop=True)
                            last.then_inc(msg_ps, 1)

                @block.scalar
                def _(act):
                    act.sem_inc(msg_ok, 1)
                    n = turns(act)
                    with act.Fori(0, n) as i:
                        for u in range(U):
                            g, v = i * U + u, u % 2
                            act.wait_ge(msg_ps, g + 2)
                            for s in range(S):
                                act.wait_ge(added[s], i * 16 * U + 16)
                            A.activation(flat(msg[u][:, :, :]), psM[v][:, :], ACT.Copy).then_inc(msg_ok, 1)

                @block.vector
                def _(dve):
                    dve.sem_inc(used, 1)
                    n = turns(dve)
                    with dve.Fori(0, n) as i:
                        for u in range(U):
                            g, v = i * U + u, u % 2
                            dve.wait_ge(rec_in[u], (i + 1) * 16)
                            dve.sem_inc(gate_v, 1)
                            j = dve.value_load(rec[u][0:1, R_J:R_J + 1], min_val=0, max_val=NT)
                            srcs = rec[u][:, R_SUM:R_SUM + S].bitcast(fp32)
                            dve.wait_ge(msg_ps, (g - 1 if u else g) + 1)
                            V.tensor_copy(scaled[v][:, :], flat(h[:, ds(j, 1), :])).then_inc(sc_ok, 1)
                            V.tensor_copy(spread[v][:, :, :], bc(srcs, 2, P)).then_inc(spr_ok, 1)
                            dve.wait_ge(rows_ok, g + 1)
                            V.tensor_tensor(same[v][:, :, :], psR[v][:, :].rearrange("p (s n) -> p s n", s=S),
                                            bc(srcs, 2, P), ALU.is_equal).then_inc(same_ok, 1)
                            dve.drain()
                            V.tensor_tensor(before[v][:, :, :], same[v][:, :, :], bc(lower[:, :], 1, S), ALU.mult)
                            V.tensor_tensor(away[v][:, :], spare[:, :].to_broadcast([P, S]), srcs, ALU.subtract)
                            dve.drain()
                            V.tensor_reduce(dup[v][:, :], before[v][:, :, :], AX.X, ALU.max)
                            dve.drain()
                            V.tensor_tensor(away[v][:, :], away[v][:, :], dup[v][:, :], ALU.mult)
                            dve.drain()
                            for s in range(S):
                                dve.wait_ge(added[s], i * 16 * U + 16)
                            V.tensor_tensor(to[u][:, :], away[v][:, :], srcs, ALU.add).then_inc(to_ok, 1)
                            V.drain().then_inc(used, 1)

                @block.gpsimd
                def _(pool):
                    n = turns(pool)
                    with pool.Fori(0, n) as i:
                        for u in range(U):
                            g = i * U + u
                            pool.wait_ge(to_ok, g + 1)
                            pool.wait_ge(msg_ok, g + 2)
                            for s in range(S):
                                pool.wait_ge(added[s], g * 16 + 16)
                                pool.sem_inc(gate, 1)
                                G.indirect_dma_start(out=sum_d[s], out_offset=bass.IndirectOffsetOnAxis(
                                    ap=to[u][:, s:s + 1], axis=0), in_=msg[u][:, s, :], in_offset=None,
                                    compute_op=ALU.add).then_inc(added[s], 16)
                    for s in range(S):
                        pool.wait_ge(added[s], n * 16 * U + 16)
                    pool.sem_inc(gate, 1)

            with ExitStack() as fi:
                q = [sb(f"q{s}", [P, NT, D], fp32, fi) for s in range(2)]
                xn = sb("xn", [P, NT, D], fp32, fi)
                ison = sb("ison", [P, NT], fp32, fi)
                hc = [sb(f"hcf{v}", [P, P], fp32, fi) for v in range(2)]
                ht = [sb(f"htf{v}", [P, P], fp32, fi) for v in range(2)]
                mean = sb("mean3", [P, NT], fp32, fi)
                var = sb("var3", [P, NT], fp32, fi)
                pt = [pb(f"ptf{v}", [P, 512], fp32, fi) for v in range(2)]
                pm = [pb(f"pmf{v}", [P, 512], fp32, fi) for v in range(2)]
                xn_in = sem("xn_in")
                q_in = sem("sums_in")
                q_used = sem("sums_used")
                mroot = sem("root_f")
                agg_ok = sem("aggregate_ready")
                fetched = sem("fetched_f")
                turned = sem("turned_f")
                stored = sem("stored_f")
                mult = sem("mult_f")
                relud = sem("relu_f")
                out_ok = sem("out_ready")
                out_out = sem("out_stored")
                sq = h[:, 0:NT, :]
                agg = q[0]

                with nc.Block() as block:
                    @block.sync
                    def _(sp):
                        def rows(t):
                            return t[0:NT * P, :].rearrange("(j p) c -> p j c", p=P)
                        sp.dma_start(xn[:, :, :], rows(x3_d)).then_inc(xn_in, 16)
                        sp.dma_start(q[0][:, :, :], rows(sum_d[0])).then_inc(q_in, 16)
                        for s in range(1, S):
                            if s > 1:
                                sp.wait_ge(q_used, s - 1)
                            sp.dma_start(q[1][:, :, :], rows(sum_d[s])).then_inc(q_in, 16)
                        sp.wait_ge(xn_in, 16)

                    @block.scalar
                    def _(act):
                        A.activation(ison[:, :], degOn[:, :], ACT.Sqrt).then_inc(mroot, 1)

                    @block.vector
                    def _(dve):
                        for s in range(1, S):
                            dve.wait_ge(q_in, 16 * (s + 1))
                            V.tensor_tensor(agg[:, :, :], agg[:, :, :], q[1][:, :, :], ALU.add).then_inc(q_used, 1)
                            dve.drain()
                        dve.wait_ge(mroot, 1)
                        V.reciprocal(ison[:, :], ison[:, :])
                        dve.drain()
                        V.tensor_tensor(agg[:, :, :], agg[:, :, :], bc(ison[:, :], 2, D), ALU.mult)

                def per_tile(eng, body):
                    with eng.Fori(0, NT // 2) as i:
                        body(i, range(2))
                    body(NT // 2, range(1))

                with nc.Block() as block:
                    @block.scalar
                    def _(act):
                        act.sem_inc(stored, 1)
                        def body(i, vs):
                            for v in vs:
                                act.wait_ge(turned, i * 2 + 1)
                                A.activation(hc[v][:, :], flat(agg[:, ds(i * 2 + v, 1), :]), ACT.Copy).then_inc(fetched, 1)
                            for v in vs:
                                act.wait_ge(turned, i * 2 + v + 2)
                                act.wait_ge(mult, i * 2 + 1)
                                A.activation(ht[v][:, :], pt[v][:, 0:P], ACT.Copy).then_inc(stored, 1)
                        per_tile(act, body)

                    @block.tensor
                    def _(pe):
                        pe.sem_inc(turned, 1)
                        pe.sem_inc(mult, 1)
                        def body(i, vs):
                            for v in vs:
                                pe.wait_ge(fetched, i * 2 + v + 1)
                                pe.wait_ge(stored, i * 2 + 1)
                                PE.transpose(pt[v][:, 0:P], hc[v][:, :], ident[:, :]).then_inc(turned, 1)
                            for v in vs:
                                pe.wait_ge(stored, i * 2 + v + 2)
                                pe.wait_ge(relud, i * 2 + 1)
                                PE.matmul(pm[v][:, 0:D], ht[v][:, :], w3[:, :], start=True, stop=True).then_inc(mult, 1)
                        per_tile(pe, body)

                    @block.vector
                    def _(dve):
                        dve.sem_inc(relud, 1)
                        def body(i, vs):
                            for v in vs:
                                dve.wait_ge(mult, i * 2 + v + 2)
                                x_ = flat(xn[:, ds(i * 2 + v, 1), :])
                                V.scalar_tensor_tensor(x_, pm[v][:, 0:D], 0.0, x_, ALU.max, ALU.add).then_inc(relud, 1)
                        per_tile(dve, body)

                ln_v, ln_s = normalised(xn[:, :, :], sq, mean[:, :], var[:, :], "L3")
                with nc.Block() as block:
                    @block.vector
                    def _(dve):
                        ln_v(dve)
                        V.drain().then_inc(out_ok, 1)

                    @block.scalar
                    def _(act):
                        ln_s(act)

                    @block.sync
                    def _(sp):
                        sp.wait_ge(out_ok, 1)
                        full = N // P
                        sp.dma_start(out[0:full * P, :].rearrange("(j p) c -> p j c", p=P),
                                     xn[:, 0:full, :]).then_inc(out_out, 16)
                        sp.dma_start(out[full * P:N, :], xn[0:N - full * P, full, :]).then_inc(out_out, 16)
                        sp.wait_ge(out_out, 32)


def lay_out(inputs):
    import numpy as np
    g = {k: np.asarray(v) for k, v in inputs.items()}

    def padded(a, rows, value=0):
        return np.concatenate([a, np.full((rows - a.shape[0],) + a.shape[1:], value, a.dtype)])

    arrays = {"x": padded(g["x"], NPAD)}
    for name in ("src", "dst"):
        arrays[name] = padded(g[name], EPAD, NT * P).reshape(P, EC)
    s, t = padded(g["src"], E + S + 1), padded(g["edge_type_4"], E + S + 1)
    arrays["windows"] = np.stack([a[k:k + E + 1] for a in (s, t) for k in range(S)], axis=1)
    arrays["edge_attr"] = g["edge_attr_128"]
    W0 = g["L0_gnn_W"]
    arrays["W0"] = W0.transpose(1, 0, 2)
    arrays["W0T"] = W0.transpose(2, 0, 1)
    att = g["L0_gnn_att_vectors"]
    for name, part in (("attI", att[:, :, :C]), ("attJ", att[:, :, C:])):
        a = np.zeros((H, C, H, K5), np.float32)
        for h in range(H):
            a[h, :, h, :] = part[:, h, :].T
        arrays[name] = a.reshape(D, H * K5)
    arrays["probs"] = g["L0_gnn_confounder_probs"]
    arrays["importance"] = g["L0_gnn_edge_importance"]
    arrays["bias0"] = g["L0_gnn_bias"]
    for name in ("Ws", "Wd"):
        arrays[name] = g["L1_gnn_" + name].transpose(1, 0, 2)
        arrays[name + "T"] = g["L1_gnn_" + name].transpose(2, 0, 1)
    for name, part in (("attS", g["L1_gnn_att_s"]), ("attD", g["L1_gnn_att_d"])):
        a = np.zeros((H, C, 3, H), np.float32)
        for h in range(H):
            a[h, :, :, h] = part[:, h, :].T
        arrays[name] = a.reshape(D, 3, H)
    arrays["bias1"] = g["L1_gnn_b"]
    arrays["w1a"] = g["L2_gnn_w1a"].reshape(2, P, HID).transpose(1, 0, 2)
    arrays["b1a"] = g["L2_gnn_b1a"].reshape(2, P).T
    arrays["w1b"] = g["L2_gnn_w1b"].reshape(2, P, HID).transpose(1, 0, 2)
    arrays["b1b"] = g["L2_gnn_b1b"].reshape(2, P).T
    arrays["w1c"] = g["L2_gnn_w1c"].reshape(2, P, HID).transpose(1, 0, 2)
    arrays["b1c"] = g["L2_gnn_b1c"]
    arrays["w2a"] = g["L2_gnn_w2a"].reshape(3, P, HID).transpose(1, 0, 2)
    arrays["b2a"] = g["L2_gnn_b2a"]
    arrays["w2b"] = g["L2_gnn_w2b"].reshape(2, P, D).transpose(1, 0, 2)
    arrays["b2b"] = g["L2_gnn_b2b"]
    arrays["w3T"] = g["L3_gnn_weight"].T
    arrays = {f"in_{k}": np.ascontiguousarray(v) for k, v in arrays.items()}
    return arrays, None


def kernel(**inputs):
    import numpy as np
    import concourse.bacc as bacc
    from concourse.bass_utils import run_bass_kernel_spmd

    nc = bacc.Bacc("TRN2", target_bir_lowering=False, num_devices=1)
    arrays, _ = lay_out(inputs)
    args = [nc.dram_tensor(k, a.shape, mybir.dt.from_np(a.dtype), kind="ExternalInput").ap()
            for k, a in arrays.items()]
    out = nc.dram_tensor("out", [N, D], mybir.dt.float32, kind="ExternalOutput").ap()
    gnn(nc, *args, out)
    r = run_bass_kernel_spmd(nc, [arrays], core_ids=[0])
    return r.results[0]["out"]
```

```python
import concourse.bass as bass
from concourse import mybir
from contextlib import ExitStack

P = 128
N, E, D = 6250, 100000, 128
NT = -(-N // P)
NTP = NT + 1
NPAD = NTP * P
EC = -(-E // P)
EPAD = EC * P
H, C, K5, T4 = 4, 32, 5, 4
S = 4
B = 4
U = 2 * B
GC = -(-(int(E * 1.04) // S + NTP + 2 * U) // P)
GMAX = GC * P
ROWS = NPAD + P
REC = 20
R_SRC, R_EID, R_SUM, R_ANY, R_J, R_IDX, R_TYPE = 0, S, 2 * S, 3 * S, 4 * S, REC, REC + S
BIG = 2e30
LOW = -1e30
CL = 60
CLS = 10
HALF = 17
A0, A1 = D + H * K5, D + H
HID = 256


def gnn(nc, x, src, dst, windows, edge_attr, W0, W0T, attI, attJ, probs, importance, bias0,
        Ws, WsT, Wd, WdT, attS, attD, bias1, w1a, b1a, w1b, b1b, w1c, b1c, w2a, b2a, w2b, b2b,
        w3T, out):
    fp32, bf16, i32, u32 = mybir.dt.float32, mybir.dt.bfloat16, mybir.dt.int32, mybir.dt.uint32
    ALU, ACT, AX = mybir.AluOpType, mybir.ActivationFunctionType, mybir.AxisListType
    ds = bass.ds
    V, A, PE, G = nc.vector, nc.scalar, nc.tensor, nc.gpsimd

    def dram(name, shape, dt):
        return nc.dram_tensor(name, shape, dt).ap()

    perm_d = dram("nodes_by_degree", [NT * P, 4], i32)
    item_d = dram("item_table", [GMAX, 2], i32)
    rec_d = dram("item_records", [GMAX, P, REC], i32)
    rec0_d = dram("item_records_layer0", [GMAX, P, REC], i32)
    tab0_d = dram("table_layer0", [NPAD, T4 * A0], fp32)
    own0_d = dram("own_parts_layer0", [P, NTP, T4 * H * K5], fp32)
    tab1_d = [dram(f"table_layer1_{i}", [NPAD, A1], fp32) for i in range(3)]
    tab2_d = dram("table_layer2", [NPAD, HID], fp32)
    x3_d = dram("x_before_layer3", [NPAD, D], fp32)
    sum_d = [dram(f"sums_by_source_{s}", [ROWS, D], fp32) for s in range(S)]

    top = ExitStack()
    with top:
        def sb(name, shape, dt=fp32, ctx=top):
            return ctx.enter_context(nc.sbuf_tensor(name, shape, dt))

        def pb(name, shape, dt=fp32, ctx=top):
            return ctx.enter_context(nc.psum_tensor(name, shape, dt))

        live = []

        def sem(name):
            live.append(nc.alloc_semaphore(name=name))
            return live[-1]

        def fresh_semaphores():
            nc.clear_and_free_semaphores(live)
            nc.all_engine_barrier()
            live.clear()


        def bc(ap, axis, n):
            v = ap.unsqueeze(axis)
            shape = list(v.shape)
            shape[axis] = n
            return v.to_broadcast(shape)

        def flat(ap):
            return ap.rearrange("p a c -> p (a c)")

        xr = sb("xr", [P, NTP, D])
        ident = sb("ident", [P, P])
        identb = sb("identb", [P, P], bf16)
        nid = sb("nid", [P, NTP], i32)
        degI = sb("degI", [P, NTP])
        degO = sb("degO", [P, NTP])
        degOn = sb("degOn", [P, NT])
        node_info = sb("node_info", [P, NTP, 2])
        trips = sb("trips", [1, 1], i32)
        iotaS = sb("iotaS", [P, S])
        iotaT = sb("iotaT", [P, T4])
        place = sb("place", [P, 1])
        strict = sb("strict", [P, P])
        lower = sb("lower", [P, P])

        with ExitStack() as ph:
            e32 = [sb(f"e32_{w}", [P, EC], i32, ph) for w in "ds"]
            part = [[sb(f"part_{w}{q}", [P, EC], i32, ph) for q in "lh"] for w in "ds"]
            lo = [sb(f"lo_{w}", [P, EC], bf16, ph) for w in "ds"]
            hi = [sb(f"hi_{w}", [P, EC], bf16, ph) for w in "ds"]
            row128 = sb("row128", [P, P], bf16, ph)
            oneL = [sb(f"oneL{i}", [P, HALF, P], bf16, ph) for i in range(2)]
            oneH = [sb(f"oneH{i}", [P, HALF, NT], bf16, ph) for i in range(2)]
            ones = sb("ones", [P, P], fp32, ph)
            zeros = sb("zeros", [P, D * 2], fp32, ph)
            zerob = sb("zerob", [P, P], bf16, ph)
            nrev = sb("nrev", [P, NT], fp32, ph)
            nnum = sb("nnum", [P, NT], i32, ph)
            degIn = sb("degIn", [P, NT], fp32, ph)
            rsn = sb("rsn", [P, NT], fp32, ph)
            cls = sb("cls", [P, NT], bf16, ph)
            in_cls = sb("in_cls", [P, CL, NT], bf16, ph)
            behind = sb("behind", [P, CL, NT], fp32, ph)
            of_cls = sb("of_cls", [P, CL, NT], fp32, ph)
            up_to = sb("up_to", [P, CL, NT], fp32, ph)
            cones = sb("cones", [P, CL * NT], fp32, ph)
            onesb = sb("onesb", [P, P], bf16, ph)
            strictb = sb("strictb", [P, P], bf16, ph)
            rank = sb("rank", [P, NT], fp32, ph)
            ranki = sb("ranki", [P, NT], u32, ph)
            tot = sb("tot", [P, NT], fp32, ph)
            incl = sb("incl", [P, NT], fp32, ph)
            noderec = sb("noderec", [P, NT, 4], i32, ph)
            permrec = sb("permrec", [P, NTP, 4], i32, ph)
            dmax = sb("dmax", [P, NTP], fp32, ph)
            nci = sb("nci", [P, NTP], i32, ph)
            ncf = sb("ncf", [P, NTP], fp32, ph)
            ends = sb("ends", [P, NTP], fp32, ph)
            tripf = sb("tripf", [1, 1], i32, ph)
            gnum = sb("gnum", [P, GC], fp32, ph)
            jof = sb("jof", [P, 2, GC], fp32, ph)
            start = sb("start", [P, 2, GC], fp32, ph)
            hit = sb("hit", [P, GC], fp32, ph)
            items = sb("items", [P, GC, 2], i32, ph)
            hist = [pb(f"hist_{w}", [P, 512], fp32, ph) for w in "ds"]
            pre = pb("pre", [P, 512], fp32, ph)
            cnt = [[pb(f"cnt_{w}{v}", [P, 512], fp32, ph) for w in "bo"] for v in range(2)]
            edges_in = [sem("edges_in_d"), sem("edges_in_s")]
            consts = sem("consts")
            cst2 = sem("consts_first")
            zeroed = sem("zeroed")
            onehot = [sem("onehot0"), sem("onehot1")]
            counted = [sem("counted0"), sem("counted1")]
            hist_done = sem("hist_done")
            degs = sem("degrees_ready")
            prefix = sem("prefix_done")
            cls_ok = sem("classes_ready")
            cls_cnt = sem("classes_counted")
            cls_use = sem("counts_copied")
            ranks = sem("ranks_ready")
            perm_out = sem("perm_stored")
            perm_in = sem("perm_in")
            perm_ok = sem("perm_unpacked")
            dmax_ok = sem("dmax_ready")
            items_ok = sem("items_ready")
            items_out = sem("items_stored")
            STEPS = EC // (2 * HALF)

            block = ph.enter_context(nc.Block())

            @block.sync
            def _(sp):
                for w, e in enumerate((dst, src)):
                    sp.dma_start(e32[w][:, :], e).then_inc(edges_in[w], 16)
                sp.wait_ge(consts, 1)
                for s in range(S):
                    for r in range(NPAD // P):
                        sp.dma_start(sum_d[s][r * P:(r + 1) * P, :], zeros[:, 0:D]).then_inc(zeroed, 16)
                sp.wait_ge(perm_out, 16 * NT)
                sp.dma_start(permrec[:, 0:NT, :],
                             perm_d[0:NT * P, :].rearrange("(j p) w -> p j w", p=P)).then_inc(perm_in, 16)
                sp.wait_ge(items_ok, 1)
                sp.dma_start(item_d.rearrange("(p c) w -> p c w", p=P), items[:, :, :]).then_inc(items_out, 16)
                sp.wait_ge(items_out, 16)
                sp.wait_ge(zeroed, 16 * S * (NPAD // P))

            @block.gpsimd
            def _(pool):
                G.memset(zeros[:, :], 0.0).then_inc(consts, 1)
                G.memset(cones[:, :], 1.0).then_inc(cst2, 1)
                G.memset(zerob[:, :], 0.0).then_inc(cst2, 1)
                G.memset(ones[:, :], 1.0).then_inc(cst2, 1)
                G.memset(ident[:, :], 0.0).then_inc(cst2, 1)
                G.memset(strict[:, :], 0.0).then_inc(cst2, 1)
                G.memset(lower[:, :], 1.0).then_inc(cst2, 1)
                G.iota(row128[:, :], [[1, P]], base=0, channel_multiplier=0,
                       allow_small_or_imprecise_dtypes=True).then_inc(cst2, 1)
                pool.wait_ge(cst2, 7)
                G.affine_select(out=ident[:, :], in_=ident[:, :], compare_op=ALU.not_equal, fill=1.0,
                                base=0, pattern=[[-1, P]], channel_multiplier=1).then_inc(cst2, 1)
                G.affine_select(out=strict[:, :], in_=strict[:, :], compare_op=ALU.is_ge, fill=1.0,
                                base=0, pattern=[[-1, P]], channel_multiplier=1).then_inc(cst2, 1)
                G.affine_select(out=lower[:, :], in_=lower[:, :], compare_op=ALU.is_gt, fill=0.0,
                                base=0, pattern=[[-1, P]], channel_multiplier=1).then_inc(cst2, 1)
                G.iota(nnum[:, :], [[P, NT]], base=0, channel_multiplier=1).then_inc(cst2, 1)
                G.iota(nrev[:, :], [[-P, NT]], base=8191, channel_multiplier=-1,
                       allow_small_or_imprecise_dtypes=True).then_inc(cst2, 1)
                G.iota(iotaS[:, :], [[1, S]], base=0, channel_multiplier=0,
                       allow_small_or_imprecise_dtypes=True).then_inc(cst2, 1)
                G.iota(iotaT[:, :], [[1, T4]], base=1, channel_multiplier=0,
                       allow_small_or_imprecise_dtypes=True).then_inc(cst2, 1)
                G.iota(place[:, :], [[1, 1]], base=0, channel_multiplier=1,
                       allow_small_or_imprecise_dtypes=True).then_inc(cst2, 1)
                G.iota(gnum[:, :], [[1, GC]], base=0, channel_multiplier=GC,
                       allow_small_or_imprecise_dtypes=True).then_inc(cst2, 1)
                pool.wait_ge(ranks, 1)
                for j in range(NT):
                    G.indirect_dma_start(out=perm_d, out_offset=bass.IndirectOffsetOnAxis(ap=ranki[:, j:j + 1], axis=0),
                                         in_=noderec[:, j, :], in_offset=None).then_inc(perm_out, 16)
                pool.wait_ge(perm_ok, 1)
                G.partition_all_reduce(dmax[:, :], degI[:, :], P, bass.bass_isa.ReduceOp.max).then_inc(dmax_ok, 1)

            @block.vector
            def _(dve):
                for w in range(2):
                    dve.wait_ge(edges_in[w], 16)
                    V.tensor_scalar(part[w][0][:, :], e32[w][:, :], P - 1, None, ALU.bitwise_and)
                    V.tensor_scalar(part[w][1][:, :], e32[w][:, :], 7, None, ALU.arith_shift_right)
                dve.drain()
                for w in range(2):
                    V.tensor_copy(lo[w][:, :], part[w][0][:, :])
                    V.tensor_copy(hi[w][:, :], part[w][1][:, :])
                dve.drain()
                dve.wait_ge(cst2, 16)
                for w in range(2):
                    with dve.Fori(0, STEPS) as i:
                        for v in range(2):
                            dve.wait_ge(counted[v], i + w * STEPS + 1)
                            at = (i * 2 + v) * HALF
                            V.tensor_tensor(oneL[v][:, :, :], bc(lo[w][:, ds(at, HALF)], 2, P),
                                            bc(row128[:, :], 1, HALF), ALU.is_equal)
                            V.tensor_tensor(oneH[v][:, :, :], bc(hi[w][:, ds(at, HALF)], 2, NT),
                                            bc(row128[:, 0:NT], 1, HALF), ALU.is_equal).then_inc(onehot[v], 1)
                dve.wait_ge(hist_done, 1)
                V.tensor_copy(degIn[:, :], hist[0][:, 0:NT])
                V.tensor_copy(degOn[:, :], hist[1][:, 0:NT])
                V.tensor_copy(identb[:, :], ident[:, :])
                V.tensor_copy(strictb[:, :], strict[:, :])
                V.tensor_copy(onesb[:, :], ones[:, :])
                dve.drain()
                V.tensor_scalar(rsn[:, :], degIn[:, :], float(CL - 1), -1.0, ALU.min, ALU.mult).then_inc(degs, 1)
                dve.drain()
                V.tensor_scalar(cls[:, :], rsn[:, :], float(CL - 1), None, ALU.add)
                dve.drain()
                V.tensor_tensor(in_cls[:, :, :], bc(cls[:, :], 1, CL), bc(row128[:, 0:CL], 2, NT),
                                ALU.is_equal).then_inc(cls_ok, 1)
                dve.wait_ge(prefix, 1)
                V.tensor_copy(tot[:, :], pre[:, NT:2 * NT])
                dve.drain()
                V.tensor_tensor_scan(incl[:, :], ones[:, 0:NT], tot[:, :], 0.0, ALU.mult, ALU.add)
                dve.drain()
                V.tensor_tensor(incl[:, :], incl[:, :], tot[:, :], ALU.subtract)
                dve.drain()
                V.tensor_tensor(rsn[:, :], incl[:, :], pre[:, 0:NT], ALU.add)
                dve.drain()
                V.tensor_copy(noderec[:, :, 0], nnum[:, :])
                V.tensor_copy(noderec[:, :, 1], rsn[:, :])
                V.tensor_copy(noderec[:, :, 2], degIn[:, :])
                V.tensor_copy(noderec[:, :, 3], degOn[:, :])
                V.tensor_scalar(incl[:, :], nrev[:, :], float(8191 - N) + 0.5, None, ALU.is_lt)
                dve.drain()
                V.tensor_tensor(degOn[:, :], degOn[:, :], incl[:, :], ALU.max)
                for q in range(CL // CLS):
                    dve.wait_ge(cls_cnt, q + 1)
                    for w, t in enumerate((behind, of_cls)):
                        last = V.tensor_copy(flat(t[:, q * CLS:(q + 1) * CLS, :]), cnt[q % 2][w][:, 0:CLS * NT])
                    last.then_inc(cls_use, 1)
                dve.drain()
                V.tensor_tensor_scan(flat(up_to[:, :, :]), cones[:, :], flat(of_cls[:, :, :]), 0.0, ALU.mult, ALU.add)
                V.tensor_tensor(behind[:, :, :], behind[:, :, :], of_cls[:, :, :], ALU.subtract)
                dve.drain()
                V.tensor_tensor(behind[:, :, :], behind[:, :, :], up_to[:, :, :], ALU.add)
                dve.drain()
                V.tensor_tensor(behind[:, :, :], behind[:, :, :], in_cls[:, :, :], ALU.mult)
                dve.drain()
                V.tensor_reduce(rank[:, :], behind[:, :, :].rearrange("p c j -> p j c"), AX.X, ALU.add)
                dve.drain()
                V.tensor_copy(ranki[:, :], rank[:, :]).then_inc(ranks, 1)
                dve.wait_ge(perm_in, 16)
                V.tensor_copy(nid[:, 0:NT], permrec[:, 0:NT, 0])
                V.tensor_scalar(nid[:, NT:NTP], place[:, :], float(NT * P), None, ALU.add)
                V.memset(node_info[:, NT:NTP, :], 0.0)
                V.memset(degI[:, NT:NTP], 0.0)
                V.memset(degO[:, NT:NTP], 0.0)
                V.tensor_copy(node_info[:, 0:NT, :], permrec[:, 0:NT, 1:3])
                V.tensor_copy(degO[:, 0:NT], permrec[:, 0:NT, 3])
                V.tensor_copy(degI[:, 0:NT], permrec[:, 0:NT, 2]).then_inc(perm_ok, 1)
                dve.wait_ge(dmax_ok, 1)
                V.tensor_scalar(nci[:, :], dmax[:, :], 1.0, float(S - 1), ALU.max, ALU.add)
                dve.drain()
                V.tensor_scalar(nci[:, :], nci[:, :], S.bit_length() - 1, None, ALU.arith_shift_right)
                dve.drain()
                V.tensor_copy(ncf[:, :], nci[:, :])
                dve.drain()
                V.tensor_tensor_scan(ends[:, :], ones[:, 0:NTP], ncf[:, :], 0.0, ALU.mult, ALU.add)
                dve.drain()
                V.tensor_scalar(tripf[:, :], ends[0:1, NT - 1:NT], float(U - 1), None, ALU.add)
                dve.drain()
                V.tensor_scalar(trips[:, :], tripf[:, :], U.bit_length() - 1, None, ALU.arith_shift_right)
                V.memset(jof[:, :, :], 0.0)
                V.memset(start[:, :, :], 0.0)
                dve.drain()
                for j in range(NT):
                    a, b = j % 2, (j + 1) % 2
                    V.scalar_tensor_tensor(jof[:, b, :], gnum[:, :], ends[:, j:j + 1], jof[:, a, :], ALU.is_ge, ALU.add)
                    V.tensor_scalar(hit[:, :], gnum[:, :], ends[:, j:j + 1], ends[:, j:j + 1], ALU.is_ge, ALU.mult)
                    dve.drain()
                    V.tensor_tensor(start[:, b, :], hit[:, :], start[:, a, :], ALU.max)
                    dve.drain()
                b = NT % 2
                V.tensor_tensor(hit[:, :], gnum[:, :], start[:, b, :], ALU.subtract)
                V.tensor_copy(items[:, :, 0], jof[:, b, :])
                dve.drain()
                V.tensor_scalar(items[:, :, 1], hit[:, :], float(S), None, ALU.mult).then_inc(items_ok, 1)

            @block.tensor
            def _(pe):
                for c in counted:
                    pe.sem_inc(c, 1)
                pe.wait_ge(cst2, 16)
                for w in range(2):
                    PE.matmul(hist[w][:, 0:NT], zerob[:, :], zerob[:, 0:NT], start=True, stop=False)
                    with pe.Fori(0, STEPS) as i:
                        for v in range(2):
                            pe.wait_ge(onehot[v], i + 1 + w * STEPS)
                            for t in range(HALF):
                                last = PE.matmul(hist[w][:, 0:NT], oneL[v][:, t, :], oneH[v][:, t, :],
                                                 start=False, stop=False)
                            last.then_inc(counted[v], 1)
                    last = PE.matmul(hist[w][:, 0:NT], zerob[:, :], zerob[:, 0:NT], start=False, stop=True)
                last.then_inc(hist_done, 1)
                pe.wait_ge(degs, 1)
                PE.matmul(pre[:, 0:NT], strict[:, :], degIn[:, :], start=True, stop=True)
                PE.matmul(pre[:, NT:2 * NT], ones[:, :], degIn[:, :], start=True, stop=True).then_inc(prefix, 1)
                pe.wait_ge(cls_ok, 1)
                for q in range(CL // CLS):
                    if q > 1:
                        pe.wait_ge(cls_use, q - 1)
                    c = flat(in_cls[:, q * CLS:(q + 1) * CLS, :])
                    PE.matmul(cnt[q % 2][0][:, 0:CLS * NT], strictb[:, :], c, start=True, stop=True)
                    PE.matmul(cnt[q % 2][1][:, 0:CLS * NT], onesb[:, :], c, start=True, stop=True).then_inc(cls_cnt, 1)

        def turns(eng):
            return eng.value_load(trips[0:1, 0:1], min_val=1, max_val=GMAX // U - 3)

        with ExitStack() as ph:
            jk = [sb(f"jk{b}", [P, B, 2], i32, ph) for b in range(2)]
            info = [sb(f"info{b}", [P, B, 2], fp32, ph) for b in range(2)]
            kb = [sb(f"kb{b}", [P, B], fp32, ph) for b in range(2)]
            rs = [sb(f"rs{b}", [P, B], fp32, ph) for b in range(2)]
            kk = [sb(f"kk{b}", [P, B, S], fp32, ph) for b in range(2)]
            ee = [sb(f"ee{b}", [P, B, S], fp32, ph) for b in range(2)]
            ok = [sb(f"ok{b}", [P, B, S], fp32, ph) for b in range(2)]
            t1 = [sb(f"t1{b}", [P, B, S], fp32, ph) for b in range(2)]
            t2 = [sb(f"t2{b}", [P, B, S], fp32, ph) for b in range(2)]
            trash = sb("trash", [P, B, S], fp32, ph)
            eq = [sb(f"eq{b}", [P, B * S, T4], fp32, ph) for b in range(2)]
            win = [sb(f"win{b}", [P, B], u32, ph) for b in range(2)]
            we = [sb(f"we{b}", [P, B, 2 * S], i32, ph) for b in range(2)]
            wf = [sb(f"wf{b}", [P, B, 2 * S], fp32, ph) for b in range(2)]
            rec = [sb(f"rec{b}", [P, B, 2 * REC], i32, ph) for b in range(2)]
            recf = [r[:, :, :].bitcast(fp32) for r in rec]
            jj = [sb(f"jj{b}", [P, B], i32, ph) for b in range(2)]
            lift = [sb(f"lift{b}", [P, B], fp32, ph) for b in range(2)]
            jk_in = [sem(f"jk_in{b}") for b in range(2)]
            info_in = [sem(f"info_in{b}") for b in range(2)]
            jk_used = [sem(f"jk_used{b}") for b in range(2)]
            win_ok = [sem(f"window_index_ready{b}") for b in range(2)]
            gate = sem("pool_gate_records")
            gate2 = sem("act_gate_records")
            gate3 = sem("sync_gate_records")
            win_in = [sem(f"windows_in{b}") for b in range(2)]
            rec_ok = [sem(f"record_ready{b}") for b in range(2)]
            rec_out = [sem(f"record_stored{b}") for b in range(2)]
            rec_blank = sem("record_blank")

            block = ph.enter_context(nc.Block())

            @block.sync
            def _(sp):
                n = turns(sp) + 2
                with sp.Fori(0, n) as i:
                    for b in range(2):
                        sp.wait_ge(jk_used[b], i + 1)
                        sp.dma_start(jk[b][:, :, :], item_d[ds(i * U + b * B, B), :].partition_broadcast(P)
                                     ).then_inc(jk_in[b], 16)
                    for b in range(2):
                        sp.wait_ge(jk_in[b], (i + 1) * 16)
                        sp.sem_inc(gate3, 1)
                        for u in range(B):
                            j = sp.value_load(jk[b][0:1, u, 0:1], min_val=0, max_val=NT)
                            sp.dma_start(info[b][:, u, :], node_info[:, ds(j, 1), :].rearrange("p a w -> p (a w)")
                                         ).then_inc(info_in[b], 16)

            @block.gpsimd
            def _(pool):
                n = turns(pool) + 1
                with pool.Fori(0, n) as i:
                    for b in range(2):
                        pool.wait_ge(win_ok[b], i + 1)
                        pool.sem_inc(gate, 1)
                        for u in range(B):
                            G.indirect_dma_start(out=we[b][:, u, :], out_offset=None, in_=windows,
                                                 in_offset=bass.IndirectOffsetOnAxis(ap=win[b][:, u:u + 1], axis=0)
                                                 ).then_inc(win_in[b], 16)

            @block.scalar
            def _(act):
                n = turns(act) + 1
                act.wait_ge(rec_blank, 2)
                for b in range(2):
                    for half, to in enumerate((rec_d, rec0_d)):
                        act.dma_start(to[GMAX - (b + 1) * B:GMAX - b * B, :, :].rearrange("u p w -> p u w"),
                                      rec[b][:, :, half * REC:(half + 1) * REC]).then_inc(rec_out[b], 16)
                with act.Fori(0, n) as i:
                    for b in range(2):
                        act.wait_ge(rec_ok[b], i + 1)
                        for half, to in enumerate((rec_d, rec0_d)):
                            act.dma_start(to[ds(i * U + b * B, B), :, :].rearrange("u p w -> p u w"),
                                          rec[b][:, :, half * REC:(half + 1) * REC]).then_inc(rec_out[b], 16)
                for b in range(2):
                    act.wait_ge(rec_out[b], n * 32 + 32)
                    act.sem_inc(gate2, 1)

            @block.vector
            def _(dve):
                n = turns(dve) + 1
                V.tensor_scalar(trash[:, :, :].rearrange("p u s -> p (u s)"), place[:, :].to_broadcast([P, B * S]),
                                float(NPAD), None, ALU.add)
                for b in range(2):
                    V.memset(rec[b][:, :, :], 0).then_inc(rec_blank, 1)
                dve.drain()
                for c in jk_used:
                    dve.sem_inc(c, 1)
                def windows_index(i, b):
                    dve.wait_ge(info_in[b], (i + 1) * 16 * B)
                    V.tensor_copy(kb[b][:, :], jk[b][:, :, 1])
                    V.tensor_copy(jj[b][:, :], jk[b][:, :, 0])
                    dve.drain()
                    V.tensor_tensor(rs[b][:, :], info[b][:, :, 0], kb[b][:, :], ALU.add)
                    V.tensor_tensor(kk[b][:, :, :], bc(kb[b][:, :], 2, S), bc(iotaS[:, :], 1, B), ALU.add)
                    V.tensor_scalar(lift[b][:, :], kb[b][:, :], 0.0, -BIG, ALU.is_equal, ALU.mult)
                    dve.drain()
                    V.tensor_scalar(win[b][:, :], rs[b][:, :], float(E), None, ALU.min).then_inc(win_ok[b], 1)
                    V.tensor_tensor(ok[b][:, :, :], kk[b][:, :, :], bc(info[b][:, :, 1], 2, S), ALU.is_lt)
                    V.drain().then_inc(jk_used[b], 1)

                def record(i, b):
                    V.tensor_tensor(ee[b][:, :, :], bc(rs[b][:, :], 2, S), bc(iotaS[:, :], 1, B), ALU.add)
                    dve.wait_ge(rec_out[b], i * 32 + 32)
                    V.tensor_copy(rec[b][:, :, R_J], jj[b][:, :])
                    V.tensor_copy(recf[b][:, :, R_J + 1], lift[b][:, :])
                    V.tensor_scalar(recf[b][:, :, R_ANY:R_ANY + S], ok[b][:, :, :], 1.0, BIG, ALU.subtract, ALU.mult)
                    dve.drain()
                    V.tensor_tensor(rec[b][:, :, R_EID:R_EID + S], ee[b][:, :, :], ok[b][:, :, :], ALU.mult)
                    dve.wait_ge(win_in[b], (i + 1) * 16 * B)
                    V.tensor_copy(wf[b][:, :, :], we[b][:, :, :])
                    dve.drain()
                    V.tensor_tensor(t1[b][:, :, :], wf[b][:, :, 0:S], ok[b][:, :, :], ALU.mult)
                    V.scalar_tensor_tensor(t2[b][:, :, :], wf[b][:, :, S:2 * S], 1.0, ok[b][:, :, :], ALU.add, ALU.mult)
                    V.tensor_tensor(ee[b][:, :, :], wf[b][:, :, 0:S], trash[:, :, :], ALU.subtract)
                    dve.drain()
                    V.tensor_tensor(ee[b][:, :, :], ee[b][:, :, :], ok[b][:, :, :], ALU.mult)
                    V.tensor_copy(rec[b][:, :, R_SRC:R_SRC + S], t1[b][:, :, :])
                    V.scalar_tensor_tensor(kk[b][:, :, :], t1[b][:, :, :], float(T4), t2[b][:, :, :], ALU.mult, ALU.add)
                    V.tensor_tensor(eq[b][:, :, :], bc(t2[b][:, :, :].rearrange("p u s -> p (u s)"), 2, T4),
                                    bc(iotaT[:, :], 1, B * S), ALU.is_equal)
                    dve.drain()
                    V.tensor_tensor(rec[b][:, :, R_IDX:R_IDX + S], kk[b][:, :, :], ok[b][:, :, :], ALU.subtract)
                    V.tensor_tensor(recf[b][:, :, R_SUM:R_SUM + S], ee[b][:, :, :], trash[:, :, :], ALU.add)
                    V.tensor_scalar(recf[b][:, :, R_TYPE:R_TYPE + S * T4],
                                    eq[b][:, :, :].rearrange("p (u s) t -> p u (s t)", u=B),
                                    1.0, BIG, ALU.subtract, ALU.mult).then_inc(rec_ok[b], 1)

                for b in range(2):
                    windows_index(0, b)
                with dve.Fori(0, n) as i:
                    for b in range(2):
                        record(i, b)
                        windows_index(i + 1, b)

        fresh_semaphores()

        h = sb("h", [P, NTP, D])
        rhs0 = sb("rhs0", [P, T4, A0])
        rhs0i = sb("rhs0i", [P, T4, H * K5])
        rhs1 = sb("rhs1", [P, 3, D + 2 * H])
        soft = sb("soft", [P, K5])
        impt = sb("impt", [P, T4])
        bias = sb("bias", [P, 4, D])
        with ExitStack() as ph:
            wT = sb("wT", [P, T4, D], fp32, ph)
            wsT = sb("wsT", [P, 3, D], fp32, ph)
            wdT = sb("wdT", [P, 3, D], fp32, ph)
            aI = sb("aI", [P, H * K5], fp32, ph)
            aJ = sb("aJ", [P, H * K5], fp32, ph)
            aS = sb("aS", [P, 3, H], fp32, ph)
            aD = sb("aD", [P, 3, H], fp32, ph)
            pk = sb("pk", [P, K5], fp32, ph)
            sm = sb("sm", [P, 2], fp32, ph)
            wps = pb("wps", [P, 512], fp32, ph)
            w_in = sem("weights_in")
            probs_in = sem("probs_in")
            x_in = sem("x_in")
            wp = sem("score_weights_done")
            mx = sem("probs_max_ready")
            ex = sem("probs_exp_ready")

            block = ph.enter_context(nc.Block())

            @block.sync
            def _(sp):
                sp.dma_start(pk[:, :], probs.partition_broadcast(P)).then_inc(probs_in, 16)
                for to, frm in ((wT[:, :, :], W0T), (wsT[:, :, :], WsT), (wdT[:, :, :], WdT),
                                (aI[:, :], attI), (aJ[:, :], attJ), (aS[:, :, :], attS), (aD[:, :, :], attD),
                                (rhs0[:, :, 0:D], W0), (rhs1[:, :, 0:D], Ws),
                                (impt[:, :], importance.partition_broadcast(P)),
                                (bias[:, 0, :], bias0.partition_broadcast(P)),
                                (bias[:, 1:4, :], bias1.partition_broadcast(P))):
                    sp.dma_start(to, frm).then_inc(w_in, 16)
                sp.wait_ge(w_in, 16 * 12)

            @block.gpsimd
            def _(pool):
                for j in range(NTP):
                    G.indirect_dma_start(out=xr[:, j, :], out_offset=None, in_=x,
                                         in_offset=bass.IndirectOffsetOnAxis(ap=nid[:, j:j + 1].bitcast(u32), axis=0)
                                         ).then_inc(x_in, 16)
                pool.wait_ge(x_in, 16 * NTP)

            @block.tensor
            def _(pe):
                pe.wait_ge(w_in, 16 * 12)
                for t in range(T4):
                    PE.matmul(wps[:, t * 40:t * 40 + 20], wT[:, t, :], aJ[:, :], start=True, stop=True)
                    PE.matmul(wps[:, t * 40 + 20:t * 40 + 40], wT[:, t, :], aI[:, :], start=True, stop=True)
                for l in range(3):
                    PE.matmul(wps[:, 160 + 8 * l:164 + 8 * l], wsT[:, l, :], aS[:, l, :], start=True, stop=True)
                    last = PE.matmul(wps[:, 164 + 8 * l:168 + 8 * l], wdT[:, l, :], aD[:, l, :], start=True, stop=True)
                last.then_inc(wp, 1)

            @block.scalar
            def _(act):
                act.wait_ge(mx, 1)
                A.activation(soft[:, :], pk[:, :], ACT.Exp).then_inc(ex, 1)

            @block.vector
            def _(dve):
                dve.wait_ge(probs_in, 16)
                V.tensor_reduce(sm[:, 0:1], pk[:, :], AX.X, ALU.max)
                dve.drain()
                V.tensor_scalar(pk[:, :], pk[:, :], sm[:, 0:1], None, ALU.subtract).then_inc(mx, 1)
                dve.wait_ge(ex, 1)
                V.tensor_reduce(sm[:, 0:1], soft[:, :], AX.X, ALU.add)
                dve.drain()
                V.reciprocal(sm[:, 1:2], sm[:, 0:1])
                dve.drain()
                V.tensor_scalar(soft[:, :], soft[:, :], sm[:, 1:2], None, ALU.mult)
                dve.wait_ge(wp, 1)
                v = wps[:, 0:160].rearrange("p (t w) -> p t w", t=T4)
                V.tensor_copy(rhs0[:, :, D:A0], v[:, :, 0:20])
                V.tensor_copy(rhs0i[:, :, :], v[:, :, 20:40])
                V.tensor_copy(rhs1[:, :, D:D + 2 * H], wps[:, 160:184].rearrange("p (l w) -> p l w", l=3))

        def node_table(tag, frm, rhs, pieces, stage, table):
            with ExitStack() as ph:
                ht = [sb(f"ht_{tag}{v}", [P, P], fp32, ph) for v in range(2)]
                hc = [sb(f"hc_{tag}{v}", [P, P], fp32, ph) for v in range(2)]
                tps = [pb(f"tps_{tag}{v}", [P, 512], fp32, ph) for v in range(2)]
                banks = max(p[0] for p in pieces) + 1
                mps = [[pb(f"mps_{tag}{v}{b}", [P, 512], fp32, ph) for b in range(banks)] for v in range(2)]
                fetched = sem(f"tile_copied_{tag}")
                turned = sem(f"tile_transposed_{tag}")
                stored = sem(f"transpose_stored_{tag}")
                mult = sem(f"tile_multiplied_{tag}")
                staged = sem(f"tile_staged_{tag}")
                rows_out = sem(f"rows_out_{tag}")
                block = ph.enter_context(nc.Block())

                @block.scalar
                def _(act):
                    for c in (stored,):
                        act.sem_inc(c, 1)
                    with act.Fori(0, NTP // 2) as i:
                        for v in range(2):
                            act.wait_ge(turned, (i * 2 + v - 1 if v else i * 2) + 1)
                            A.activation(hc[v][:, :], frm[:, ds(i * 2 + v, 1), :].rearrange("p a c -> p (a c)"),
                                         ACT.Copy).then_inc(fetched, 1)
                        for v in range(2):
                            act.wait_ge(turned, i * 2 + v + 2)
                            act.wait_ge(mult, i * 2 + 1)
                            A.activation(ht[v][:, :], tps[v][:, 0:P], ACT.Copy).then_inc(stored, 1)

                @block.tensor
                def _(pe):
                    for c in (turned, mult):
                        pe.sem_inc(c, 1)
                    with pe.Fori(0, NTP // 2) as i:
                        for v in range(2):
                            pe.wait_ge(fetched, i * 2 + v + 1)
                            pe.wait_ge(stored, i * 2 + 1)
                            PE.transpose(tps[v][:, 0:P], hc[v][:, :], ident[:, :]).then_inc(turned, 1)
                        for v in range(2):
                            pe.wait_ge(stored, i * 2 + v + 2)
                            pe.wait_ge(staged, i * 2 + 1)
                            for b, a, z, op, _ in pieces:
                                last = PE.matmul(mps[v][b][:, a:z], ht[v][:, :], op, start=True, stop=True)
                            last.then_inc(mult, 1)

                @block.vector
                def _(dve):
                    for c in (staged,):
                        dve.sem_inc(c, 1)
                    with dve.Fori(0, NTP // 2) as i:
                        for v in range(2):
                            dve.wait_ge(mult, i * 2 + v + 2)
                            for b, a, z, _, to in pieces:
                                for lo_, hi_, dest in to:
                                    last = V.tensor_copy(dest(i * 2 + v), mps[v][b][:, lo_:hi_])
                            last.then_inc(staged, 1)

                @block.gpsimd
                def _(pool):
                    for j in range(NTP):
                        pool.wait_ge(staged, j + 2)
                        G.indirect_dma_start(out=table, out_offset=bass.IndirectOffsetOnAxis(
                            ap=nid[:, j:j + 1].bitcast(u32), axis=0), in_=stage[:, j, :], in_offset=None
                        ).then_inc(rows_out, 16)
                    pool.wait_ge(rows_out, 16 * NTP)

        def attention(tag, T, table, own, acc, g, prod, term, zt):
            L = T * H
            ZW = H * K5 if T > 1 else H
            OW = T * ZW
            with ExitStack() as ph:
                rec = [sb(f"rec_{tag}{b}", [P, B, REC], i32, ph) for b in range(2)]
                if T > 1:
                    idx = [sb(f"idx_{tag}{b}", [P, B, S], i32, ph) for b in range(2)]
                    mask = [sb(f"mask_{tag}{b}", [P, B * S, T], fp32, ph) for b in range(2)]
                    al = sb(f"al_{tag}", [P, B * S, H], fp32, ph)
                ob = [sb(f"own_{tag}{b}", [P, B, OW], fp32, ph) for b in range(2)]
                tile = [sb(f"tile_{tag}{b}", [1, B], i32, ph) for b in range(2)]
                z = sb(f"z_{tag}", [P, B, S, ZW], fp32, ph)
                sc = [sb(f"sc_{tag}{b}", [P, B, S, L], fp32, ph) for b in range(2)]
                lift = sb(f"lift_{tag}", [P, L, B + 1], fp32, ph)
                item_max = sb(f"item_max_{tag}", [P, L, B + 1], fp32, ph)
                run_max = sb(f"run_max_{tag}", [P, L, B + 1], fp32, ph)
                shrink = [sb(f"shrink_{tag}{b}", [P, 2, L, B], fp32, ph) for b in range(2)]
                si = sb(f"si_{tag}", [P, B, L], fp32, ph)
                A_ = [sb(f"run_sum_{tag}{u}", [P, L, C + 1], fp32, ph) for u in range(2)]
                sums = [[pb(f"sums_{tag}{b}{u}", [P, 512], fp32, ph) for u in range(B)] for b in range(2)]
                rec_in = [sem(f"rec_in_{tag}{b}") for b in range(2)]
                own_in = [sem(f"own_in_{tag}{b}") for b in range(2)]
                rec_read = [sem(f"rec_read_by_vector_{tag}{b}") for b in range(2)]
                gathered = [sem(f"gathered_{tag}{b}") for b in range(2)]
                gate_p, gate_s, gate_a = sem(f"gate_pool_{tag}"), sem(f"gate_sync_{tag}"), sem(f"gate_act_{tag}")
                scored = sem(f"scores_ready_{tag}")
                weighed = sem(f"weights_ready_{tag}")
                shr_arg = sem(f"shrink_arguments_{tag}")
                shr_ok = sem(f"shrink_ready_{tag}")
                prods = sem(f"products_ready_{tag}")
                summed = sem(f"products_summed_{tag}")
                merged = sem(f"sums_merged_{tag}")
                kept = sem(f"sums_kept_{tag}")
                NREC = 3 if T > 1 else 1
                ahead = T > 1
                block = ph.enter_context(nc.Block())

                @block.sync
                def _(sp):
                    def fetch(i, b):
                        g0 = i * U + b * B
                        sp.wait_ge(rec_read[b], i + 1)
                        sp.dma_start(rec[b][:, :, :], rec_d[ds(g0, B), :, :].rearrange("u p w -> p u w")
                                     ).then_inc(rec_in[b], 16)
                        if T > 1:
                            sp.dma_start(idx[b][:, :, :], rec0_d[ds(g0, B), :, 0:S].rearrange("u p w -> p u w")
                                         ).then_inc(rec_in[b], 16)
                            sp.dma_start(mask[b][:, :, :].rearrange("p (u s) t -> p u (s t)", u=B),
                                         rec0_d[ds(g0, B), :, S:S + S * T].rearrange("u p w -> p u w").bitcast(fp32)
                                         ).then_inc(rec_in[b], 16)
                        sp.wait_ge(rec_in[b], (i + 1) * 16 * NREC)
                        sp.sem_inc(gate_s, 1)
                        for u in range(B):
                            j = sp.value_load(rec[b][0:1, u, R_J:R_J + 1], min_val=0, max_val=NT)
                            sp.dma_start(ob[b][:, u, :], own[:, ds(j, 1), :].rearrange("p a w -> p (a w)")
                                         ).then_inc(own_in[b], 16)

                    n = turns(sp)
                    with sp.Fori(0, n) as i:
                        for b in range(2):
                            fetch(i, b)
                    if ahead:
                        fetch(n, 0)

                @block.gpsimd
                def _(pool):
                    def gather(i, b):
                        pool.wait_ge(rec_in[b], (i + 1) * 16 * NREC)
                        for u in range(B):
                            pool.wait_ge(prods, (i * 2 + b) * B + u + 1)
                            pool.sem_inc(gate_p, 1)
                            for s in range(S):
                                at = (idx[b][:, u, s:s + 1] if T > 1 else
                                      rec[b][:, u, R_SRC + s:R_SRC + s + 1]).bitcast(u32)
                                G.indirect_dma_start(out=g[b][:, u, s, :], out_offset=None, in_=table,
                                                     in_offset=bass.IndirectOffsetOnAxis(ap=at, axis=0)
                                                     ).then_inc(gathered[b], 16)

                    n = turns(pool)
                    with pool.Fori(0, n) as i:
                        for b in range(2):
                            gather(i, b)
                    if ahead:
                        gather(n, 0)

                @block.scalar
                def _(act):
                    def exps(k, b):
                        act.wait_ge(scored, k + 1)
                        A.activation(sc[b][:, :, :, :], sc[b][:, :, :, :], ACT.Exp).then_inc(weighed, 1)
                        act.wait_ge(shr_arg, k + 1)
                        A.activation(shrink[b][:, :, :, :], shrink[b][:, :, :, :], ACT.Exp).then_inc(shr_ok, 1)

                    act.sem_inc(kept, 2)
                    n = turns(act)
                    if ahead:
                        exps(0, 0)
                    with act.Fori(0, n) as i:
                        for b in range(2):
                            k = i * 2 + b
                            if ahead:
                                exps(k + 1, 1 - b)
                            else:
                                exps(k, b)
                            js = [act.value_load(tile[b][0:1, u:u + 1], min_val=0, max_val=NT) for u in range(B)]
                            for u in range(B):
                                act.wait_ge(merged, k * B + u + 1)
                                act.wait_ge(kept, k * B + u + 2)
                                A.activation(flat(acc[:, ds(js[u], 1), :]), A_[u % 2][:, :, :].rearrange("p l c -> p (l c)"),
                                             ACT.Copy).then_inc(kept, 1)

                @block.tensor
                def _(pe):
                    pe.sem_inc(summed, 2)
                    n = turns(pe)
                    with pe.Fori(0, n) as i:
                        for b in range(2):
                            for u in range(B):
                                pe.wait_ge(prods, (i * 2 + b) * B + u + 1 + 2 * B)
                                for s in range(S):
                                    last = PE.matmul(sums[b][u][:, 0:T * D], ident[:, :], prod[u % 2][:, s, :],
                                                     start=(s == 0), stop=(s == S - 1))
                                last.then_inc(summed, 1)

                @block.vector
                def _(dve):
                    def scores(i, b):
                        dve.wait_ge(own_in[b], (i + 1) * 16 * B)
                        V.tensor_copy(item_max[:, :, 0:1], run_max[:, :, B:B + 1])
                        V.tensor_copy(lift[:, :, 1:B + 1],
                                      bc(rec[b][:, :, R_J + 1].bitcast(fp32), 1, L))
                        if T > 1:
                            for u in range(B):
                                V.tensor_tensor(zt[:, u, :, :].rearrange("p s (t w) -> p s t w", t=T),
                                                bc(ob[b][:, u, :].rearrange("p (t w) -> p t w", t=T), 1, S),
                                                bc(mask[b][:, u * S:(u + 1) * S, :], 3, ZW), ALU.add)
                            dve.drain()
                            V.tensor_reduce(z[:, :, :, :].rearrange("p u s w -> p (u s) w"),
                                            zt[:, :, :, :].rearrange("p u s (t w) -> p (u s) w t", t=T), AX.X, ALU.max)
                            dve.drain()
                        dve.wait_ge(gathered[b], (i + 1) * 16 * S * B)
                        if T > 1:
                            V.tensor_tensor(z[:, :, :, :], z[:, :, :, :], g[b][:, :, :, D:D + ZW], ALU.add)
                        else:
                            V.tensor_tensor(z[:, :, :, :], bc(ob[b][:, :, :], 2, S), g[b][:, :, :, D:D + ZW], ALU.add)
                        dve.drain()
                        zf = z[:, :, :, :].rearrange("p u s w -> p (u s w)")
                        V.scalar_tensor_tensor(zf, zf, 0.2, zf, ALU.mult, ALU.max)
                        dve.drain()
                        if T > 1:
                            zz = zf.rearrange("p (a k) -> p a k", k=K5)
                            V.tensor_tensor(zz, zz, bc(soft[:, :], 1, B * S * H), ALU.mult)
                            dve.drain()
                            V.tensor_reduce(al[:, :, :].rearrange("p a h -> p (a h)"), zz, AX.X, ALU.add)
                            dve.drain()
                            V.tensor_tensor(sc[b][:, :, :, :].rearrange("p u s (t h) -> p (u s) t h", t=T),
                                            bc(al[:, :, :], 2, T), bc(mask[b][:, :, :], 3, H), ALU.add)
                        else:
                            V.tensor_tensor(sc[b][:, :, :, :], z[:, :, :, :],
                                            bc(rec[b][:, :, R_ANY:R_ANY + S].bitcast(fp32), 3, H), ALU.add)
                        dve.drain()
                        im = item_max[:, :, 1:B + 1].rearrange("p l u -> p u l")
                        V.tensor_reduce(im, sc[b][:, :, :, :].rearrange("p u s l -> p u l s"), AX.X, ALU.max)
                        V.tensor_copy(tile[b][:, :], rec[b][0:1, :, R_J])
                        V.drain().then_inc(rec_read[b], 1)
                        V.tensor_scalar(im, im, LOW, None, ALU.max)
                        dve.drain()
                        V.tensor_tensor(sc[b][:, :, :, :], sc[b][:, :, :, :], bc(im, 2, S),
                                        ALU.subtract).then_inc(scored, 1)

                    def maxima(k, b):
                        shrunk, taken = shrink[b][:, 0, :, :], shrink[b][:, 1, :, :]
                        V.tensor_tensor_scan(run_max[:, :, :].rearrange("p l u -> p (l u)"),
                                             lift[:, :, :].rearrange("p l u -> p (l u)"),
                                             item_max[:, :, :].rearrange("p l u -> p (l u)"), 0.0, ALU.add, ALU.max)
                        dve.drain()
                        V.tensor_tensor(taken, item_max[:, :, 1:B + 1], run_max[:, :, 1:B + 1], ALU.subtract)
                        V.tensor_tensor(shrunk, run_max[:, :, 0:B], lift[:, :, 1:B + 1], ALU.add)
                        dve.drain()
                        V.tensor_tensor(shrunk, shrunk, run_max[:, :, 1:B + 1], ALU.subtract).then_inc(shr_arg, 1)

                    def weigh(k, b, u):
                        dve.wait_ge(summed, k * B + u + 1)
                        w = sc[b][:, u, :, :]
                        if T > 1:
                            for s in range(S):
                                last = V.tensor_tensor(
                                    prod[u % 2][:, s, :].rearrange("p (t h c) -> p t h c", t=T, h=H),
                                    bc(w[:, s, :].rearrange("p (t h) -> p t h", t=T), 3, C),
                                    bc(g[b][:, u, s, 0:D].rearrange("p (h c) -> p h c", h=H), 1, T), ALU.mult)
                        else:
                            last = V.tensor_tensor(prod[u % 2][:, :, :].rearrange("p s (h c) -> p s h c", h=H),
                                                   bc(w, 3, C),
                                                   g[b][:, u, :, 0:D].rearrange("p s (h c) -> p s h c", h=H), ALU.mult)
                        last.then_inc(prods, 1)

                    def merge(k, b, u):
                        shrunk, taken = shrink[b][:, 0, :, :], shrink[b][:, 1, :, :]
                        dve.wait_ge(summed, k * B + u + 3)
                        dve.wait_ge(kept, k * B + u + 1)
                        V.tensor_tensor(term[:, :, 0:C],
                                        sums[b][u][:, 0:T * D].rearrange("p (l c) -> p l c", c=C),
                                        bc(taken[:, :, u], 2, C), ALU.mult)
                        V.tensor_tensor(term[:, :, C], si[:, u, :], taken[:, :, u], ALU.mult)
                        V.tensor_tensor(A_[u % 2][:, :, :], A_[1 - u % 2][:, :, :], bc(shrunk[:, :, u], 2, C + 1), ALU.mult)
                        dve.drain()
                        V.tensor_tensor(A_[u % 2][:, :, :], A_[u % 2][:, :, :], term,
                                        ALU.add).then_inc(merged, 1)
                        dve.drain()

                    def item_sums(k, b):
                        dve.wait_ge(weighed, k + 1)
                        V.tensor_reduce(si[:, :, :], sc[b][:, :, :, :].rearrange("p u s l -> p u l s"), AX.X, ALU.add)

                    for c in rec_read:
                        dve.sem_inc(c, 1)
                    dve.sem_inc(prods, 2 * B)
                    n = turns(dve)
                    V.memset(run_max[:, :, :], LOW)
                    V.memset(lift[:, :, :], -BIG)
                    V.memset(A_[1][:, :, :], 0.0)
                    dve.drain()
                    if ahead:
                        scores(0, 0)
                        maxima(0, 0)
                    with dve.Fori(0, n) as i:
                        for b in range(2):
                            k = i * 2 + b
                            if not ahead:
                                scores(i, b)
                                maxima(k, b)
                            item_sums(k, b)
                            weigh(k, b, 0)
                            weigh(k, b, 1)
                            if ahead:
                                scores(i + b, 1 - b)
                                dve.wait_ge(shr_ok, k + 1)
                                weigh(k, b, 2)
                                merge(k, b, 0)
                                weigh(k, b, 3)
                                merge(k, b, 1)
                                maxima(k + 1, 1 - b)
                            else:
                                dve.wait_ge(shr_ok, k + 1)
                                merge(k, b, 0)
                                weigh(k, b, 2)
                                merge(k, b, 1)
                                weigh(k, b, 3)
                            merge(k, b, 2)
                            merge(k, b, 3)

        def normalised(v, t, mean, var, tag):
            half = sem(f"variance_{tag}")
            root = sem(f"root_{tag}")

            def vector(dve):
                V.tensor_reduce(mean, v, AX.X, ALU.add)
                dve.drain()
                V.tensor_scalar(mean, mean, 1.0 / D, None, ALU.mult)
                dve.drain()
                V.tensor_tensor(v, v, bc(mean, 2, D), ALU.subtract)
                dve.drain()
                V.tensor_tensor(t, v, v, ALU.mult)
                dve.drain()
                V.tensor_reduce(var, t, AX.X, ALU.add)
                dve.drain()
                V.tensor_scalar(var, var, 1.0 / D, 1e-5, ALU.mult, ALU.add).then_inc(half, 1)
                dve.wait_ge(root, 1)
                V.reciprocal(var, var)
                dve.drain()
                V.tensor_tensor(v, v, bc(var, 2, D), ALU.mult)
                dve.drain()

            def scalar(act):
                act.wait_ge(half, 1)
                A.activation(var, var, ACT.Sqrt).then_inc(root, 1)
            return vector, scalar

        with ExitStack() as att:
            SUMS0 = NTP * T4 * H * (C + 1)
            ROOM0 = NTP * T4 * A0
            big = sb("big", [P, max(ROOM0, SUMS0 + U * S * A0)], fp32, att)
            own1 = sb("own_layer1", [P, NTP, H], fp32, att)
            mean = sb("mean", [P, NTP], fp32, att)
            var = sb("var", [P, NTP], fp32, att)
            W2 = 2 * A0
            stage0 = big[:, 0:ROOM0].rearrange("p (j w) -> p j w", j=NTP)

            def room(at, *shape):
                size = 1
                for k in shape:
                    size *= k
                names = "abcd"[:len(shape)]
                v = big[:, at:at + size].rearrange(f"p ({' '.join(names)}) -> p {' '.join(names)}",
                                                   **dict(zip(names, shape)))
                return v, at + size

            def scratch(T):
                hf = flat(h[:, :, :])
                n, m = S * T * D, T * H * (C + 1)
                prod = [hf[:, v * n:(v + 1) * n].rearrange("p (s w) -> p s w", s=S) for v in range(2)]
                term = hf[:, 2 * n:2 * n + m].rearrange("p (l c) -> p l c", c=C + 1)
                zt = hf[:, 2 * n + m:2 * n + m + B * S * T4 * H * K5].rearrange(
                    "p (u s w) -> p u s w", u=B, s=S) if T > 1 else None
                return prod, term, zt

            def at0(a, z):
                return lambda t: flat(stage0[:, ds(t, 1), a:z])

            r0 = flat(rhs0[:, :, :])
            own0 = flat(h[:, :, :])[:, 0:NTP * T4 * H * K5].rearrange("p (j w) -> p j w", j=NTP)
            node_table("L0", xr, rhs0,
                       [(0, 0, W2, r0[:, 0:W2], [(0, W2, at0(0, W2))]),
                        (1, 0, W2, r0[:, W2:2 * W2], [(0, W2, at0(W2, 2 * W2))]),
                        (2, 0, T4 * 20, flat(rhs0i[:, :, :]),
                         [(0, T4 * 20, lambda t: flat(own0[:, ds(t, 1), :]))])],
                       stage0, tab0_d)
            own_out = sem("own_parts_stored")
            with nc.Block() as block:
                @block.sync
                def _(sp):
                    sp.dma_start(own0_d, own0).then_inc(own_out, 16)
                    sp.wait_ge(own_out, 16)

                @block.vector
                def _(dve):
                    V.tensor_tensor(xr[:, :, :], xr[:, :, :], bc(bias[:, 0, :], 1, NTP), ALU.add)
                    dve.drain()
                    V.tensor_tensor(xr[:, :, :], xr[:, :, :], stage0[:, :, 0:D], ALU.add)
            L0 = T4 * H
            acc0, at = room(0, NTP, L0 * (C + 1))
            g0 = []
            for b in range(2):
                v, at = room(at, B, S, A0)
                g0.append(v)
            attention("L0", T4, tab0_d.rearrange("n (t w) -> (n t) w", t=T4), own0_d, acc0, g0, *scratch(T4))
            ln_v, ln_s = normalised(xr[:, :, :], h[:, :, :], mean[:, :], var[:, :], "L0")
            with nc.Block() as block:
                @block.vector
                def _(dve):
                    a = acc0[:, 0:NT, :].rearrange("p j (l c) -> p j l c", c=C + 1)
                    srun = big[:, SUMS0:SUMS0 + NT * L0].rearrange("p (j l) -> p j l", j=NT)
                    V.tensor_scalar(srun, a[:, :, :, C], 1e-30, None, ALU.max)
                    dve.drain()
                    V.reciprocal(srun, srun)
                    dve.drain()
                    for t in range(T4):
                        V.tensor_scalar(srun[:, :, t * H:(t + 1) * H], srun[:, :, t * H:(t + 1) * H],
                                        impt[:, t:t + 1], None, ALU.mult)
                    dve.drain()
                    for t in range(T4):
                        V.tensor_tensor(h[:, 0:NT, :].rearrange("p j (h c) -> p j h c", h=H),
                                        a[:, :, t * H:(t + 1) * H, 0:C],
                                        bc(srun[:, :, t * H:(t + 1) * H], 3, C), ALU.mult)
                        dve.drain()
                        V.tensor_tensor(xr[:, 0:NT, :], xr[:, 0:NT, :], h[:, 0:NT, :], ALU.add)
                        dve.drain()
                    ln_v(dve)
                    V.tensor_copy(h[:, :, :], xr[:, :, :])

                @block.scalar
                def _(act):
                    ln_s(act)

            fresh_semaphores()
            stage1, at = room(0, NTP, A1)
            acc1, at = room(at, NTP, H * (C + 1))
            g1 = []
            for b in range(2):
                v, at = room(at, B, S, A1)
                g1.append(v)
            s1, at = room(at, NT, H)
            for l in range(3):
                node_table(f"L1{l}", h, rhs1,
                           [(0, 0, D + 2 * H, rhs1[:, l, :],
                             [(0, A1, lambda t: flat(stage1[:, ds(t, 1), :])),
                              (A1, A1 + H, lambda t: flat(own1[:, ds(t, 1), :]))])],
                           stage1, tab1_d[l])
                attention(f"L1{l}", 1, tab1_d[l], own1, acc1, g1, *scratch(1))
                if l == 2:
                    ln_v, ln_s = normalised(xr[:, :, :], h[:, :, :], mean[:, :], var[:, :], "L1")
                with nc.Block() as block:
                    @block.vector
                    def _(dve):
                        a = acc1[:, 0:NT, :].rearrange("p j (l c) -> p j l c", c=C + 1)
                        V.tensor_scalar(s1, a[:, :, :, C], 1e-16, None, ALU.add)
                        dve.drain()
                        V.reciprocal(s1, s1)
                        dve.drain()
                        V.tensor_tensor(h[:, 0:NT, :].rearrange("p j (h c) -> p j h c", h=H),
                                        a[:, :, :, 0:C], bc(s1, 3, C), ALU.mult)
                        V.memset(h[:, NT:NTP, :], 0.0)
                        dve.drain()
                        V.tensor_tensor(h[:, :, :], h[:, :, :], bc(bias[:, l + 1, :], 1, NTP), ALU.add)
                        dve.drain()
                        if l < 2:
                            V.tensor_scalar(h[:, :, :], h[:, :, :], 0.0, None, ALU.max)
                        else:
                            V.tensor_tensor(xr[:, :, :], xr[:, :, :], h[:, :, :], ALU.add)
                            dve.drain()
                            ln_v(dve)

                    if l == 2:
                        @block.scalar
                        def _(act):
                            ln_s(act)
                fresh_semaphores()

        with ExitStack() as mlp:
            big = sb("big2", [P, NTP * HID], fp32, mlp)
            w1 = sb("w1", [P, 2, HID], fp32, mlp)
            w2 = sb("w2", [P, 2, HID], fp32, mlp)
            w3 = sb("w3", [P, 2, HID], fp32, mlp)
            w4 = sb("w4", [P, 3, HID], fp32, mlp)
            w5 = sb("w5", [P, 2, D], fp32, mlp)
            ba = sb("ba", [P, 2], fp32, mlp)
            bb = sb("bb", [P, 2], fp32, mlp)
            bcr = sb("bcr", [P, HID], fp32, mlp)
            b4 = sb("b4", [P, HID], fp32, mlp)
            b5 = sb("b5", [P, D], fp32, mlp)
            wm_in = sem("mlp_weights_in")
            with nc.Block() as block:
                @block.sync
                def _(sp):
                    for to, frm in ((w1[:, :, :], w1a), (w2[:, :, :], w1b), (w3[:, :, :], w1c), (w4[:, :, :], w2a),
                                    (w5[:, :, :], w2b), (ba[:, :], b1a), (bb[:, :], b1b),
                                    (bcr[:, :], b1c.partition_broadcast(P)), (b4[:, :], b2a.partition_broadcast(P)),
                                    (b5[:, :], b2b.partition_broadcast(P))):
                        sp.dma_start(to, frm).then_inc(wm_in, 16)
                    sp.wait_ge(wm_in, 160)
            stage2 = big[:, :].rearrange("p (j w) -> p j w", j=NTP)
            node_table("L2", xr, w1,
                       [(0, 0, HID, w1[:, 0, :], [(0, HID, lambda t: flat(stage2[:, ds(t, 1), :]))])],
                       stage2, tab2_d)

            with ExitStack() as ph:
                total = big[:, :].rearrange("p (j f n) -> p j f n", j=NTP, f=2)
                rec = [sb(f"rec_m{u}", [P, REC], i32, ph) for u in range(U)]
                gx = [sb(f"gx{u}", [P, S, HID], fp32, ph) for u in range(U)]
                ge = [sb(f"ge{u}", [P, S, D], fp32, ph) for u in range(U)]
                off = [sb(f"off{u}", [P, S], bf16, ph) for u in range(U)]
                eT = [sb(f"eT{v}", [P, S * P], fp32, ph) for v in range(2)]
                h1 = [sb(f"h1_{f}", [P, S * P], fp32, ph) for f in range(2)]
                h2 = [sb(f"h2_{f}", [P, S, P], fp32, ph) for f in range(2)]
                part = [sb(f"partial{f}", [P, P], fp32, ph) for f in range(2)]
                psT = [pb(f"psT{v}", [P, 512], fp32, ph) for v in range(2)]
                ps1 = [pb(f"ps1_{f}", [P, 512], fp32, ph) for f in range(2)]
                ps2 = [pb(f"ps2_{f}", [P, 512], fp32, ph) for f in range(2)]
                rec_in = [sem(f"rec_in_m{u}") for u in range(U)]
                rec_free = [sem(f"rec_free_m{u}") for u in range(U)]
                gathered = [sem(f"gathered_m{u}") for u in range(U)]
                rows_used = [sem(f"rows_used_m{u}") for u in range(U)]
                gate = sem("gate_m")
                gate_v = sem("gate_mv")
                masks = sem("masks_ready_m")
                turned = sem("edges_transposed_m")
                eT_ok = sem("edges_stored_m")
                lin1 = sem("hidden1_linear_m")
                act1 = sem("hidden1_ready_m")
                lin2 = sem("hidden2_linear_m")
                act2 = sem("hidden2_ready_m")
                summed = sem("hidden2_summed_m")
                block = ph.enter_context(nc.Block())

                @block.sync
                def _(sp):
                    n = turns(sp)
                    with sp.Fori(0, n) as i:
                        for u in range(U):
                            sp.wait_ge(rec_free[u], i + 1)
                            sp.dma_start(rec[u][:, :], rec_d[ds(i * U + u, 1), :, :]
                                         .rearrange("a p w -> (a p) w")).then_inc(rec_in[u], 16)

                @block.gpsimd
                def _(pool):
                    n = turns(pool)
                    with pool.Fori(0, n) as i:
                        for u in range(U):
                            pool.wait_ge(rec_in[u], (i + 1) * 16)
                            pool.wait_ge(rows_used[u], i + 1)
                            pool.sem_inc(gate, 1)
                            for s in range(S):
                                G.indirect_dma_start(out=ge[u][:, s, :], out_offset=None, in_=edge_attr,
                                                     in_offset=bass.IndirectOffsetOnAxis(
                                                         ap=rec[u][:, R_EID + s:R_EID + s + 1].bitcast(u32), axis=0)
                                                     ).then_inc(gathered[u], 16)
                            for s in range(S):
                                G.indirect_dma_start(out=gx[u][:, s, :], out_offset=None, in_=tab2_d,
                                                     in_offset=bass.IndirectOffsetOnAxis(
                                                         ap=rec[u][:, R_SRC + s:R_SRC + s + 1].bitcast(u32), axis=0)
                                                     ).then_inc(gathered[u], 16)

                @block.tensor
                def _(pe):
                    for c in (lin2, *rows_used):
                        pe.sem_inc(c, 1)
                    n = turns(pe)
                    with pe.Fori(0, n) as i:
                        for u in range(U):
                            g = i * U + u
                            pe.wait_ge(gathered[u], (i + 1) * 32 * S)
                            pe.wait_ge(eT_ok, (g - 1 if u else g) + 1)
                            for s in range(S):
                                last = PE.transpose(psT[u % 2][:, s * P:(s + 1) * P], ge[u][:, s, :], ident[:, :])
                            last.then_inc(turned, 1)
                            pe.wait_ge(act1, g * 2 + 1)
                            for f in range(2):
                                for s in range(S):
                                    last = PE.matmul(ps1[f][:, s * P:(s + 1) * P], gx[u][:, s, f * P:(f + 1) * P],
                                              ident[:, :], start=(s == 0), stop=False, skip_group_check=True)
                            last.then_inc(rows_used[u], 1)
                            pe.wait_ge(eT_ok, g + 2)
                            for f in range(2):
                                last = PE.matmul(ps1[f][:, :], w1[:, 1, f * P:(f + 1) * P], eT[u % 2][:, :],
                                                 start=False, stop=True, skip_group_check=True)
                                last.then_inc(lin1, 1)
                            pe.wait_ge(act2, g * 2 + 1)
                            pe.wait_ge(masks, g + 1)
                            for f in range(2):
                                for s in range(S):
                                    PE.matmul(ps2[f][:, s * P:(s + 1) * P],
                                              off[u][:, s:s + 1].to_broadcast([P, P]), identb[:, :],
                                              start=(s == 0), stop=False, skip_group_check=True)
                            pe.wait_ge(act1, g * 2 + 2 + 1)
                            for f in range(2):
                                for k in range(2):
                                    last = PE.matmul(ps2[f][:, :], w2[:, k, f * P:(f + 1) * P], h1[k][:, :],
                                                     start=False, stop=(k == 1), skip_group_check=True)
                                last.then_inc(lin2, 1)

                @block.scalar
                def _(act):
                    for c in (eT_ok, act1, act2):
                        act.sem_inc(c, 1)
                    n = turns(act)
                    with act.Fori(0, n) as i:
                        for u in range(U):
                            g = i * U + u
                            act.wait_ge(turned, g + 1)
                            A.activation(eT[u % 2][:, :], psT[u % 2][:, :], ACT.Copy).then_inc(eT_ok, 1)
                            act.wait_ge(lin2, g * 2 + 1)
                            for f in range(2):
                                act.wait_ge(lin1, g * 2 + f + 1)
                                A.activation(h1[f][:, :], ps1[f][:, :], ACT.Relu, bias=ba[:, f:f + 1]).then_inc(act1, 1)
                            act.wait_ge(summed, g * 2 + 1)
                            for f in range(2):
                                act.wait_ge(lin2, g * 2 + f + 2)
                                A.activation(flat(h2[f][:, :, :]), ps2[f][:, :], ACT.Relu, bias=bb[:, f:f + 1]
                                             ).then_inc(act2, 1)

                @block.vector
                def _(dve):
                    for c in (*rec_free, summed):
                        dve.sem_inc(c, 1)
                    n = turns(dve)
                    V.memset(big[:, :], 0.0)
                    dve.drain()
                    with dve.Fori(0, n) as i:
                        for u in range(U):
                            g = i * U + u
                            dve.wait_ge(rec_in[u], (i + 1) * 16)
                            dve.sem_inc(gate_v, 1)
                            j = dve.value_load(rec[u][0:1, R_J:R_J + 1], min_val=0, max_val=NT)
                            V.tensor_copy(off[u][:, :], rec[u][:, R_ANY:R_ANY + S].bitcast(fp32)).then_inc(masks, 1)
                            for f in range(2):
                                dve.wait_ge(act2, g * 2 + f + 2)
                                V.tensor_reduce(part[f][:, :], h2[f][:, :, :].rearrange("p s n -> p n s"), AX.X, ALU.add
                                                ).then_inc(summed, 1)
                            dve.drain()
                            for f in range(2):
                                t = total[:, ds(j, 1), f, :].rearrange("p a n -> p (a n)")
                                last = V.tensor_tensor(t, t, part[f][:, :], ALU.add)
                            dve.wait_ge(gathered[u], (i + 1) * 32 * S)
                            dve.sem_inc(gate_v, 1)
                            V.drain().then_inc(rec_free[u], 1)

            with ExitStack() as ph:
                inv = sb("inv", [P, NTP], fp32, ph)
                has = sb("has", [P, NTP], fp32, ph)
                fx = sb("fx", [P, 2, P], fp32, ph)
                su = [sb(f"su{v}", [P, 2, P], fp32, ph) for v in range(2)]
                xc = [sb(f"xc{v}", [P, P], fp32, ph) for v in range(2)]
                ag = [sb(f"ag{v}", [P, HID], fp32, ph) for v in range(2)]
                kT = [sb(f"kT{v}", [P, 3, P], fp32, ph) for v in range(2)]
                zz = [sb(f"zz{v}", [P, HID], fp32, ph) for v in range(2)]
                zT = [sb(f"zT{v}", [P, 2, P], fp32, ph) for v in range(2)]
                pA = [pb(f"pA{v}", [P, 512], fp32, ph) for v in range(2)]
                pT = [pb(f"pT{v}", [P, 512], fp32, ph) for v in range(2)]
                pZ = [pb(f"pZ{v}", [P, 512], fp32, ph) for v in range(2)]
                pO = [pb(f"pO{v}", [P, 512], fp32, ph) for v in range(2)]
                total = big[:, :].rearrange("p (j f n) -> p j f n", j=NTP, f=2)
                fetched = sem("sums_fetched_n")
                aggp = sem("agg_product_n")
                agg = sem("agg_ready_n")
                tr1 = sem("inputs_transposed_n")
                st1 = sem("inputs_stored_n")
                lin = sem("hidden_linear_n")
                hid = sem("hidden_ready_n")
                tr2 = sem("hidden_transposed_n")
                st2 = sem("hidden_stored_n")
                fin = sem("mlp_output_n")
                added = sem("mlp_output_added_n")
                block = ph.enter_context(nc.Block())

                @block.scalar
                def _(act):
                    with act.Fori(0, NTP // 2) as i:
                        for v in range(2):
                            t = i * 2 + v
                            act.wait_ge(fin, i * 2 + 1)
                            A.activation(su[v][:, :, :], total[:, ds(t, 1), :, :].rearrange("p a f n -> p (a f) n"),
                                         ACT.Copy)
                            A.activation(xc[v][:, :], flat(xr[:, ds(t, 1), :]), ACT.Copy).then_inc(fetched, 1)
                        for v in range(2):
                            act.wait_ge(tr1, i * 2 + v + 1)
                            A.activation(kT[v][:, :, :], pT[v][:, 0:3 * P].rearrange("p (a n) -> p a n", a=3),
                                         ACT.Copy).then_inc(st1, 1)
                        for v in range(2):
                            act.wait_ge(tr2, i * 2 + v + 1)
                            A.activation(zT[v][:, :, :], pT[v][:, 0:2 * P].rearrange("p (a n) -> p a n", a=2),
                                         ACT.Copy).then_inc(st2, 1)

                @block.tensor
                def _(pe):
                    for c in (fin,):
                        pe.sem_inc(c, 1)
                    with pe.Fori(0, NTP // 2) as i:
                        for v in range(2):
                            pe.wait_ge(fetched, i * 2 + v + 1)
                            for k in range(2):
                                last = PE.matmul(pA[v][:, 0:HID], su[v][:, k, :], w3[:, k, :], start=(k == 0), stop=(k == 1))
                            last.then_inc(aggp, 1)
                        for v in range(2):
                            pe.wait_ge(agg, i * 2 + v + 1)
                            PE.transpose(pT[v][:, 0:P], xc[v][:, :], ident[:, :])
                            for k in range(2):
                                last = PE.transpose(pT[v][:, (k + 1) * P:(k + 2) * P], ag[v][:, k * P:(k + 1) * P],
                                                    ident[:, :])
                            last.then_inc(tr1, 1)
                        for v in range(2):
                            pe.wait_ge(st1, i * 2 + v + 1)
                            for k in range(3):
                                last = PE.matmul(pZ[v][:, 0:HID], kT[v][:, k, :], w4[:, k, :], start=(k == 0), stop=(k == 2))
                            last.then_inc(lin, 1)
                        for v in range(2):
                            pe.wait_ge(hid, i * 2 + v + 1)
                            for k in range(2):
                                last = PE.transpose(pT[v][:, k * P:(k + 1) * P], zz[v][:, k * P:(k + 1) * P], ident[:, :])
                            last.then_inc(tr2, 1)
                        for v in range(2):
                            pe.wait_ge(st2, i * 2 + v + 1)
                            pe.wait_ge(added, i * 2 + 1)
                            for k in range(2):
                                last = PE.matmul(pO[v][:, 0:D], zT[v][:, k, :], w5[:, k, :], start=(k == 0), stop=(k == 1))
                            last.then_inc(fin, 1)

                @block.vector
                def _(dve):
                    for c in (added,):
                        dve.sem_inc(c, 1)
                    V.tensor_scalar(inv[:, :], degI[:, :], 1.0, None, ALU.max)
                    V.tensor_scalar(has[:, :], degI[:, :], 1.0, None, ALU.min)
                    dve.drain()
                    V.reciprocal(inv[:, :], inv[:, :])
                    dve.drain()
                    with dve.Fori(0, NTP // 2) as i:
                        for v in range(2):
                            t = i * 2 + v
                            dve.wait_ge(aggp, i * 2 + v + 1)
                            V.tensor_scalar(ag[v][:, :], pA[v][:, 0:HID], inv[:, ds(t, 1)], None, ALU.mult)
                            V.drain()
                            V.scalar_tensor_tensor(ag[v][:, :], bcr[:, :], has[:, ds(t, 1)], ag[v][:, :],
                                                   ALU.mult, ALU.add).then_inc(agg, 1)
                        for v in range(2):
                            dve.wait_ge(lin, i * 2 + v + 1)
                            V.tensor_tensor(zz[v][:, :], pZ[v][:, 0:HID], b4[:, :], ALU.add)
                            V.drain()
                            V.tensor_scalar(zz[v][:, :], zz[v][:, :], 0.0, None, ALU.max).then_inc(hid, 1)
                        for v in range(2):
                            t = i * 2 + v
                            dve.wait_ge(fin, i * 2 + v + 2)
                            x_ = flat(xr[:, ds(t, 1), :])
                            V.tensor_tensor(x_, x_, pO[v][:, 0:D], ALU.add).then_inc(added, 1)

            with ExitStack() as ph:
                mean = sb("mean2", [P, NTP], fp32, ph)
                var = sb("var2", [P, NTP], fp32, ph)
                ln_v, ln_s = normalised(xr[:, :, :], h[:, :, :], mean[:, :], var[:, :], "L2")
                block = ph.enter_context(nc.Block())

                @block.vector
                def _(dve):
                    V.tensor_tensor(xr[:, :, :], xr[:, :, :], bc(b5[:, :], 1, NTP), ALU.add)
                    dve.drain()
                    ln_v(dve)

                @block.scalar
                def _(act):
                    ln_s(act)

        fresh_semaphores()

        with ExitStack() as ph:
            w3 = sb("w3T_", [P, D], fp32, ph)
            iso = sb("iso", [P, NTP], fp32, ph)
            rec = [sb(f"rec_s{u}", [P, REC], i32, ph) for u in range(U)]
            spread = [sb(f"spread{v}", [P, S, P], fp32, ph) for v in range(2)]
            same = [sb(f"same{v}", [P, S, P], fp32, ph) for v in range(2)]
            before = [sb(f"before{v}", [P, S, P], fp32, ph) for v in range(2)]
            dup = [sb(f"dup{v}", [P, S], fp32, ph) for v in range(2)]
            away = [sb(f"away{v}", [P, S], fp32, ph) for v in range(2)]
            to = [sb(f"to{u}", [P, S], u32, ph) for u in range(U)]
            msg = [sb(f"msg{u}", [P, S, D], fp32, ph) for u in range(U)]
            spare = sb("spare", [P, 1], fp32, ph)
            blank = sb("blank", [P, D], fp32, ph)
            blank_ok = sem("blank_ready")
            scaled = [sb(f"scaled{v}", [P, D], fp32, ph) for v in range(2)]
            psR = [pb(f"psR{v}", [P, 512], fp32, ph) for v in range(2)]
            psM = [pb(f"psM{v}", [P, 512], fp32, ph) for v in range(2)]
            w_in = sem("w3_in")
            root = sem("root_s")
            deg_ok = sem("deg_clamped_s")
            x_out = sem("x3_stored")
            rec_in = [sem(f"rec_in_s{u}") for u in range(U)]
            spr_ok = sem("sources_spread")
            rows_ok = sem("sources_in_rows")
            same_ok = sem("equality_ready")
            to_ok = sem("targets_ready")
            msg_ps = sem("messages_summed")
            msg_ok = sem("messages_stored")
            sc_ok = sem("scaled_ready")
            used = sem("slots_used_s")
            added = [sem(f"added_{s}") for s in range(S)]
            gate = sem("gate_s")
            passed = sem("adds_before_this_done")
            gate_v = sem("gate_sv")

            with nc.Block() as block:
                @block.sync
                def _(sp):
                    sp.dma_start(w3[:, :], w3T).then_inc(w_in, 16)
                    sp.wait_ge(w_in, 16)

                @block.gpsimd
                def _(pool):
                    for j in range(NTP):
                        G.indirect_dma_start(out=x3_d, out_offset=bass.IndirectOffsetOnAxis(
                            ap=nid[:, j:j + 1].bitcast(u32), axis=0), in_=xr[:, j, :], in_offset=None).then_inc(x_out, 16)
                    pool.wait_ge(blank_ok, 1)
                    for s in range(S):
                        pool.dma_start(sum_d[s][NPAD:ROWS, :], blank[:, :]).then_inc(added[s], 16)
                    pool.wait_ge(x_out, 16 * NTP)
                    for s in range(S):
                        pool.wait_ge(added[s], 16)

                @block.vector
                def _(dve):
                    V.memset(blank[:, :], 0.0).then_inc(blank_ok, 1)
                    V.tensor_scalar(iso[:, :], degO[:, :], 1.0, None, ALU.max).then_inc(deg_ok, 1)
                    V.tensor_scalar(spare[:, :], place[:, :], float(NT * P), None, ALU.add)
                    dve.wait_ge(root, 1)
                    V.reciprocal(iso[:, :], iso[:, :])
                    dve.drain()
                    V.tensor_tensor(h[:, :, :], xr[:, :, :], bc(iso[:, :], 2, D), ALU.mult)

                @block.scalar
                def _(act):
                    act.wait_ge(deg_ok, 1)
                    A.activation(iso[:, :], iso[:, :], ACT.Sqrt).then_inc(root, 1)

            with nc.Block() as block:
                @block.sync
                def _(sp):
                    n = turns(sp)
                    with sp.Fori(0, n) as i:
                        for u in range(U):
                            sp.wait_ge(used, i * U + u + 1)
                            sp.dma_start(rec[u][:, :], rec_d[ds(i * U + u, 1), :, :]
                                         .rearrange("a p w -> (a p) w")).then_inc(rec_in[u], 16)

                @block.tensor
                def _(pe):
                    pe.sem_inc(msg_ps, 2)
                    n = turns(pe)
                    with pe.Fori(0, n) as i:
                        for u in range(U):
                            g, v = i * U + u, u % 2
                            if v == 0:
                                for w in range(2):
                                    pe.wait_ge(spr_ok, g + w + 1)
                                    for s in range(S):
                                        last = PE.transpose(psR[w][:, s * P:(s + 1) * P], spread[w][:, s, :], ident[:, :])
                                    last.then_inc(rows_ok, 1)
                            pe.wait_ge(same_ok, g + 1)
                            pe.wait_ge(sc_ok, g + 1)
                            pe.wait_ge(msg_ok, g + 1)
                            for s in range(S):
                                last = PE.matmul(psM[v][:, s * P:(s + 1) * P], same[v][:, s, :], scaled[v][:, :],
                                                 start=True, stop=True)
                            last.then_inc(msg_ps, 1)

                @block.scalar
                def _(act):
                    act.sem_inc(msg_ok, 2)
                    n = turns(act)
                    with act.Fori(0, n) as i:
                        for u in range(U):
                            g, v = i * U + u, u % 2
                            act.wait_ge(msg_ps, g + 3)
                            act.wait_ge(passed, g * S + 2 * S)
                            A.activation(flat(msg[u][:, :, :]), psM[v][:, :], ACT.Copy).then_inc(msg_ok, 1)

                @block.vector
                def _(dve):
                    dve.sem_inc(used, U)
                    n = turns(dve)
                    with dve.Fori(0, n) as i:
                        for u in range(U):
                            g, v = i * U + u, u % 2
                            if v == 0:
                                for w in range(2):
                                    dve.wait_ge(rec_in[u + w], (i + 1) * 16)
                                    dve.sem_inc(gate_v, 1)
                                    j = dve.value_load(rec[u + w][0:1, R_J:R_J + 1], min_val=0, max_val=NT)
                                    V.tensor_copy(spread[w][:, :, :], bc(rec[u + w][:, R_SUM:R_SUM + S].bitcast(fp32), 2, P)
                                                  ).then_inc(spr_ok, 1)
                                    dve.wait_ge(msg_ps, g + w + 1)
                                    V.tensor_copy(scaled[w][:, :], flat(h[:, ds(j, 1), :])).then_inc(sc_ok, 1)
                            srcs = rec[u][:, R_SUM:R_SUM + S].bitcast(fp32)
                            V.tensor_tensor(away[v][:, :], spare[:, :].to_broadcast([P, S]), srcs, ALU.subtract)
                            dve.wait_ge(msg_ps, g + 1)
                            dve.wait_ge(rows_ok, g + 1)
                            V.tensor_tensor(same[v][:, :, :], psR[v][:, :].rearrange("p (s n) -> p s n", s=S),
                                            bc(srcs, 2, P), ALU.is_equal).then_inc(same_ok, 1)
                            dve.drain()
                            V.tensor_tensor(before[v][:, :, :], same[v][:, :, :], bc(lower[:, :], 1, S), ALU.mult)
                            dve.drain()
                            V.tensor_reduce(dup[v][:, :], before[v][:, :, :], AX.X, ALU.max)
                            dve.drain()
                            V.tensor_tensor(away[v][:, :], away[v][:, :], dup[v][:, :], ALU.mult)
                            dve.drain()
                            dve.wait_ge(passed, g * S + 2 * S)
                            V.tensor_tensor(to[u][:, :], away[v][:, :], srcs, ALU.add).then_inc(to_ok, 1)
                            V.drain().then_inc(used, 1)

                @block.gpsimd
                def _(pool):
                    pool.sem_inc(passed, S * U)
                    n = turns(pool)
                    with pool.Fori(0, n) as i:
                        for u in range(U):
                            g = i * U + u
                            pool.wait_ge(to_ok, g + 1)
                            pool.wait_ge(msg_ok, g + 3)
                            for s in range(S):
                                pool.wait_ge(added[s], g * 16 + 16)
                                pool.sem_inc(passed, 1)
                                G.indirect_dma_start(out=sum_d[s], out_offset=bass.IndirectOffsetOnAxis(
                                    ap=to[u][:, s:s + 1], axis=0), in_=msg[u][:, s, :], in_offset=None,
                                    compute_op=ALU.add).then_inc(added[s], 16)
                    for s in range(S):
                        pool.wait_ge(added[s], n * 16 * U + 16)
                    pool.sem_inc(gate, 1)

            with ExitStack() as fi:
                q = [sb(f"q{s}", [P, NT, D], fp32, fi) for s in range(2)]
                xn = sb("xn", [P, NT, D], fp32, fi)
                ison = sb("ison", [P, NT], fp32, fi)
                hc = [sb(f"hcf{v}", [P, P], fp32, fi) for v in range(2)]
                ht = [sb(f"htf{v}", [P, P], fp32, fi) for v in range(2)]
                mean = sb("mean3", [P, NT], fp32, fi)
                var = sb("var3", [P, NT], fp32, fi)
                pt = [pb(f"ptf{v}", [P, 512], fp32, fi) for v in range(2)]
                pm = [pb(f"pmf{v}", [P, 512], fp32, fi) for v in range(2)]
                xn_in = sem("xn_in")
                q_in = sem("sums_in")
                q_used = sem("sums_used")
                mroot = sem("root_f")
                agg_ok = sem("aggregate_ready")
                fetched = sem("fetched_f")
                turned = sem("turned_f")
                stored = sem("stored_f")
                mult = sem("mult_f")
                relud = sem("relu_f")
                out_ok = sem("out_ready")
                out_out = sem("out_stored")
                sq = h[:, 0:NT, :]
                agg = q[0]

                with nc.Block() as block:
                    @block.sync
                    def _(sp):
                        def rows(t):
                            return t[0:NT * P, :].rearrange("(j p) c -> p j c", p=P)
                        sp.dma_start(xn[:, :, :], rows(x3_d)).then_inc(xn_in, 16)
                        sp.dma_start(q[0][:, :, :], rows(sum_d[0])).then_inc(q_in, 16)
                        for s in range(1, S):
                            if s > 1:
                                sp.wait_ge(q_used, s - 1)
                            sp.dma_start(q[1][:, :, :], rows(sum_d[s])).then_inc(q_in, 16)
                        sp.wait_ge(xn_in, 16)

                    @block.scalar
                    def _(act):
                        A.activation(ison[:, :], degOn[:, :], ACT.Sqrt).then_inc(mroot, 1)

                    @block.vector
                    def _(dve):
                        for s in range(1, S):
                            dve.wait_ge(q_in, 16 * (s + 1))
                            V.tensor_tensor(agg[:, :, :], agg[:, :, :], q[1][:, :, :], ALU.add).then_inc(q_used, 1)
                            dve.drain()
                        dve.wait_ge(mroot, 1)
                        V.reciprocal(ison[:, :], ison[:, :])
                        dve.drain()
                        V.tensor_tensor(agg[:, :, :], agg[:, :, :], bc(ison[:, :], 2, D), ALU.mult)

                def per_tile(eng, body):
                    with eng.Fori(0, NT // 2) as i:
                        body(i, range(2))
                    body(NT // 2, range(1))

                with nc.Block() as block:
                    @block.scalar
                    def _(act):
                        act.sem_inc(stored, 1)
                        def body(i, vs):
                            for v in vs:
                                act.wait_ge(turned, i * 2 + 1)
                                A.activation(hc[v][:, :], flat(agg[:, ds(i * 2 + v, 1), :]), ACT.Copy).then_inc(fetched, 1)
                            for v in vs:
                                act.wait_ge(turned, i * 2 + v + 2)
                                act.wait_ge(mult, i * 2 + 1)
                                A.activation(ht[v][:, :], pt[v][:, 0:P], ACT.Copy).then_inc(stored, 1)
                        per_tile(act, body)

                    @block.tensor
                    def _(pe):
                        pe.sem_inc(turned, 1)
                        pe.sem_inc(mult, 1)
                        def body(i, vs):
                            for v in vs:
                                pe.wait_ge(fetched, i * 2 + v + 1)
                                pe.wait_ge(stored, i * 2 + 1)
                                PE.transpose(pt[v][:, 0:P], hc[v][:, :], ident[:, :]).then_inc(turned, 1)
                            for v in vs:
                                pe.wait_ge(stored, i * 2 + v + 2)
                                pe.wait_ge(relud, i * 2 + 1)
                                PE.matmul(pm[v][:, 0:D], ht[v][:, :], w3[:, :], start=True, stop=True).then_inc(mult, 1)
                        per_tile(pe, body)

                    @block.vector
                    def _(dve):
                        dve.sem_inc(relud, 1)
                        def body(i, vs):
                            for v in vs:
                                dve.wait_ge(mult, i * 2 + v + 2)
                                x_ = flat(xn[:, ds(i * 2 + v, 1), :])
                                V.scalar_tensor_tensor(x_, pm[v][:, 0:D], 0.0, x_, ALU.max, ALU.add).then_inc(relud, 1)
                        per_tile(dve, body)

                ln_v, ln_s = normalised(xn[:, :, :], sq, mean[:, :], var[:, :], "L3")
                with nc.Block() as block:
                    @block.vector
                    def _(dve):
                        ln_v(dve)
                        V.drain().then_inc(out_ok, 1)

                    @block.scalar
                    def _(act):
                        ln_s(act)

                    @block.sync
                    def _(sp):
                        sp.wait_ge(out_ok, 1)
                        full = N // P
                        sp.dma_start(out[0:full * P, :].rearrange("(j p) c -> p j c", p=P),
                                     xn[:, 0:full, :]).then_inc(out_out, 16)
                        sp.dma_start(out[full * P:N, :], xn[0:N - full * P, full, :]).then_inc(out_out, 16)
                        sp.wait_ge(out_out, 32)


def lay_out(inputs):
    import numpy as np
    g = {k: np.asarray(v) for k, v in inputs.items()}

    def padded(a, rows, value=0):
        return np.concatenate([a, np.full((rows - a.shape[0],) + a.shape[1:], value, a.dtype)])

    arrays = {"x": padded(g["x"], NPAD)}
    for name in ("src", "dst"):
        arrays[name] = padded(g[name], EPAD, NT * P).reshape(P, EC)
    s, t = padded(g["src"], E + S + 1), padded(g["edge_type_4"], E + S + 1)
    arrays["windows"] = np.stack([a[k:k + E + 1] for a in (s, t) for k in range(S)], axis=1)
    arrays["edge_attr"] = g["edge_attr_128"]
    W0 = g["L0_gnn_W"]
    arrays["W0"] = W0.transpose(1, 0, 2)
    arrays["W0T"] = W0.transpose(2, 0, 1)
    att = g["L0_gnn_att_vectors"]
    for name, part in (("attI", att[:, :, :C]), ("attJ", att[:, :, C:])):
        a = np.zeros((H, C, H, K5), np.float32)
        for h in range(H):
            a[h, :, h, :] = part[:, h, :].T
        arrays[name] = a.reshape(D, H * K5)
    arrays["probs"] = g["L0_gnn_confounder_probs"]
    arrays["importance"] = g["L0_gnn_edge_importance"]
    arrays["bias0"] = g["L0_gnn_bias"]
    for name in ("Ws", "Wd"):
        arrays[name] = g["L1_gnn_" + name].transpose(1, 0, 2)
        arrays[name + "T"] = g["L1_gnn_" + name].transpose(2, 0, 1)
    for name, part in (("attS", g["L1_gnn_att_s"]), ("attD", g["L1_gnn_att_d"])):
        a = np.zeros((H, C, 3, H), np.float32)
        for h in range(H):
            a[h, :, :, h] = part[:, h, :].T
        arrays[name] = a.reshape(D, 3, H)
    arrays["bias1"] = g["L1_gnn_b"]
    arrays["w1a"] = g["L2_gnn_w1a"].reshape(2, P, HID).transpose(1, 0, 2)
    arrays["b1a"] = g["L2_gnn_b1a"].reshape(2, P).T
    arrays["w1b"] = g["L2_gnn_w1b"].reshape(2, P, HID).transpose(1, 0, 2)
    arrays["b1b"] = g["L2_gnn_b1b"].reshape(2, P).T
    arrays["w1c"] = g["L2_gnn_w1c"].reshape(2, P, HID).transpose(1, 0, 2)
    arrays["b1c"] = g["L2_gnn_b1c"]
    arrays["w2a"] = g["L2_gnn_w2a"].reshape(3, P, HID).transpose(1, 0, 2)
    arrays["b2a"] = g["L2_gnn_b2a"]
    arrays["w2b"] = g["L2_gnn_w2b"].reshape(2, P, D).transpose(1, 0, 2)
    arrays["b2b"] = g["L2_gnn_b2b"]
    arrays["w3T"] = g["L3_gnn_weight"].T
    arrays = {f"in_{k}": np.ascontiguousarray(v) for k, v in arrays.items()}
    return arrays, None


def kernel(**inputs):
    import numpy as np
    import concourse.bacc as bacc
    from concourse.bass_utils import run_bass_kernel_spmd

    nc = bacc.Bacc("TRN2", target_bir_lowering=False, num_devices=1)
    arrays, _ = lay_out(inputs)
    args = [nc.dram_tensor(k, a.shape, mybir.dt.from_np(a.dtype), kind="ExternalInput").ap()
            for k, a in arrays.items()]
    out = nc.dram_tensor("out", [N, D], mybir.dt.float32, kind="ExternalOutput").ap()
    gnn(nc, *args, out)
    r = run_bass_kernel_spmd(nc, [arrays], core_ids=[0])
    return r.results[0]["out"]
```

```python
import concourse.bass as bass
from concourse import mybir
from contextlib import ExitStack

P = 128
N, E, D = 6250, 100000, 128
NT = -(-N // P)
NTP = NT + 1
NPAD = NTP * P
EC = -(-E // P)
EPAD = EC * P
H, C, K5, T4 = 4, 32, 5, 4
S = 4
B = 4
U = 2 * B
GC = -(-(int(E * 1.04) // S + NTP + 2 * U) // P)
GMAX = GC * P
ROWS = NPAD + P
REC = 20
R_SRC, R_EID, R_SUM, R_ANY, R_J, R_IDX, R_TYPE = 0, S, 2 * S, 3 * S, 4 * S, REC, REC + S
BIG = 2e30
LOW = -1e30
CL = 60
CLS = 10
HALF = 17
A0, A1 = D + H * K5, D + H
HID = 256


def gnn(nc, x, src, dst, windows, edge_windows, W0, W0T, attI, attJ, probs, importance, bias0,
        Ws, WsT, Wd, WdT, attS, attD, bias1, w1a, b1a, w1b, b1b, w1c, b1c, w2a, b2a, w2b, b2b,
        w3T, out):
    fp32, bf16, i32, u32 = mybir.dt.float32, mybir.dt.bfloat16, mybir.dt.int32, mybir.dt.uint32
    ALU, ACT, AX = mybir.AluOpType, mybir.ActivationFunctionType, mybir.AxisListType
    ds = bass.ds
    V, A, PE, G = nc.vector, nc.scalar, nc.tensor, nc.gpsimd

    def dram(name, shape, dt):
        return nc.dram_tensor(name, shape, dt).ap()

    perm_d = dram("nodes_by_degree", [NT * P, 4], i32)
    item_d = dram("item_table", [GMAX, 2], i32)
    rec_d = dram("item_records", [GMAX, P, REC], i32)
    rec0_d = dram("item_records_layer0", [GMAX, P, REC], i32)
    tab0_d = dram("table_layer0", [NPAD, T4 * A0], fp32)
    own0_d = dram("own_parts_layer0", [P, NTP, T4 * H * K5], fp32)
    tab1_d = [dram(f"table_layer1_{i}", [NPAD, A1], fp32) for i in range(3)]
    tab2_d = dram("table_layer2", [NPAD, HID], fp32)
    x3_d = dram("x_before_layer3", [NPAD, D], fp32)
    sum_d = [dram(f"sums_by_source_{s}", [ROWS, D], fp32) for s in range(S)]

    top = ExitStack()
    with top:
        def sb(name, shape, dt=fp32, ctx=top):
            return ctx.enter_context(nc.sbuf_tensor(name, shape, dt))

        def pb(name, shape, dt=fp32, ctx=top):
            return ctx.enter_context(nc.psum_tensor(name, shape, dt))

        live = []

        def sem(name):
            live.append(nc.alloc_semaphore(name=name))
            return live[-1]

        def fresh_semaphores():
            nc.clear_and_free_semaphores(live)
            nc.all_engine_barrier()
            live.clear()


        def bc(ap, axis, n):
            v = ap.unsqueeze(axis)
            shape = list(v.shape)
            shape[axis] = n
            return v.to_broadcast(shape)

        def flat(ap):
            return ap.rearrange("p a c -> p (a c)")

        xr = sb("xr", [P, NTP, D])
        ident = sb("ident", [P, P])
        identb = sb("identb", [P, P], bf16)
        nid = sb("nid", [P, NTP], i32)
        degI = sb("degI", [P, NTP])
        degO = sb("degO", [P, NTP])
        degOn = sb("degOn", [P, NT])
        node_info = sb("node_info", [P, NTP, 2])
        trips = sb("trips", [1, 1], i32)
        iotaS = sb("iotaS", [P, S])
        iotaT = sb("iotaT", [P, T4])
        place = sb("place", [P, 1])
        strict = sb("strict", [P, P])
        lower = sb("lower", [P, P])

        with ExitStack() as ph:
            e32 = [sb(f"e32_{w}", [P, EC], i32, ph) for w in "ds"]
            part = [[sb(f"part_{w}{q}", [P, EC], i32, ph) for q in "lh"] for w in "ds"]
            lo = [sb(f"lo_{w}", [P, EC], bf16, ph) for w in "ds"]
            hi = [sb(f"hi_{w}", [P, EC], bf16, ph) for w in "ds"]
            row128 = sb("row128", [P, P], bf16, ph)
            oneL = [sb(f"oneL{i}", [P, HALF, P], bf16, ph) for i in range(2)]
            oneH = [sb(f"oneH{i}", [P, HALF, NT], bf16, ph) for i in range(2)]
            ones = sb("ones", [P, P], fp32, ph)
            zeros = sb("zeros", [P, D * 2], fp32, ph)
            zerob = sb("zerob", [P, P], bf16, ph)
            nrev = sb("nrev", [P, NT], fp32, ph)
            nnum = sb("nnum", [P, NT], i32, ph)
            degIn = sb("degIn", [P, NT], fp32, ph)
            rsn = sb("rsn", [P, NT], fp32, ph)
            cls = sb("cls", [P, NT], bf16, ph)
            in_cls = sb("in_cls", [P, CL, NT], bf16, ph)
            behind = sb("behind", [P, CL, NT], fp32, ph)
            of_cls = sb("of_cls", [P, CL, NT], fp32, ph)
            up_to = sb("up_to", [P, CL, NT], fp32, ph)
            cones = sb("cones", [P, CL * NT], fp32, ph)
            onesb = sb("onesb", [P, P], bf16, ph)
            strictb = sb("strictb", [P, P], bf16, ph)
            rank = sb("rank", [P, NT], fp32, ph)
            ranki = sb("ranki", [P, NT], u32, ph)
            tot = sb("tot", [P, NT], fp32, ph)
            incl = sb("incl", [P, NT], fp32, ph)
            noderec = sb("noderec", [P, NT, 4], i32, ph)
            permrec = sb("permrec", [P, NTP, 4], i32, ph)
            dmax = sb("dmax", [P, NTP], fp32, ph)
            nci = sb("nci", [P, NTP], i32, ph)
            ncf = sb("ncf", [P, NTP], fp32, ph)
            ends = sb("ends", [P, NTP], fp32, ph)
            tripf = sb("tripf", [1, 1], i32, ph)
            gnum = sb("gnum", [P, GC], fp32, ph)
            jof = sb("jof", [P, 2, GC], fp32, ph)
            start = sb("start", [P, 2, GC], fp32, ph)
            hit = sb("hit", [P, GC], fp32, ph)
            items = sb("items", [P, GC, 2], i32, ph)
            hist = [pb(f"hist_{w}", [P, 512], fp32, ph) for w in "ds"]
            pre = pb("pre", [P, 512], fp32, ph)
            cnt = [[pb(f"cnt_{w}{v}", [P, 512], fp32, ph) for w in "bo"] for v in range(2)]
            edges_in = [sem("edges_in_d"), sem("edges_in_s")]
            consts = sem("consts")
            cst2 = sem("consts_first")
            zeroed = sem("zeroed")
            onehot = [sem("onehot0"), sem("onehot1")]
            counted = [sem("counted0"), sem("counted1")]
            hist_done = sem("hist_done")
            degs = sem("degrees_ready")
            prefix = sem("prefix_done")
            cls_ok = sem("classes_ready")
            cls_cnt = sem("classes_counted")
            cls_use = sem("counts_copied")
            ranks = sem("ranks_ready")
            perm_out = sem("perm_stored")
            perm_in = sem("perm_in")
            perm_ok = sem("perm_unpacked")
            dmax_ok = sem("dmax_ready")
            items_ok = sem("items_ready")
            items_out = sem("items_stored")
            STEPS = EC // (2 * HALF)

            block = ph.enter_context(nc.Block())

            @block.sync
            def _(sp):
                for w, e in enumerate((dst, src)):
                    sp.dma_start(e32[w][:, :], e).then_inc(edges_in[w], 16)
                sp.wait_ge(consts, 1)
                for s in range(S):
                    for r in range(NPAD // P):
                        sp.dma_start(sum_d[s][r * P:(r + 1) * P, :], zeros[:, 0:D]).then_inc(zeroed, 16)
                sp.wait_ge(perm_out, 16 * NT)
                sp.dma_start(permrec[:, 0:NT, :],
                             perm_d[0:NT * P, :].rearrange("(j p) w -> p j w", p=P)).then_inc(perm_in, 16)
                sp.wait_ge(items_ok, 1)
                sp.dma_start(item_d.rearrange("(p c) w -> p c w", p=P), items[:, :, :]).then_inc(items_out, 16)
                sp.wait_ge(items_out, 16)
                sp.wait_ge(zeroed, 16 * S * (NPAD // P))

            @block.gpsimd
            def _(pool):
                G.memset(zeros[:, :], 0.0).then_inc(consts, 1)
                G.memset(cones[:, :], 1.0).then_inc(cst2, 1)
                G.memset(zerob[:, :], 0.0).then_inc(cst2, 1)
                G.memset(ones[:, :], 1.0).then_inc(cst2, 1)
                G.memset(ident[:, :], 0.0).then_inc(cst2, 1)
                G.memset(strict[:, :], 0.0).then_inc(cst2, 1)
                G.memset(lower[:, :], 1.0).then_inc(cst2, 1)
                G.iota(row128[:, :], [[1, P]], base=0, channel_multiplier=0,
                       allow_small_or_imprecise_dtypes=True).then_inc(cst2, 1)
                pool.wait_ge(cst2, 7)
                G.affine_select(out=ident[:, :], in_=ident[:, :], compare_op=ALU.not_equal, fill=1.0,
                                base=0, pattern=[[-1, P]], channel_multiplier=1).then_inc(cst2, 1)
                G.affine_select(out=strict[:, :], in_=strict[:, :], compare_op=ALU.is_ge, fill=1.0,
                                base=0, pattern=[[-1, P]], channel_multiplier=1).then_inc(cst2, 1)
                G.affine_select(out=lower[:, :], in_=lower[:, :], compare_op=ALU.is_gt, fill=0.0,
                                base=0, pattern=[[-1, P]], channel_multiplier=1).then_inc(cst2, 1)
                G.iota(nnum[:, :], [[P, NT]], base=0, channel_multiplier=1).then_inc(cst2, 1)
                G.iota(nrev[:, :], [[-P, NT]], base=8191, channel_multiplier=-1,
                       allow_small_or_imprecise_dtypes=True).then_inc(cst2, 1)
                G.iota(iotaS[:, :], [[1, S]], base=0, channel_multiplier=0,
                       allow_small_or_imprecise_dtypes=True).then_inc(cst2, 1)
                G.iota(iotaT[:, :], [[1, T4]], base=1, channel_multiplier=0,
                       allow_small_or_imprecise_dtypes=True).then_inc(cst2, 1)
                G.iota(place[:, :], [[1, 1]], base=0, channel_multiplier=1,
                       allow_small_or_imprecise_dtypes=True).then_inc(cst2, 1)
                G.iota(gnum[:, :], [[1, GC]], base=0, channel_multiplier=GC,
                       allow_small_or_imprecise_dtypes=True).then_inc(cst2, 1)
                pool.wait_ge(ranks, 1)
                for j in range(NT):
                    G.indirect_dma_start(out=perm_d, out_offset=bass.IndirectOffsetOnAxis(ap=ranki[:, j:j + 1], axis=0),
                                         in_=noderec[:, j, :], in_offset=None).then_inc(perm_out, 16)
                pool.wait_ge(perm_ok, 1)
                G.partition_all_reduce(dmax[:, :], degI[:, :], P, bass.bass_isa.ReduceOp.max).then_inc(dmax_ok, 1)

            @block.vector
            def _(dve):
                for w in range(2):
                    dve.wait_ge(edges_in[w], 16)
                    V.tensor_scalar(part[w][0][:, :], e32[w][:, :], P - 1, None, ALU.bitwise_and)
                    V.tensor_scalar(part[w][1][:, :], e32[w][:, :], 7, None, ALU.arith_shift_right)
                dve.drain()
                for w in range(2):
                    V.tensor_copy(lo[w][:, :], part[w][0][:, :])
                    V.tensor_copy(hi[w][:, :], part[w][1][:, :])
                dve.drain()
                dve.wait_ge(cst2, 16)
                for w in range(2):
                    with dve.Fori(0, STEPS) as i:
                        for v in range(2):
                            dve.wait_ge(counted[v], i + w * STEPS + 1)
                            at = (i * 2 + v) * HALF
                            V.tensor_tensor(oneL[v][:, :, :], bc(lo[w][:, ds(at, HALF)], 2, P),
                                            bc(row128[:, :], 1, HALF), ALU.is_equal)
                            V.tensor_tensor(oneH[v][:, :, :], bc(hi[w][:, ds(at, HALF)], 2, NT),
                                            bc(row128[:, 0:NT], 1, HALF), ALU.is_equal).then_inc(onehot[v], 1)
                dve.wait_ge(hist_done, 1)
                V.tensor_copy(degIn[:, :], hist[0][:, 0:NT])
                V.tensor_copy(degOn[:, :], hist[1][:, 0:NT])
                V.tensor_copy(identb[:, :], ident[:, :])
                V.tensor_copy(strictb[:, :], strict[:, :])
                V.tensor_copy(onesb[:, :], ones[:, :])
                dve.drain()
                V.tensor_scalar(rsn[:, :], degIn[:, :], float(CL - 1), -1.0, ALU.min, ALU.mult).then_inc(degs, 1)
                dve.drain()
                V.tensor_scalar(cls[:, :], rsn[:, :], float(CL - 1), None, ALU.add)
                dve.drain()
                V.tensor_tensor(in_cls[:, :, :], bc(cls[:, :], 1, CL), bc(row128[:, 0:CL], 2, NT),
                                ALU.is_equal).then_inc(cls_ok, 1)
                dve.wait_ge(prefix, 1)
                V.tensor_copy(tot[:, :], pre[:, NT:2 * NT])
                dve.drain()
                V.tensor_tensor_scan(incl[:, :], ones[:, 0:NT], tot[:, :], 0.0, ALU.mult, ALU.add)
                dve.drain()
                V.tensor_tensor(incl[:, :], incl[:, :], tot[:, :], ALU.subtract)
                dve.drain()
                V.tensor_tensor(rsn[:, :], incl[:, :], pre[:, 0:NT], ALU.add)
                dve.drain()
                V.tensor_copy(noderec[:, :, 0], nnum[:, :])
                V.tensor_copy(noderec[:, :, 1], rsn[:, :])
                V.tensor_copy(noderec[:, :, 2], degIn[:, :])
                V.tensor_copy(noderec[:, :, 3], degOn[:, :])
                V.tensor_scalar(incl[:, :], nrev[:, :], float(8191 - N) + 0.5, None, ALU.is_lt)
                dve.drain()
                V.tensor_tensor(degOn[:, :], degOn[:, :], incl[:, :], ALU.max)
                for q in range(CL // CLS):
                    dve.wait_ge(cls_cnt, q + 1)
                    for w, t in enumerate((behind, of_cls)):
                        last = V.tensor_copy(flat(t[:, q * CLS:(q + 1) * CLS, :]), cnt[q % 2][w][:, 0:CLS * NT])
                    last.then_inc(cls_use, 1)
                dve.drain()
                V.tensor_tensor_scan(flat(up_to[:, :, :]), cones[:, :], flat(of_cls[:, :, :]), 0.0, ALU.mult, ALU.add)
                V.tensor_tensor(behind[:, :, :], behind[:, :, :], of_cls[:, :, :], ALU.subtract)
                dve.drain()
                V.tensor_tensor(behind[:, :, :], behind[:, :, :], up_to[:, :, :], ALU.add)
                dve.drain()
                V.tensor_tensor(behind[:, :, :], behind[:, :, :], in_cls[:, :, :], ALU.mult)
                dve.drain()
                V.tensor_reduce(rank[:, :], behind[:, :, :].rearrange("p c j -> p j c"), AX.X, ALU.add)
                dve.drain()
                V.tensor_copy(ranki[:, :], rank[:, :]).then_inc(ranks, 1)
                dve.wait_ge(perm_in, 16)
                V.tensor_copy(nid[:, 0:NT], permrec[:, 0:NT, 0])
                V.tensor_scalar(nid[:, NT:NTP], place[:, :], float(NT * P), None, ALU.add)
                V.memset(node_info[:, NT:NTP, :], 0.0)
                V.memset(degI[:, NT:NTP], 0.0)
                V.memset(degO[:, NT:NTP], 0.0)
                V.tensor_copy(node_info[:, 0:NT, :], permrec[:, 0:NT, 1:3])
                V.tensor_copy(degO[:, 0:NT], permrec[:, 0:NT, 3])
                V.tensor_copy(degI[:, 0:NT], permrec[:, 0:NT, 2]).then_inc(perm_ok, 1)
                dve.wait_ge(dmax_ok, 1)
                V.tensor_scalar(nci[:, :], dmax[:, :], 1.0, float(S - 1), ALU.max, ALU.add)
                dve.drain()
                V.tensor_scalar(nci[:, :], nci[:, :], S.bit_length() - 1, None, ALU.arith_shift_right)
                dve.drain()
                V.tensor_copy(ncf[:, :], nci[:, :])
                dve.drain()
                V.tensor_tensor_scan(ends[:, :], ones[:, 0:NTP], ncf[:, :], 0.0, ALU.mult, ALU.add)
                dve.drain()
                V.tensor_scalar(tripf[:, :], ends[0:1, NT - 1:NT], float(U - 1), None, ALU.add)
                dve.drain()
                V.tensor_scalar(trips[:, :], tripf[:, :], U.bit_length() - 1, None, ALU.arith_shift_right)
                V.memset(jof[:, :, :], 0.0)
                V.memset(start[:, :, :], 0.0)
                dve.drain()
                for j in range(NT):
                    a, b = j % 2, (j + 1) % 2
                    V.scalar_tensor_tensor(jof[:, b, :], gnum[:, :], ends[:, j:j + 1], jof[:, a, :], ALU.is_ge, ALU.add)
                    V.tensor_scalar(hit[:, :], gnum[:, :], ends[:, j:j + 1], ends[:, j:j + 1], ALU.is_ge, ALU.mult)
                    dve.drain()
                    V.tensor_tensor(start[:, b, :], hit[:, :], start[:, a, :], ALU.max)
                    dve.drain()
                b = NT % 2
                V.tensor_tensor(hit[:, :], gnum[:, :], start[:, b, :], ALU.subtract)
                V.tensor_copy(items[:, :, 0], jof[:, b, :])
                dve.drain()
                V.tensor_scalar(items[:, :, 1], hit[:, :], float(S), None, ALU.mult).then_inc(items_ok, 1)

            @block.tensor
            def _(pe):
                for c in counted:
                    pe.sem_inc(c, 1)
                pe.wait_ge(cst2, 16)
                for w in range(2):
                    PE.matmul(hist[w][:, 0:NT], zerob[:, :], zerob[:, 0:NT], start=True, stop=False)
                    with pe.Fori(0, STEPS) as i:
                        for v in range(2):
                            pe.wait_ge(onehot[v], i + 1 + w * STEPS)
                            for t in range(HALF):
                                last = PE.matmul(hist[w][:, 0:NT], oneL[v][:, t, :], oneH[v][:, t, :],
                                                 start=False, stop=False)
                            last.then_inc(counted[v], 1)
                    last = PE.matmul(hist[w][:, 0:NT], zerob[:, :], zerob[:, 0:NT], start=False, stop=True)
                last.then_inc(hist_done, 1)
                pe.wait_ge(degs, 1)
                PE.matmul(pre[:, 0:NT], strict[:, :], degIn[:, :], start=True, stop=True)
                PE.matmul(pre[:, NT:2 * NT], ones[:, :], degIn[:, :], start=True, stop=True).then_inc(prefix, 1)
                pe.wait_ge(cls_ok, 1)
                for q in range(CL // CLS):
                    if q > 1:
                        pe.wait_ge(cls_use, q - 1)
                    c = flat(in_cls[:, q * CLS:(q + 1) * CLS, :])
                    PE.matmul(cnt[q % 2][0][:, 0:CLS * NT], strictb[:, :], c, start=True, stop=True)
                    PE.matmul(cnt[q % 2][1][:, 0:CLS * NT], onesb[:, :], c, start=True, stop=True).then_inc(cls_cnt, 1)

        def turns(eng):
            return eng.value_load(trips[0:1, 0:1], min_val=1, max_val=GMAX // U - 3)

        with ExitStack() as ph:
            jk = [sb(f"jk{b}", [P, B, 2], i32, ph) for b in range(2)]
            tiles = sb("tiles", [P, NTP], fp32, ph)
            of = [sb(f"of{b}", [P, B, NTP], fp32, ph) for b in range(2)]
            of_start = [sb(f"of_start{b}", [P, B, NTP], fp32, ph) for b in range(2)]
            of_deg = [sb(f"of_deg{b}", [P, B, NTP], fp32, ph) for b in range(2)]
            jf = [sb(f"jf{b}", [P, B], fp32, ph) for b in range(2)]
            info = [sb(f"info{b}", [P, 2, B], fp32, ph) for b in range(2)]
            tiles_ok = sem("tiles_ready")
            kb = [sb(f"kb{b}", [P, B], fp32, ph) for b in range(2)]
            rs = [sb(f"rs{b}", [P, B], fp32, ph) for b in range(2)]
            kk = [sb(f"kk{b}", [P, B, S], fp32, ph) for b in range(2)]
            ee = [sb(f"ee{b}", [P, B, S], fp32, ph) for b in range(2)]
            ok = [sb(f"ok{b}", [P, B, S], fp32, ph) for b in range(2)]
            t1 = [sb(f"t1{b}", [P, B, S], fp32, ph) for b in range(2)]
            t2 = [sb(f"t2{b}", [P, B, S], fp32, ph) for b in range(2)]
            trash = sb("trash", [P, B, S], fp32, ph)
            eq = [sb(f"eq{b}", [P, B * S, T4], fp32, ph) for b in range(2)]
            win = [sb(f"win{b}", [P, B], u32, ph) for b in range(2)]
            we = [sb(f"we{b}", [P, B, 2 * S], i32, ph) for b in range(2)]
            wf = [sb(f"wf{b}", [P, B, 2 * S], fp32, ph) for b in range(2)]
            rec = [sb(f"rec{b}", [P, B, 2 * REC], i32, ph) for b in range(2)]
            recf = [r[:, :, :].bitcast(fp32) for r in rec]
            jj = [sb(f"jj{b}", [P, B], i32, ph) for b in range(2)]
            lift = [sb(f"lift{b}", [P, B], fp32, ph) for b in range(2)]
            jk_in = [sem(f"jk_in{b}") for b in range(2)]
            jk_used = [sem(f"jk_used{b}") for b in range(2)]
            win_ok = [sem(f"window_index_ready{b}") for b in range(2)]
            gate = sem("pool_gate_records")
            gate2 = sem("act_gate_records")
            gate3 = sem("sync_gate_records")
            win_in = [sem(f"windows_in{b}") for b in range(2)]
            rec_ok = [sem(f"record_ready{b}") for b in range(2)]
            rec_out = [sem(f"record_stored{b}") for b in range(2)]
            rec_blank = sem("record_blank")

            block = ph.enter_context(nc.Block())

            def serve(eng, b, gate):
                def fetch(i):
                    eng.wait_ge(jk_used[b], i + 1)
                    eng.dma_start(jk[b][:, :, :], item_d[ds(i * U + b * B, B), :].partition_broadcast(P)
                                  ).then_inc(jk_in[b], 16)

                def store(i):
                    for half, to in enumerate((rec_d, rec0_d)):
                        eng.dma_start(to[ds(i * U + b * B, B), :, :].rearrange("u p w -> p u w"),
                                      rec[b][:, :, half * REC:(half + 1) * REC]).then_inc(rec_out[b], 16)

                n = turns(eng) + 1
                eng.wait_ge(rec_blank, 2)
                store(GMAX // U - 1)
                fetch(0)
                with eng.Fori(0, n) as i:
                    fetch(i + 1)
                    eng.wait_ge(rec_ok[b], i + 1)
                    store(i)
                eng.wait_ge(rec_out[b], n * 32 + 32)
                eng.sem_inc(gate, 1)

            @block.sync
            def _(sp):
                serve(sp, 0, gate3)

            @block.scalar
            def _(act):
                serve(act, 1, gate2)

            @block.gpsimd
            def _(pool):
                G.iota(tiles[:, :], [[1, NTP]], base=0, channel_multiplier=0,
                       allow_small_or_imprecise_dtypes=True).then_inc(tiles_ok, 1)
                n = turns(pool) + 1
                with pool.Fori(0, n) as i:
                    for b in range(2):
                        pool.wait_ge(win_ok[b], i + 1)
                        pool.sem_inc(gate, 1)
                        for u in range(B):
                            G.indirect_dma_start(out=we[b][:, u, :], out_offset=None, in_=windows,
                                                 in_offset=bass.IndirectOffsetOnAxis(ap=win[b][:, u:u + 1], axis=0)
                                                 ).then_inc(win_in[b], 16)

            @block.vector
            def _(dve):
                n = turns(dve) + 1
                V.tensor_scalar(trash[:, :, :].rearrange("p u s -> p (u s)"), place[:, :].to_broadcast([P, B * S]),
                                float(NPAD), None, ALU.add)
                for b in range(2):
                    V.memset(rec[b][:, :, :], 0).then_inc(rec_blank, 1)
                dve.drain()
                for c in jk_used:
                    dve.sem_inc(c, 1)
                def windows_index(i, b):
                    dve.wait_ge(jk_in[b], (i + 1) * 16)
                    V.tensor_copy(kb[b][:, :], jk[b][:, :, 1])
                    V.tensor_copy(jj[b][:, :], jk[b][:, :, 0])
                    V.tensor_copy(jf[b][:, :], jk[b][:, :, 0])
                    V.drain().then_inc(jk_used[b], 1)
                    V.tensor_tensor(of[b][:, :, :], bc(jf[b][:, :], 2, NTP), bc(tiles[:, :], 1, B), ALU.is_equal)
                    dve.drain()
                    V.tensor_tensor(of_start[b][:, :, :], of[b][:, :, :], bc(node_info[:, :, 0], 1, B), ALU.mult)
                    V.tensor_tensor(of_deg[b][:, :, :], of[b][:, :, :], bc(node_info[:, :, 1], 1, B), ALU.mult)
                    dve.drain()
                    V.tensor_reduce(info[b][:, 0, :], of_start[b][:, :, :], AX.X, ALU.add)
                    V.tensor_reduce(info[b][:, 1, :], of_deg[b][:, :, :], AX.X, ALU.add)
                    dve.drain()
                    V.tensor_tensor(rs[b][:, :], info[b][:, 0, :], kb[b][:, :], ALU.add)
                    V.tensor_tensor(kk[b][:, :, :], bc(kb[b][:, :], 2, S), bc(iotaS[:, :], 1, B), ALU.add)
                    V.tensor_scalar(lift[b][:, :], kb[b][:, :], 0.0, -BIG, ALU.is_equal, ALU.mult)
                    dve.drain()
                    V.tensor_scalar(win[b][:, :], rs[b][:, :], float(E), None, ALU.min).then_inc(win_ok[b], 1)
                    V.tensor_tensor(ok[b][:, :, :], kk[b][:, :, :], bc(info[b][:, 1, :], 2, S), ALU.is_lt)
                    dve.drain()

                def record(i, b):
                    dve.wait_ge(rec_out[b], i * 32 + 32)
                    V.tensor_copy(rec[b][:, :, R_J], jj[b][:, :])
                    V.tensor_copy(rec[b][:, :, R_EID], win[b][:, :])
                    V.tensor_copy(recf[b][:, :, R_J + 1], lift[b][:, :])
                    V.tensor_scalar(recf[b][:, :, R_ANY:R_ANY + S], ok[b][:, :, :], 1.0, BIG, ALU.subtract, ALU.mult)
                    dve.drain()
                    dve.wait_ge(win_in[b], (i + 1) * 16 * B)
                    V.tensor_copy(wf[b][:, :, :], we[b][:, :, :])
                    dve.drain()
                    V.tensor_tensor(t1[b][:, :, :], wf[b][:, :, 0:S], ok[b][:, :, :], ALU.mult)
                    V.scalar_tensor_tensor(t2[b][:, :, :], wf[b][:, :, S:2 * S], 1.0, ok[b][:, :, :], ALU.add, ALU.mult)
                    V.tensor_tensor(ee[b][:, :, :], wf[b][:, :, 0:S], trash[:, :, :], ALU.subtract)
                    dve.drain()
                    V.tensor_tensor(ee[b][:, :, :], ee[b][:, :, :], ok[b][:, :, :], ALU.mult)
                    V.tensor_copy(rec[b][:, :, R_SRC:R_SRC + S], t1[b][:, :, :])
                    V.scalar_tensor_tensor(kk[b][:, :, :], t1[b][:, :, :], float(T4), t2[b][:, :, :], ALU.mult, ALU.add)
                    V.tensor_tensor(eq[b][:, :, :], bc(t2[b][:, :, :].rearrange("p u s -> p (u s)"), 2, T4),
                                    bc(iotaT[:, :], 1, B * S), ALU.is_equal)
                    dve.drain()
                    V.tensor_tensor(rec[b][:, :, R_IDX:R_IDX + S], kk[b][:, :, :], ok[b][:, :, :], ALU.subtract)
                    V.tensor_tensor(recf[b][:, :, R_SUM:R_SUM + S], ee[b][:, :, :], trash[:, :, :], ALU.add)
                    V.tensor_scalar(recf[b][:, :, R_TYPE:R_TYPE + S * T4],
                                    eq[b][:, :, :].rearrange("p (u s) t -> p u (s t)", u=B),
                                    1.0, BIG, ALU.subtract, ALU.mult).then_inc(rec_ok[b], 1)

                dve.wait_ge(tiles_ok, 1)
                for b in range(2):
                    windows_index(0, b)
                with dve.Fori(0, n) as i:
                    for b in range(2):
                        record(i, b)
                        windows_index(i + 1, b)

        fresh_semaphores()

        h = sb("h", [P, NTP, D])
        rhs0 = sb("rhs0", [P, T4, A0])
        rhs0i = sb("rhs0i", [P, T4, H * K5])
        rhs1 = sb("rhs1", [P, 3, D + 2 * H])
        soft = sb("soft", [P, K5])
        impt = sb("impt", [P, T4])
        bias = sb("bias", [P, 4, D])
        with ExitStack() as ph:
            wT = sb("wT", [P, T4, D], fp32, ph)
            wsT = sb("wsT", [P, 3, D], fp32, ph)
            wdT = sb("wdT", [P, 3, D], fp32, ph)
            aI = sb("aI", [P, H * K5], fp32, ph)
            aJ = sb("aJ", [P, H * K5], fp32, ph)
            aS = sb("aS", [P, 3, H], fp32, ph)
            aD = sb("aD", [P, 3, H], fp32, ph)
            pk = sb("pk", [P, K5], fp32, ph)
            sm = sb("sm", [P, 2], fp32, ph)
            wps = pb("wps", [P, 512], fp32, ph)
            w_in = sem("weights_in")
            probs_in = sem("probs_in")
            wp = sem("score_weights_done")
            mx = sem("probs_max_ready")
            ex = sem("probs_exp_ready")

            block = ph.enter_context(nc.Block())

            @block.sync
            def _(sp):
                sp.dma_start(pk[:, :], probs.partition_broadcast(P)).then_inc(probs_in, 16)
                for to, frm in ((wT[:, :, :], W0T), (wsT[:, :, :], WsT), (wdT[:, :, :], WdT),
                                (aI[:, :], attI), (aJ[:, :], attJ), (aS[:, :, :], attS), (aD[:, :, :], attD),
                                (rhs0[:, :, 0:D], W0), (rhs1[:, :, 0:D], Ws),
                                (impt[:, :], importance.partition_broadcast(P)),
                                (bias[:, 0, :], bias0.partition_broadcast(P)),
                                (bias[:, 1:4, :], bias1.partition_broadcast(P))):
                    sp.dma_start(to, frm).then_inc(w_in, 16)
                sp.wait_ge(w_in, 16 * 12)

            @block.tensor
            def _(pe):
                pe.wait_ge(w_in, 16 * 12)
                for t in range(T4):
                    PE.matmul(wps[:, t * 40:t * 40 + 20], wT[:, t, :], aJ[:, :], start=True, stop=True)
                    PE.matmul(wps[:, t * 40 + 20:t * 40 + 40], wT[:, t, :], aI[:, :], start=True, stop=True)
                for l in range(3):
                    PE.matmul(wps[:, 160 + 8 * l:164 + 8 * l], wsT[:, l, :], aS[:, l, :], start=True, stop=True)
                    last = PE.matmul(wps[:, 164 + 8 * l:168 + 8 * l], wdT[:, l, :], aD[:, l, :], start=True, stop=True)
                last.then_inc(wp, 1)

            @block.scalar
            def _(act):
                act.wait_ge(mx, 1)
                A.activation(soft[:, :], pk[:, :], ACT.Exp).then_inc(ex, 1)

            @block.vector
            def _(dve):
                dve.wait_ge(probs_in, 16)
                V.tensor_reduce(sm[:, 0:1], pk[:, :], AX.X, ALU.max)
                dve.drain()
                V.tensor_scalar(pk[:, :], pk[:, :], sm[:, 0:1], None, ALU.subtract).then_inc(mx, 1)
                dve.wait_ge(ex, 1)
                V.tensor_reduce(sm[:, 0:1], soft[:, :], AX.X, ALU.add)
                dve.drain()
                V.reciprocal(sm[:, 1:2], sm[:, 0:1])
                dve.drain()
                V.tensor_scalar(soft[:, :], soft[:, :], sm[:, 1:2], None, ALU.mult)
                dve.wait_ge(wp, 1)
                v = wps[:, 0:160].rearrange("p (t w) -> p t w", t=T4)
                V.tensor_copy(rhs0[:, :, D:A0], v[:, :, 0:20])
                V.tensor_copy(rhs0i[:, :, :], v[:, :, 20:40])
                V.tensor_copy(rhs1[:, :, D:D + 2 * H], wps[:, 160:184].rearrange("p (l w) -> p l w", l=3))

        def node_table(tag, frm, rhs, pieces, stage, table, source=None):
            with ExitStack() as ph:
                ht = [sb(f"ht_{tag}{v}", [P, P], fp32, ph) for v in range(2)]
                hc = [sb(f"hc_{tag}{v}", [P, P], fp32, ph) for v in range(2)]
                tps = [pb(f"tps_{tag}{v}", [P, 512], fp32, ph) for v in range(2)]
                banks = max(p[0] for p in pieces) + 1
                mps = [[pb(f"mps_{tag}{v}{b}", [P, 512], fp32, ph) for b in range(banks)] for v in range(2)]
                fetched = sem(f"tile_copied_{tag}")
                turned = sem(f"tile_transposed_{tag}")
                stored = sem(f"transpose_stored_{tag}")
                mult = sem(f"tile_multiplied_{tag}")
                staged = sem(f"tile_staged_{tag}")
                rows_out = sem(f"rows_out_{tag}")
                groups = 5 if source is not None else 1
                TG = NTP // groups
                rows_in = [sem(f"rows_in_{tag}{q}") for q in range(groups)]
                block = ph.enter_context(nc.Block())

                @block.scalar
                def _(act):
                    for c in (stored,):
                        act.sem_inc(c, 1)
                    for q in range(groups):
                        if source is not None:
                            act.wait_ge(rows_in[q], TG * 16)
                        with act.Fori(q * TG // 2, (q + 1) * TG // 2) as i:
                            for v in range(2):
                                act.wait_ge(turned, (i * 2 + v - 1 if v else i * 2) + 1)
                                A.activation(hc[v][:, :], frm[:, ds(i * 2 + v, 1), :].rearrange("p a c -> p (a c)"),
                                             ACT.Copy).then_inc(fetched, 1)
                            for v in range(2):
                                act.wait_ge(turned, i * 2 + v + 2)
                                act.wait_ge(mult, i * 2 + 1)
                                A.activation(ht[v][:, :], tps[v][:, 0:P], ACT.Copy).then_inc(stored, 1)

                @block.tensor
                def _(pe):
                    for c in (turned, mult):
                        pe.sem_inc(c, 1)
                    with pe.Fori(0, NTP // 2) as i:
                        for v in range(2):
                            pe.wait_ge(fetched, i * 2 + v + 1)
                            pe.wait_ge(stored, i * 2 + 1)
                            PE.transpose(tps[v][:, 0:P], hc[v][:, :], ident[:, :]).then_inc(turned, 1)
                        for v in range(2):
                            pe.wait_ge(stored, i * 2 + v + 2)
                            pe.wait_ge(staged, i * 2 + 1)
                            for b, a, z, op, _ in pieces:
                                last = PE.matmul(mps[v][b][:, a:z], ht[v][:, :], op, start=True, stop=True)
                            last.then_inc(mult, 1)

                @block.vector
                def _(dve):
                    for c in (staged,):
                        dve.sem_inc(c, 1)
                    with dve.Fori(0, NTP // 2) as i:
                        for v in range(2):
                            dve.wait_ge(mult, i * 2 + v + 2)
                            for b, a, z, _, to in pieces:
                                for lo_, hi_, dest in to:
                                    last = V.tensor_copy(dest(i * 2 + v), mps[v][b][:, lo_:hi_])
                            last.then_inc(staged, 1)

                @block.gpsimd
                def _(pool):
                    if source is not None:
                        for j in range(NTP):
                            G.indirect_dma_start(out=frm[:, j, :], out_offset=None, in_=source,
                                                 in_offset=bass.IndirectOffsetOnAxis(
                                                     ap=nid[:, j:j + 1].bitcast(u32), axis=0)).then_inc(rows_in[j // TG], 16)
                    for j in range(NTP):
                        pool.wait_ge(staged, j + 2)
                        G.indirect_dma_start(out=table, out_offset=bass.IndirectOffsetOnAxis(
                            ap=nid[:, j:j + 1].bitcast(u32), axis=0), in_=stage[:, j, :], in_offset=None
                        ).then_inc(rows_out, 16)
                    pool.wait_ge(rows_out, 16 * NTP)

        def attention(tag, T, table, own, acc, g, prod, zt):
            L = T * H
            ZW = H * K5 if T > 1 else H
            OW = T * ZW
            with ExitStack() as ph:
                rec = [sb(f"rec_{tag}{b}", [P, B, REC], i32, ph) for b in range(2)]
                if T > 1:
                    idx = [sb(f"idx_{tag}{b}", [P, B, S], i32, ph) for b in range(2)]
                    mask = [sb(f"mask_{tag}{b}", [P, B * S, T], fp32, ph) for b in range(2)]
                    al = sb(f"al_{tag}", [P, B * S, H], fp32, ph)
                ob = [sb(f"own_{tag}{b}", [P, B, OW], fp32, ph) for b in range(2)]
                tile = [sb(f"tile_{tag}{b}", [1, B + 1], i32, ph) for b in range(2)]
                z = sb(f"z_{tag}", [P, B, S, ZW], fp32, ph)
                sc = [sb(f"sc_{tag}{b}", [P, B, S, L], fp32, ph) for b in range(2)]
                lift = sb(f"lift_{tag}", [P, L, B + 1], fp32, ph)
                item_max = sb(f"item_max_{tag}", [P, L, B + 1], fp32, ph)
                run_max = sb(f"run_max_{tag}", [P, L, B + 1], fp32, ph)
                shrink_arg = sb(f"shrink_arg_{tag}", [P, 2, L, B + 1], fp32, ph)
                shrink = [sb(f"shrink_{tag}{b}", [P, 2, L, B + 1], fp32, ph) for b in range(2)]
                item_z = sb(f"item_z_{tag}", [P, L, B + 1], fp32, ph)
                run_z = [sb(f"run_z_{tag}{b}", [P, L, B + 1], fp32, ph) for b in range(2)]
                PROD = (0, 1, 2, 1)
                prod = [*prod, sb(f"prod_{tag}", [P, S, T * D], fp32, ph)]
                carry = [sb(f"carry_{tag}{u}", [P, T * D], fp32, ph) for u in range(2)]
                sums = [[pb(f"sums_{tag}{b}{u}", [P, 512], fp32, ph) for u in range(B)] for b in range(2)]
                rec_in = [sem(f"rec_in_{tag}{b}") for b in range(2)]
                own_in = [sem(f"own_in_{tag}{b}") for b in range(2)]
                rec_read = [sem(f"rec_read_by_vector_{tag}{b}") for b in range(2)]
                gathered = [sem(f"gathered_{tag}{b}") for b in range(2)]
                gate_p, gate_s, gate_a = sem(f"gate_pool_{tag}"), sem(f"gate_sync_{tag}"), sem(f"gate_act_{tag}")
                scored = sem(f"scores_ready_{tag}")
                weighed = sem(f"weights_ready_{tag}")
                shr_arg = sem(f"shrink_arguments_{tag}")
                shr_ok = sem(f"shrink_ready_{tag}")
                prods = sem(f"products_ready_{tag}")
                summed = sem(f"products_summed_{tag}")
                carried = sem(f"sum_before_shrunk_{tag}")
                z_ok = sem(f"exponential_sums_ready_{tag}")
                tiles_read = sem(f"tiles_read_{tag}")
                kept = sem(f"sums_kept_{tag}")
                NREC = 3 if T > 1 else 1
                ahead = T > 1
                block = ph.enter_context(nc.Block())

                @block.sync
                def _(sp):
                    def fetch(i, b):
                        g0 = i * U + b * B
                        sp.wait_ge(rec_read[b], i + 1)
                        sp.dma_start(rec[b][:, :, :], rec_d[ds(g0, B), :, :].rearrange("u p w -> p u w")
                                     ).then_inc(rec_in[b], 16)
                        if T > 1:
                            sp.dma_start(idx[b][:, :, :], rec0_d[ds(g0, B), :, 0:S].rearrange("u p w -> p u w")
                                         ).then_inc(rec_in[b], 16)
                            sp.dma_start(mask[b][:, :, :].rearrange("p (u s) t -> p u (s t)", u=B),
                                         rec0_d[ds(g0, B), :, S:S + S * T].rearrange("u p w -> p u w").bitcast(fp32)
                                         ).then_inc(rec_in[b], 16)
                        sp.wait_ge(rec_in[b], (i + 1) * 16 * NREC)
                        sp.sem_inc(gate_s, 1)
                        for u in range(B):
                            j = sp.value_load(rec[b][0:1, u, R_J:R_J + 1], min_val=0, max_val=NT)
                            sp.dma_start(ob[b][:, u, :], own[:, ds(j, 1), :].rearrange("p a w -> p (a w)")
                                         ).then_inc(own_in[b], 16)

                    n = turns(sp)
                    with sp.Fori(0, n) as i:
                        for b in range(2):
                            fetch(i, b)
                    if ahead:
                        fetch(n, 0)

                @block.gpsimd
                def _(pool):
                    def gather(i, b):
                        pool.wait_ge(rec_in[b], (i + 1) * 16 * NREC)
                        for u in range(B):
                            pool.wait_ge(prods, (i * 2 + b) * B + u + 1)
                            pool.sem_inc(gate_p, 1)
                            for s in range(S):
                                at = (idx[b][:, u, s:s + 1] if T > 1 else
                                      rec[b][:, u, R_SRC + s:R_SRC + s + 1]).bitcast(u32)
                                G.indirect_dma_start(out=g[b][:, u, s, :], out_offset=None, in_=table,
                                                     in_offset=bass.IndirectOffsetOnAxis(ap=at, axis=0)
                                                     ).then_inc(gathered[b], 16)

                    n = turns(pool)
                    with pool.Fori(0, n) as i:
                        for b in range(2):
                            gather(i, b)
                    if ahead:
                        gather(n, 0)

                @block.scalar
                def _(act):
                    def exps(k, b):
                        act.wait_ge(scored, k + 1)
                        A.activation(sc[b][:, :, :, :], sc[b][:, :, :, :], ACT.Exp).then_inc(weighed, 1)
                        act.wait_ge(shr_arg, k + 1)
                        A.activation(shrink[b][:, :, :, :], shrink_arg[:, :, :, :], ACT.Exp).then_inc(shr_ok, 1)

                    def keep(j, z, total):
                        to = acc[:, ds(j, 1), :].rearrange("p a (l c) -> p (a l) c", c=C + 1)
                        A.activation(to[:, :, C], z, ACT.Copy)
                        A.activation(to[:, :, 0:C], total[:, 0:T * D].rearrange("p (l c) -> p l c", c=C),
                                     ACT.Copy).then_inc(kept, 1)

                    act.sem_inc(kept, 2 * B)
                    act.sem_inc(tiles_read, 2)
                    act.sem_inc(shr_ok, 1)
                    n = turns(act)
                    if ahead:
                        exps(0, 0)
                    with act.Fori(0, n) as i:
                        for b in range(2):
                            k = i * 2 + b
                            if ahead:
                                exps(k + 1, 1 - b)
                            else:
                                exps(k, b)
                            js = [act.value_load(tile[b][0:1, u:u + 1], min_val=0, max_val=NT) for u in range(B)]
                            A.drain().then_inc(tiles_read, 1)
                            act.wait_ge(z_ok, k + 1)
                            for u in range(B):
                                act.wait_ge(carried, k * B + u + 1)
                                act.wait_ge(kept, k * B + u + 2 * B)
                                keep(js[u], run_z[b][:, :, u], sums[b][u - 1] if u else sums[1 - b][B - 1])
                    j = act.value_load(tile[1][0:1, B:B + 1], min_val=0, max_val=NT)
                    act.wait_ge(summed, n * U + 4)
                    act.wait_ge(kept, n * U + 2 * B)
                    keep(j, run_z[1][:, :, B], sums[1][B - 1])

                @block.tensor
                def _(pe):
                    pe.sem_inc(summed, 4)
                    n = turns(pe)
                    with pe.Fori(0, n) as i:
                        for b in range(2):
                            for u in range(B):
                                pe.wait_ge(prods, (i * 2 + b) * B + u + 1 + 2 * B)
                                pe.wait_ge(kept, (i * 2 + b) * B + u + 2)
                                for s in range(S):
                                    PE.matmul(sums[b][u][:, 0:T * D], ident[:, :], prod[PROD[u]][:, s, :],
                                              start=(s == 0), stop=False)
                                pe.wait_ge(carried, (i * 2 + b) * B + u + 1)
                                PE.matmul(sums[b][u][:, 0:T * D], ident[:, :], carry[u % 2][:, :],
                                          start=False, stop=True).then_inc(summed, 1)

                @block.vector
                def _(dve):
                    def scores(i, b):
                        dve.wait_ge(own_in[b], (i + 1) * 16 * B)
                        V.tensor_copy(item_max[:, :, 0:1], run_max[:, :, B:B + 1])
                        V.tensor_copy(lift[:, :, 1:B + 1],
                                      bc(rec[b][:, :, R_J + 1].bitcast(fp32), 1, L))
                        if T > 1:
                            for u in range(B):
                                V.tensor_tensor(zt[:, u, :, :].rearrange("p s (t w) -> p s t w", t=T),
                                                bc(ob[b][:, u, :].rearrange("p (t w) -> p t w", t=T), 1, S),
                                                bc(mask[b][:, u * S:(u + 1) * S, :], 3, ZW), ALU.add)
                            dve.drain()
                            V.tensor_reduce(z[:, :, :, :].rearrange("p u s w -> p (u s) w"),
                                            zt[:, :, :, :].rearrange("p u s (t w) -> p (u s) w t", t=T), AX.X, ALU.max)
                            dve.drain()
                        dve.wait_ge(gathered[b], (i + 1) * 16 * S * B)
                        if T > 1:
                            V.tensor_tensor(z[:, :, :, :], z[:, :, :, :], g[b][:, :, :, D:D + ZW], ALU.add)
                        else:
                            V.tensor_tensor(z[:, :, :, :], bc(ob[b][:, :, :], 2, S), g[b][:, :, :, D:D + ZW], ALU.add)
                        dve.drain()
                        zf = z[:, :, :, :].rearrange("p u s w -> p (u s w)")
                        V.scalar_tensor_tensor(zf, zf, 0.2, zf, ALU.mult, ALU.max)
                        dve.drain()
                        if T > 1:
                            zz = zf.rearrange("p (a k) -> p a k", k=K5)
                            V.tensor_tensor(zz, zz, bc(soft[:, :], 1, B * S * H), ALU.mult)
                            dve.drain()
                            V.tensor_reduce(al[:, :, :].rearrange("p a h -> p (a h)"), zz, AX.X, ALU.add)
                            dve.drain()
                            V.tensor_tensor(sc[b][:, :, :, :].rearrange("p u s (t h) -> p (u s) t h", t=T),
                                            bc(al[:, :, :], 2, T), bc(mask[b][:, :, :], 3, H), ALU.add)
                        else:
                            V.tensor_tensor(sc[b][:, :, :, :], z[:, :, :, :],
                                            bc(rec[b][:, :, R_ANY:R_ANY + S].bitcast(fp32), 3, H), ALU.add)
                        dve.drain()
                        im = item_max[:, :, 1:B + 1].rearrange("p l u -> p u l")
                        V.tensor_reduce(im, sc[b][:, :, :, :].rearrange("p u s l -> p u l s"), AX.X, ALU.max)
                        dve.wait_ge(tiles_read, i * 2 + b + 1)
                        V.tensor_copy(tile[b][:, 0:1], tile[1 - b][:, B:B + 1])
                        V.tensor_copy(tile[b][:, 1:B + 1], rec[b][0:1, :, R_J])
                        V.drain().then_inc(rec_read[b], 1)
                        V.tensor_scalar(im, im, LOW, None, ALU.max)
                        dve.drain()
                        V.tensor_tensor(sc[b][:, :, :, :], sc[b][:, :, :, :], bc(im, 2, S),
                                        ALU.subtract).then_inc(scored, 1)

                    def maxima(k, b):
                        V.tensor_tensor_scan(run_max[:, :, :].rearrange("p l u -> p (l u)"),
                                             lift[:, :, :].rearrange("p l u -> p (l u)"),
                                             item_max[:, :, :].rearrange("p l u -> p (l u)"), 0.0, ALU.add, ALU.max)
                        dve.drain()
                        dve.wait_ge(shr_ok, k + 1)
                        V.tensor_tensor(shrink_arg[:, 1, :, 1:B + 1], item_max[:, :, 1:B + 1], run_max[:, :, 1:B + 1],
                                        ALU.subtract)
                        V.tensor_tensor(shrink_arg[:, 0, :, 1:B + 1], run_max[:, :, 0:B], lift[:, :, 1:B + 1], ALU.add)
                        dve.drain()
                        V.tensor_tensor(shrink_arg[:, 0, :, 1:B + 1], shrink_arg[:, 0, :, 1:B + 1],
                                        run_max[:, :, 1:B + 1], ALU.subtract).then_inc(shr_arg, 1)

                    def weigh(k, b, u):
                        dve.wait_ge(summed, k * B + u + 1 + (2 if u % 2 else 0))
                        w = sc[b][:, u, :, :]
                        if T > 1:
                            for s in range(S):
                                last = V.tensor_tensor(
                                    prod[PROD[u]][:, s, :].rearrange("p (t h c) -> p t h c", t=T, h=H),
                                    bc(w[:, s, :].rearrange("p (t h) -> p t h", t=T), 3, C),
                                    bc(g[b][:, u, s, 0:D].rearrange("p (h c) -> p h c", h=H), 1, T), ALU.mult)
                        else:
                            last = V.tensor_tensor(prod[PROD[u]][:, :, :].rearrange("p s (h c) -> p s h c", h=H),
                                                   bc(w, 3, C),
                                                   g[b][:, u, :, 0:D].rearrange("p s (h c) -> p s h c", h=H), ALU.mult)
                        last.then_inc(prods, 1)

                    def carry_on(k, b, u):
                        dve.wait_ge(summed, k * B + u + 4)
                        before = sums[b][u - 1] if u else sums[1 - b][B - 1]
                        V.tensor_tensor(carry[u % 2][:, :].rearrange("p (l c) -> p l c", c=C),
                                        before[:, 0:T * D].rearrange("p (l c) -> p l c", c=C),
                                        bc(shrink[b][:, 0, :, u + 1], 2, C), ALU.mult).then_inc(carried, 1)

                    def weights(k, b):
                        dve.wait_ge(weighed, k + 1)
                        dve.wait_ge(shr_ok, k + 2)
                        dve.wait_ge(kept, k * B + B)
                        V.tensor_tensor(sc[b][:, :, :, :], sc[b][:, :, :, :],
                                        bc(shrink[b][:, 1, :, 1:B + 1].rearrange("p l u -> p u l"), 2, S), ALU.mult)
                        V.tensor_copy(item_z[:, :, 0:1], run_z[1 - b][:, :, B:B + 1])
                        dve.drain()
                        V.tensor_reduce(item_z[:, :, 1:B + 1].rearrange("p l u -> p u l"),
                                        sc[b][:, :, :, :].rearrange("p u s l -> p u l s"), AX.X, ALU.add)
                        dve.drain()
                        V.tensor_tensor_scan(run_z[b][:, :, :].rearrange("p l u -> p (l u)"),
                                             shrink[b][:, 0, :, :].rearrange("p l u -> p (l u)"),
                                             item_z[:, :, :].rearrange("p l u -> p (l u)"), 0.0, ALU.mult, ALU.add
                                             ).then_inc(z_ok, 1)

                    for c in rec_read:
                        dve.sem_inc(c, 1)
                    dve.sem_inc(prods, 2 * B)
                    n = turns(dve)
                    V.memset(run_max[:, :, :], LOW)
                    V.memset(lift[:, :, :], -BIG)
                    V.memset(shrink_arg[:, :, :, :], LOW)
                    V.memset(tile[1][:, :], NT)
                    V.memset(run_z[1][:, :, :], 0.0)
                    V.memset(sums[1][B - 1][:, :], 0.0)
                    dve.drain()
                    if ahead:
                        scores(0, 0)
                        maxima(0, 0)
                    with dve.Fori(0, n) as i:
                        for b in range(2):
                            k = i * 2 + b
                            if not ahead:
                                scores(i, b)
                                maxima(k, b)
                            weights(k, b)
                            weigh(k, b, 0)
                            carry_on(k, b, 0)
                            weigh(k, b, 1)
                            weigh(k, b, 2)
                            carry_on(k, b, 1)
                            if ahead:
                                scores(i + b, 1 - b)
                            carry_on(k, b, 2)
                            weigh(k, b, 3)
                            if ahead:
                                maxima(k + 1, 1 - b)
                            carry_on(k, b, 3)

        def normalised(v, t, mean, var, tag):
            half = sem(f"variance_{tag}")
            root = sem(f"root_{tag}")

            def vector(dve):
                V.tensor_reduce(mean, v, AX.X, ALU.add)
                dve.drain()
                V.tensor_scalar(mean, mean, 1.0 / D, None, ALU.mult)
                dve.drain()
                V.tensor_tensor(v, v, bc(mean, 2, D), ALU.subtract)
                dve.drain()
                V.tensor_tensor(t, v, v, ALU.mult)
                dve.drain()
                V.tensor_reduce(var, t, AX.X, ALU.add)
                dve.drain()
                V.tensor_scalar(var, var, 1.0 / D, 1e-5, ALU.mult, ALU.add).then_inc(half, 1)
                dve.wait_ge(root, 1)
                V.reciprocal(var, var)
                dve.drain()
                V.tensor_tensor(v, v, bc(var, 2, D), ALU.mult)
                dve.drain()

            def scalar(act):
                act.wait_ge(half, 1)
                A.activation(var, var, ACT.Sqrt).then_inc(root, 1)
            return vector, scalar

        with ExitStack() as att:
            SUMS0 = NTP * T4 * H * (C + 1)
            ROOM0 = NTP * T4 * A0
            big = sb("big", [P, max(ROOM0, SUMS0 + U * S * A0)], fp32, att)
            own1 = sb("own_layer1", [P, NTP, H], fp32, att)
            mean = sb("mean", [P, NTP], fp32, att)
            var = sb("var", [P, NTP], fp32, att)
            W2 = 2 * A0
            stage0 = big[:, 0:ROOM0].rearrange("p (j w) -> p j w", j=NTP)

            def room(at, *shape):
                size = 1
                for k in shape:
                    size *= k
                names = "abcd"[:len(shape)]
                v = big[:, at:at + size].rearrange(f"p ({' '.join(names)}) -> p {' '.join(names)}",
                                                   **dict(zip(names, shape)))
                return v, at + size

            def scratch(T):
                hf = flat(h[:, :, :])
                n = S * T * D
                prod = [hf[:, v * n:(v + 1) * n].rearrange("p (s w) -> p s w", s=S) for v in range(2)]
                zt = hf[:, 2 * n:2 * n + B * S * T4 * H * K5].rearrange(
                    "p (u s w) -> p u s w", u=B, s=S) if T > 1 else None
                return prod, zt

            def at0(a, z):
                return lambda t: flat(stage0[:, ds(t, 1), a:z])

            r0 = flat(rhs0[:, :, :])
            own0 = flat(h[:, :, :])[:, 0:NTP * T4 * H * K5].rearrange("p (j w) -> p j w", j=NTP)
            node_table("L0", xr, rhs0,
                       [(0, 0, W2, r0[:, 0:W2], [(0, W2, at0(0, W2))]),
                        (1, 0, W2, r0[:, W2:2 * W2], [(0, W2, at0(W2, 2 * W2))]),
                        (2, 0, T4 * 20, flat(rhs0i[:, :, :]),
                         [(0, T4 * 20, lambda t: flat(own0[:, ds(t, 1), :]))])],
                       stage0, tab0_d, source=x)
            own_out = sem("own_parts_stored")
            with nc.Block() as block:
                @block.sync
                def _(sp):
                    sp.dma_start(own0_d, own0).then_inc(own_out, 16)
                    sp.wait_ge(own_out, 16)

                @block.vector
                def _(dve):
                    V.tensor_tensor(xr[:, :, :], xr[:, :, :], bc(bias[:, 0, :], 1, NTP), ALU.add)
                    dve.drain()
                    V.tensor_tensor(xr[:, :, :], xr[:, :, :], stage0[:, :, 0:D], ALU.add)
            L0 = T4 * H
            acc0, at = room(0, NTP, L0 * (C + 1))
            g0 = []
            for b in range(2):
                v, at = room(at, B, S, A0)
                g0.append(v)
            attention("L0", T4, tab0_d.rearrange("n (t w) -> (n t) w", t=T4), own0_d, acc0, g0, *scratch(T4))
            ln_v, ln_s = normalised(xr[:, :, :], h[:, :, :], mean[:, :], var[:, :], "L0")
            with nc.Block() as block:
                @block.vector
                def _(dve):
                    a = acc0[:, 0:NT, :].rearrange("p j (l c) -> p j l c", c=C + 1)
                    srun = big[:, SUMS0:SUMS0 + NT * L0].rearrange("p (j l) -> p j l", j=NT)
                    V.tensor_scalar(srun, a[:, :, :, C], 1e-30, None, ALU.max)
                    dve.drain()
                    V.reciprocal(srun, srun)
                    dve.drain()
                    for t in range(T4):
                        V.tensor_scalar(srun[:, :, t * H:(t + 1) * H], srun[:, :, t * H:(t + 1) * H],
                                        impt[:, t:t + 1], None, ALU.mult)
                    dve.drain()
                    for t in range(T4):
                        V.tensor_tensor(h[:, 0:NT, :].rearrange("p j (h c) -> p j h c", h=H),
                                        a[:, :, t * H:(t + 1) * H, 0:C],
                                        bc(srun[:, :, t * H:(t + 1) * H], 3, C), ALU.mult)
                        dve.drain()
                        V.tensor_tensor(xr[:, 0:NT, :], xr[:, 0:NT, :], h[:, 0:NT, :], ALU.add)
                        dve.drain()
                    ln_v(dve)
                    V.tensor_copy(h[:, :, :], xr[:, :, :])

                @block.scalar
                def _(act):
                    ln_s(act)

            fresh_semaphores()
            stage1, at = room(0, NTP, A1)
            acc1, at = room(at, NTP, H * (C + 1))
            g1 = []
            for b in range(2):
                v, at = room(at, B, S, A1)
                g1.append(v)
            s1, at = room(at, NT, H)
            for l in range(3):
                node_table(f"L1{l}", h, rhs1,
                           [(0, 0, D + 2 * H, rhs1[:, l, :],
                             [(0, A1, lambda t: flat(stage1[:, ds(t, 1), :])),
                              (A1, A1 + H, lambda t: flat(own1[:, ds(t, 1), :]))])],
                           stage1, tab1_d[l])
                attention(f"L1{l}", 1, tab1_d[l], own1, acc1, g1, *scratch(1))
                if l == 2:
                    ln_v, ln_s = normalised(xr[:, :, :], h[:, :, :], mean[:, :], var[:, :], "L1")
                with nc.Block() as block:
                    @block.vector
                    def _(dve):
                        a = acc1[:, 0:NT, :].rearrange("p j (l c) -> p j l c", c=C + 1)
                        V.tensor_scalar(s1, a[:, :, :, C], 1e-16, None, ALU.add)
                        dve.drain()
                        V.reciprocal(s1, s1)
                        dve.drain()
                        V.tensor_tensor(h[:, 0:NT, :].rearrange("p j (h c) -> p j h c", h=H),
                                        a[:, :, :, 0:C], bc(s1, 3, C), ALU.mult)
                        V.memset(h[:, NT:NTP, :], 0.0)
                        dve.drain()
                        V.tensor_tensor(h[:, :, :], h[:, :, :], bc(bias[:, l + 1, :], 1, NTP), ALU.add)
                        dve.drain()
                        if l < 2:
                            V.tensor_scalar(h[:, :, :], h[:, :, :], 0.0, None, ALU.max)
                        else:
                            V.tensor_tensor(xr[:, :, :], xr[:, :, :], h[:, :, :], ALU.add)
                            dve.drain()
                            ln_v(dve)

                    if l == 2:
                        @block.scalar
                        def _(act):
                            ln_s(act)
                fresh_semaphores()

        with ExitStack() as mlp:
            big = sb("big2", [P, NTP * HID], fp32, mlp)
            w1 = sb("w1", [P, 2, HID], fp32, mlp)
            w2 = sb("w2", [P, 2, HID], fp32, mlp)
            w3 = sb("w3", [P, 2, HID], fp32, mlp)
            w4 = sb("w4", [P, 3, HID], fp32, mlp)
            w5 = sb("w5", [P, 2, D], fp32, mlp)
            ba = sb("ba", [P, 2], fp32, mlp)
            bb = sb("bb", [P, 2], fp32, mlp)
            bcr = sb("bcr", [P, HID], fp32, mlp)
            b4 = sb("b4", [P, HID], fp32, mlp)
            b5 = sb("b5", [P, D], fp32, mlp)
            wm_in = sem("mlp_weights_in")
            with nc.Block() as block:
                @block.sync
                def _(sp):
                    for to, frm in ((w1[:, :, :], w1a), (w2[:, :, :], w1b), (w3[:, :, :], w1c), (w4[:, :, :], w2a),
                                    (w5[:, :, :], w2b), (ba[:, :], b1a), (bb[:, :], b1b),
                                    (bcr[:, :], b1c.partition_broadcast(P)), (b4[:, :], b2a.partition_broadcast(P)),
                                    (b5[:, :], b2b.partition_broadcast(P))):
                        sp.dma_start(to, frm).then_inc(wm_in, 16)
                    sp.wait_ge(wm_in, 160)
            stage2 = big[:, :].rearrange("p (j w) -> p j w", j=NTP)
            node_table("L2", xr, w1,
                       [(0, 0, HID, w1[:, 0, :], [(0, HID, lambda t: flat(stage2[:, ds(t, 1), :]))])],
                       stage2, tab2_d)

            with ExitStack() as ph:
                total = big[:, :].rearrange("p (j f n) -> p j f n", j=NTP, f=2)
                rec = [sb(f"rec_m{u}", [P, REC], i32, ph) for u in range(U)]
                gx = [sb(f"gx{u}", [P, S, HID], fp32, ph) for u in range(U)]
                ge = [sb(f"ge{u}", [P, S, D], fp32, ph) for u in range(U)]
                off = [sb(f"off{v}", [P, S], bf16, ph) for v in range(2)]
                eT = [sb(f"eT{v}", [P, S * P], fp32, ph) for v in range(2)]
                h0 = [sb(f"h0_{f}", [P, S * P], fp32, ph) for f in range(2)]
                h1 = [[sb(f"h1_{v}{f}", [P, S * P], fp32, ph) for f in range(2)] for v in range(2)]
                h2 = [sb(f"h2_{f}", [P, S, P], fp32, ph) for f in range(2)]
                part = [sb(f"partial{f}", [P, P], fp32, ph) for f in range(2)]
                psE = [pb(f"psE{v}", [P, 512], fp32, ph) for v in range(2)]
                psX = [pb(f"psX{f}", [P, 512], fp32, ph) for f in range(2)]
                ps1 = [pb(f"ps1_{f}", [P, 512], fp32, ph) for f in range(2)]
                ps2 = [pb(f"ps2_{f}", [P, 512], fp32, ph) for f in range(2)]
                rec_in = [sem(f"rec_in_m{u}") for u in range(U)]
                rec_free = [sem(f"rec_free_m{u}") for u in range(U)]
                gathered = [sem(f"gathered_m{u}") for u in range(U)]
                gate = sem("gate_m")
                gate_v = sem("gate_mv")
                masks = sem("masks_ready_m")
                turned = sem("edges_transposed_m")
                turned_x = sem("sources_transposed_m")
                eT_ok = sem("edges_stored_m")
                lin1 = sem("hidden1_edge_part_m")
                both1 = sem("hidden1_linear_m")
                act1 = sem("hidden1_ready_m")
                lin2 = sem("hidden2_linear_m")
                act2 = sem("hidden2_ready_m")
                summed = sem("hidden2_summed_m")
                block = ph.enter_context(nc.Block())

                def following(i, u):
                    return (i, u + 1) if u < U - 1 else (i + 1, 0)

                @block.sync
                def _(sp):
                    def fetch(i, u):
                        sp.wait_ge(rec_free[u], i + 1)
                        sp.dma_start(rec[u][:, :], rec_d[ds(i * U + u, 1), :, :]
                                     .rearrange("a p w -> (a p) w")).then_inc(rec_in[u], 16)

                    n = turns(sp)
                    with sp.Fori(0, n) as i:
                        for u in range(U):
                            fetch(i, u)
                    fetch(n, 0)

                @block.gpsimd
                def _(pool):
                    def gather(i, u):
                        pool.wait_ge(rec_in[u], (i + 1) * 16)
                        pool.wait_ge(turned_x, (i * U + u) * 2 + 2)
                        pool.sem_inc(gate, 1)
                        G.indirect_dma_start(out=ge[u][:, :, :].rearrange("p s c -> p (s c)"), out_offset=None,
                                             in_=edge_windows, in_offset=bass.IndirectOffsetOnAxis(
                                                 ap=rec[u][:, R_EID:R_EID + 1].bitcast(u32), axis=0)
                                             ).then_inc(gathered[u], 16)
                        for s in range(S):
                            G.indirect_dma_start(out=gx[u][:, s, :], out_offset=None, in_=tab2_d,
                                                 in_offset=bass.IndirectOffsetOnAxis(
                                                     ap=rec[u][:, R_SRC + s:R_SRC + s + 1].bitcast(u32), axis=0)
                                                 ).then_inc(gathered[u], 16)

                    n = turns(pool)
                    with pool.Fori(0, n) as i:
                        for u in range(U):
                            gather(i, u)
                    gather(n, 0)

                @block.tensor
                def _(pe):
                    def turn_over(i, u):
                        g = i * U + u
                        pe.wait_ge(gathered[u], (i + 1) * 16 * (S + 1))
                        pe.wait_ge(eT_ok, g + 1)
                        for s in range(S):
                            last = PE.transpose(psE[u % 2][:, s * P:(s + 1) * P], ge[u][:, s, :], ident[:, :])
                        last.then_inc(turned, 1)
                        pe.wait_ge(both1, g * 2 + 2)
                        for f in range(2):
                            for s in range(S):
                                last = PE.transpose(psX[f][:, s * P:(s + 1) * P], gx[u][:, s, f * P:(f + 1) * P],
                                                    ident[:, :])
                            last.then_inc(turned_x, 1)

                    def layer1(i, u):
                        g = i * U + u
                        pe.wait_ge(eT_ok, g + 1 + 2)
                        for f in range(2):
                            pe.wait_ge(both1, g * 2 + f + 1)
                            last = PE.matmul(ps1[f][:, :], w1[:, 1, f * P:(f + 1) * P], eT[u % 2][:, :],
                                             start=True, stop=True)
                            last.then_inc(lin1, 1)

                    def layer2(i, u):
                        g = i * U + u
                        pe.wait_ge(act2, g * 2 + 2)
                        pe.wait_ge(masks, g + 1)
                        for f in range(2):
                            for s in range(S):
                                PE.matmul(ps2[f][:, s * P:(s + 1) * P],
                                          off[u % 2][:, s:s + 1].to_broadcast([P, P]), identb[:, :],
                                          start=(s == 0), stop=False, skip_group_check=True)
                        pe.wait_ge(act1, g * 2 + 2 + 2)
                        for f in range(2):
                            for k in range(2):
                                last = PE.matmul(ps2[f][:, :], w2[:, k, f * P:(f + 1) * P], h1[u % 2][k][:, :],
                                                 start=False, stop=(k == 1), skip_group_check=True)
                            last.then_inc(lin2, 1)

                    pe.sem_inc(lin2, 4)
                    pe.sem_inc(turned_x, 2 * U)
                    n = turns(pe)
                    turn_over(0, 0)
                    layer1(0, 0)
                    with pe.Fori(0, n) as i:
                        for u in range(U):
                            turn_over(*following(i, u))
                            layer1(*following(i, u))
                            layer2(i, u)

                @block.scalar
                def _(act):
                    def store(i, u):
                        g = i * U + u
                        act.wait_ge(turned, g + 1)
                        A.activation(eT[u % 2][:, :], psE[u % 2][:, :], ACT.Copy).then_inc(eT_ok, 1)

                    def relu1(i, u):
                        g = i * U + u
                        act.wait_ge(lin2, g * 2 + 2)
                        for f in range(2):
                            act.wait_ge(both1, g * 2 + f + 3)
                            A.activation(h1[u % 2][f][:, :], h0[f][:, :], ACT.Relu, bias=ba[:, f:f + 1]).then_inc(act1, 1)

                    def relu2(i, u):
                        g = i * U + u
                        for f in range(2):
                            act.wait_ge(summed, g * 2 + f + 1)
                            act.wait_ge(lin2, g * 2 + f + 5)
                            A.activation(flat(h2[f][:, :, :]), ps2[f][:, :], ACT.Relu, bias=bb[:, f:f + 1]
                                         ).then_inc(act2, 1)

                    act.sem_inc(eT_ok, 2)
                    act.sem_inc(act2, 2)
                    act.sem_inc(act1, 2)
                    n = turns(act)
                    store(0, 0)
                    relu1(0, 0)
                    with act.Fori(0, n) as i:
                        for u in range(U):
                            store(*following(i, u))
                            relu1(*following(i, u))
                            relu2(i, u)

                @block.vector
                def _(dve):
                    def fetch_sources(i, u):
                        g = i * U + u
                        for f in range(2):
                            dve.wait_ge(act1, g * 2 + f + 1)
                            dve.wait_ge(turned_x, g * 2 + f + 1 + 2 * U)
                            V.tensor_copy(h0[f][:, :], psX[f][:, :])

                    def join(i, u):
                        g = i * U + u
                        for f in range(2):
                            dve.wait_ge(lin1, g * 2 + f + 1)
                            V.tensor_tensor(h0[f][:, :], h0[f][:, :], ps1[f][:, :], ALU.add).then_inc(both1, 1)
                        dve.wait_ge(rec_in[u], (i + 1) * 16)
                        dve.wait_ge(lin2, g * 2 + 2)
                        V.tensor_copy(off[u % 2][:, :], rec[u][:, R_ANY:R_ANY + S].bitcast(fp32)).then_inc(masks, 1)

                    for c in rec_free:
                        dve.sem_inc(c, 1)
                    dve.sem_inc(summed, 2)
                    dve.sem_inc(both1, 2)
                    n = turns(dve)
                    V.memset(big[:, :], 0.0)
                    dve.drain()
                    fetch_sources(0, 0)
                    dve.drain()
                    join(0, 0)
                    with dve.Fori(0, n) as i:
                        for u in range(U):
                            g = i * U + u
                            fetch_sources(*following(i, u))
                            dve.drain()
                            join(*following(i, u))
                            dve.sem_inc(gate_v, 1)
                            j = dve.value_load(rec[u][0:1, R_J:R_J + 1], min_val=0, max_val=NT)
                            for f in range(2):
                                dve.wait_ge(act2, g * 2 + f + 3)
                                V.tensor_reduce(part[f][:, :], h2[f][:, :, :].rearrange("p s n -> p n s"), AX.X, ALU.add
                                                ).then_inc(summed, 1)
                            dve.drain()
                            for f in range(2):
                                t = total[:, ds(j, 1), f, :].rearrange("p a n -> p (a n)")
                                last = V.tensor_tensor(t, t, part[f][:, :], ALU.add)
                            dve.wait_ge(gathered[u], (i + 1) * 16 * (S + 1))
                            dve.sem_inc(gate_v, 1)
                            V.drain().then_inc(rec_free[u], 1)

            with ExitStack() as ph:
                W = 4
                inv = sb("inv", [P, NTP], fp32, ph)
                has = sb("has", [P, NTP], fp32, ph)
                su = [sb(f"su{v}", [P, 2, P], fp32, ph) for v in range(W)]
                xc = [sb(f"xc{v}", [P, P], fp32, ph) for v in range(W)]
                ag = [sb(f"ag{v}", [P, HID], fp32, ph) for v in range(W)]
                kT = [sb(f"kT{v}", [P, 3, P], fp32, ph) for v in range(W)]
                zz = [sb(f"zz{v}", [P, HID], fp32, ph) for v in range(W)]
                zT = [sb(f"zT{v}", [P, 2, P], fp32, ph) for v in range(W)]
                psa = [pb(f"psa{v}", [P, 2, HID], fp32, ph) for v in range(W)]
                psb = [pb(f"psb{v}", [P, 512], fp32, ph) for v in range(W)]
                pA, pZ = [p[:, 0, :] for p in psa], [p[:, 1, :] for p in psa]
                pT, pO = [p[:, 0:3 * P] for p in psb], [p[:, 3 * P:4 * P] for p in psb]
                total = big[:, :].rearrange("p (j f n) -> p j f n", j=NTP, f=2)
                fetched = sem("sums_fetched_n")
                aggp = sem("agg_product_n")
                agg = sem("agg_ready_n")
                tr1 = sem("inputs_transposed_n")
                st1 = sem("inputs_stored_n")
                lin = sem("hidden_linear_n")
                hid = sem("hidden_ready_n")
                tr2 = sem("hidden_transposed_n")
                st2 = sem("hidden_stored_n")
                fin = sem("mlp_output_n")
                added = sem("mlp_output_added_n")
                block = ph.enter_context(nc.Block())

                @block.scalar
                def _(act):
                    def tiles(i, vs):
                        for v in vs:
                            t = i * W + v
                            act.wait_ge(fin, i * W + 1)
                            A.activation(su[v][:, :, :], total[:, ds(t, 1), :, :].rearrange("p a f n -> p (a f) n"),
                                         ACT.Copy)
                            A.activation(xc[v][:, :], flat(xr[:, ds(t, 1), :]), ACT.Copy).then_inc(fetched, 1)
                        for v in vs:
                            act.wait_ge(tr1, i * W + v + 1)
                            A.activation(kT[v][:, :, :], pT[v].rearrange("p (a n) -> p a n", a=3),
                                         ACT.Copy).then_inc(st1, 1)
                        for v in vs:
                            act.wait_ge(tr2, i * W + v + 1)
                            A.activation(zT[v][:, :, :], pT[v][:, 0:2 * P].rearrange("p (a n) -> p a n", a=2),
                                         ACT.Copy).then_inc(st2, 1)

                    with act.Fori(0, NTP // W) as i:
                        tiles(i, range(W))
                    tiles(NTP // W, range(NTP % W))

                @block.tensor
                def _(pe):
                    for c in (fin,):
                        pe.sem_inc(c, 1)
                    def tiles(i, vs):
                        for v in vs:
                            pe.wait_ge(fetched, i * W + v + 1)
                            for k in range(2):
                                last = PE.matmul(pA[v], su[v][:, k, :], w3[:, k, :], start=(k == 0), stop=(k == 1))
                            last.then_inc(aggp, 1)
                        for v in vs:
                            pe.wait_ge(agg, i * W + v + 1)
                            PE.transpose(pT[v][:, 0:P], xc[v][:, :], ident[:, :])
                            for k in range(2):
                                last = PE.transpose(pT[v][:, (k + 1) * P:(k + 2) * P], ag[v][:, k * P:(k + 1) * P],
                                                    ident[:, :])
                            last.then_inc(tr1, 1)
                        for v in vs:
                            pe.wait_ge(st1, i * W + v + 1)
                            for k in range(3):
                                last = PE.matmul(pZ[v], kT[v][:, k, :], w4[:, k, :], start=(k == 0), stop=(k == 2))
                            last.then_inc(lin, 1)
                        for v in vs:
                            pe.wait_ge(hid, i * W + v + 1)
                            for k in range(2):
                                last = PE.transpose(pT[v][:, k * P:(k + 1) * P], zz[v][:, k * P:(k + 1) * P], ident[:, :])
                            last.then_inc(tr2, 1)
                        for v in vs:
                            pe.wait_ge(st2, i * W + v + 1)
                            pe.wait_ge(added, i * W + 1)
                            for k in range(2):
                                last = PE.matmul(pO[v], zT[v][:, k, :], w5[:, k, :], start=(k == 0), stop=(k == 1))
                            last.then_inc(fin, 1)

                    with pe.Fori(0, NTP // W) as i:
                        tiles(i, range(W))
                    tiles(NTP // W, range(NTP % W))

                @block.vector
                def _(dve):
                    for c in (added,):
                        dve.sem_inc(c, 1)
                    V.tensor_scalar(inv[:, :], degI[:, :], 1.0, None, ALU.max)
                    V.tensor_scalar(has[:, :], degI[:, :], 1.0, None, ALU.min)
                    dve.drain()
                    V.reciprocal(inv[:, :], inv[:, :])
                    dve.drain()
                    def tiles(i, vs):
                        for v in vs:
                            t = i * W + v
                            dve.wait_ge(aggp, i * W + v + 1)
                            V.tensor_scalar(ag[v][:, :], pA[v], inv[:, ds(t, 1)], None, ALU.mult)
                            V.drain()
                            V.scalar_tensor_tensor(ag[v][:, :], bcr[:, :], has[:, ds(t, 1)], ag[v][:, :],
                                                   ALU.mult, ALU.add).then_inc(agg, 1)
                        for v in vs:
                            dve.wait_ge(lin, i * W + v + 1)
                            V.tensor_tensor(zz[v][:, :], pZ[v], b4[:, :], ALU.add)
                            V.drain()
                            V.tensor_scalar(zz[v][:, :], zz[v][:, :], 0.0, None, ALU.max).then_inc(hid, 1)
                        for v in vs:
                            t = i * W + v
                            dve.wait_ge(fin, i * W + v + 2)
                            x_ = flat(xr[:, ds(t, 1), :])
                            V.tensor_tensor(x_, x_, pO[v], ALU.add).then_inc(added, 1)

                    with dve.Fori(0, NTP // W) as i:
                        tiles(i, range(W))
                    tiles(NTP // W, range(NTP % W))

            with ExitStack() as ph:
                mean = sb("mean2", [P, NTP], fp32, ph)
                var = sb("var2", [P, NTP], fp32, ph)
                ln_v, ln_s = normalised(xr[:, :, :], h[:, :, :], mean[:, :], var[:, :], "L2")
                block = ph.enter_context(nc.Block())

                @block.vector
                def _(dve):
                    V.tensor_tensor(xr[:, :, :], xr[:, :, :], bc(b5[:, :], 1, NTP), ALU.add)
                    dve.drain()
                    ln_v(dve)

                @block.scalar
                def _(act):
                    ln_s(act)

        fresh_semaphores()

        with ExitStack() as ph:
            w3 = sb("w3T_", [P, D], fp32, ph)
            iso = sb("iso", [P, NTP], fp32, ph)
            rec = [sb(f"rec_s{u}", [P, REC], i32, ph) for u in range(U)]
            spread = [sb(f"spread{v}", [P, S, P], fp32, ph) for v in range(2)]
            same = [sb(f"same{v}", [P, S, P], fp32, ph) for v in range(2)]
            before = [sb(f"before{v}", [P, S, P], fp32, ph) for v in range(2)]
            dup = [sb(f"dup{v}", [P, S], fp32, ph) for v in range(2)]
            away = [sb(f"away{v}", [P, S], fp32, ph) for v in range(2)]
            to = [sb(f"to{u}", [P, S], u32, ph) for u in range(U)]
            msg = [sb(f"msg{u}", [P, S, D], fp32, ph) for u in range(U)]
            spare = sb("spare", [P, 1], fp32, ph)
            blank = sb("blank", [P, D], fp32, ph)
            blank_ok = sem("blank_ready")
            scaled = [sb(f"scaled{v}", [P, D], fp32, ph) for v in range(2)]
            psR = [pb(f"psR{v}", [P, 512], fp32, ph) for v in range(2)]
            psM = [pb(f"psM{v}", [P, 512], fp32, ph) for v in range(2)]
            w_in = sem("w3_in")
            root = sem("root_s")
            deg_ok = sem("deg_clamped_s")
            x_out = sem("x3_stored")
            rec_in = [sem(f"rec_in_s{u}") for u in range(U)]
            spr_ok = sem("sources_spread")
            rows_ok = sem("sources_in_rows")
            same_ok = sem("equality_ready")
            to_ok = sem("targets_ready")
            msg_ps = sem("messages_summed")
            msg_ok = sem("messages_stored")
            sc_ok = sem("scaled_ready")
            used = sem("slots_used_s")
            added = [sem(f"added_{s}") for s in range(S)]
            gate = sem("gate_s")
            passed = sem("adds_before_this_done")
            gate_v = sem("gate_sv")

            with nc.Block() as block:
                @block.sync
                def _(sp):
                    sp.dma_start(w3[:, :], w3T).then_inc(w_in, 16)
                    sp.wait_ge(w_in, 16)

                @block.gpsimd
                def _(pool):
                    for j in range(NTP):
                        G.indirect_dma_start(out=x3_d, out_offset=bass.IndirectOffsetOnAxis(
                            ap=nid[:, j:j + 1].bitcast(u32), axis=0), in_=xr[:, j, :], in_offset=None).then_inc(x_out, 16)
                    pool.wait_ge(blank_ok, 1)
                    for s in range(S):
                        pool.dma_start(sum_d[s][NPAD:ROWS, :], blank[:, :]).then_inc(added[s], 16)
                    pool.wait_ge(x_out, 16 * NTP)
                    for s in range(S):
                        pool.wait_ge(added[s], 16)

                @block.vector
                def _(dve):
                    V.memset(blank[:, :], 0.0).then_inc(blank_ok, 1)
                    V.tensor_scalar(iso[:, :], degO[:, :], 1.0, None, ALU.max).then_inc(deg_ok, 1)
                    V.tensor_scalar(spare[:, :], place[:, :], float(NT * P), None, ALU.add)
                    dve.wait_ge(root, 1)
                    V.reciprocal(iso[:, :], iso[:, :])
                    dve.drain()
                    V.tensor_tensor(h[:, :, :], xr[:, :, :], bc(iso[:, :], 2, D), ALU.mult)

                @block.scalar
                def _(act):
                    act.wait_ge(deg_ok, 1)
                    A.activation(iso[:, :], iso[:, :], ACT.Sqrt).then_inc(root, 1)

            with nc.Block() as block:
                @block.sync
                def _(sp):
                    n = turns(sp)
                    with sp.Fori(0, n) as i:
                        for u in range(U):
                            sp.wait_ge(used, i * U + u + 1)
                            sp.dma_start(rec[u][:, :], rec_d[ds(i * U + u, 1), :, :]
                                         .rearrange("a p w -> (a p) w")).then_inc(rec_in[u], 16)

                @block.tensor
                def _(pe):
                    pe.sem_inc(msg_ps, 2)
                    n = turns(pe)
                    with pe.Fori(0, n) as i:
                        for u in range(U):
                            g, v = i * U + u, u % 2
                            if v == 0:
                                for w in range(2):
                                    pe.wait_ge(spr_ok, g + w + 1)
                                    for s in range(S):
                                        last = PE.transpose(psR[w][:, s * P:(s + 1) * P], spread[w][:, s, :], ident[:, :])
                                    last.then_inc(rows_ok, 1)
                            pe.wait_ge(same_ok, g + 1)
                            pe.wait_ge(sc_ok, g + 1)
                            pe.wait_ge(msg_ok, g + 1)
                            for s in range(S):
                                last = PE.matmul(psM[v][:, s * P:(s + 1) * P], same[v][:, s, :], scaled[v][:, :],
                                                 start=True, stop=True)
                            last.then_inc(msg_ps, 1)

                @block.scalar
                def _(act):
                    act.sem_inc(msg_ok, 2)
                    n = turns(act)
                    with act.Fori(0, n) as i:
                        for u in range(U):
                            g, v = i * U + u, u % 2
                            act.wait_ge(msg_ps, g + 3)
                            act.wait_ge(passed, g * S + 2 * S)
                            A.activation(flat(msg[u][:, :, :]), psM[v][:, :], ACT.Copy).then_inc(msg_ok, 1)

                @block.vector
                def _(dve):
                    dve.sem_inc(used, U)
                    n = turns(dve)
                    with dve.Fori(0, n) as i:
                        for u in range(U):
                            g, v = i * U + u, u % 2
                            if v == 0:
                                for w in range(2):
                                    dve.wait_ge(rec_in[u + w], (i + 1) * 16)
                                    dve.sem_inc(gate_v, 1)
                                    j = dve.value_load(rec[u + w][0:1, R_J:R_J + 1], min_val=0, max_val=NT)
                                    V.tensor_copy(spread[w][:, :, :], bc(rec[u + w][:, R_SUM:R_SUM + S].bitcast(fp32), 2, P)
                                                  ).then_inc(spr_ok, 1)
                                    dve.wait_ge(msg_ps, g + w + 1)
                                    V.tensor_copy(scaled[w][:, :], flat(h[:, ds(j, 1), :])).then_inc(sc_ok, 1)
                            srcs = rec[u][:, R_SUM:R_SUM + S].bitcast(fp32)
                            V.tensor_tensor(away[v][:, :], spare[:, :].to_broadcast([P, S]), srcs, ALU.subtract)
                            dve.wait_ge(msg_ps, g + 1)
                            dve.wait_ge(rows_ok, g + 1)
                            V.tensor_tensor(same[v][:, :, :], psR[v][:, :].rearrange("p (s n) -> p s n", s=S),
                                            bc(srcs, 2, P), ALU.is_equal).then_inc(same_ok, 1)
                            dve.drain()
                            V.tensor_tensor(before[v][:, :, :], same[v][:, :, :], bc(lower[:, :], 1, S), ALU.mult)
                            dve.drain()
                            V.tensor_reduce(dup[v][:, :], before[v][:, :, :], AX.X, ALU.max)
                            dve.drain()
                            V.tensor_tensor(away[v][:, :], away[v][:, :], dup[v][:, :], ALU.mult)
                            dve.drain()
                            dve.wait_ge(passed, g * S + 2 * S)
                            V.tensor_tensor(to[u][:, :], away[v][:, :], srcs, ALU.add).then_inc(to_ok, 1)
                            V.drain().then_inc(used, 1)

                @block.gpsimd
                def _(pool):
                    pool.sem_inc(passed, S * U)
                    n = turns(pool)
                    with pool.Fori(0, n) as i:
                        for u in range(U):
                            g = i * U + u
                            pool.wait_ge(to_ok, g + 1)
                            pool.wait_ge(msg_ok, g + 3)
                            for s in range(S):
                                pool.wait_ge(added[s], g * 16 + 16)
                                pool.sem_inc(passed, 1)
                                G.indirect_dma_start(out=sum_d[s], out_offset=bass.IndirectOffsetOnAxis(
                                    ap=to[u][:, s:s + 1], axis=0), in_=msg[u][:, s, :], in_offset=None,
                                    compute_op=ALU.add).then_inc(added[s], 16)
                    for s in range(S):
                        pool.wait_ge(added[s], n * 16 * U + 16)
                    pool.sem_inc(gate, 1)

            with ExitStack() as fi:
                q = [sb(f"q{s}", [P, NT, D], fp32, fi) for s in range(2)]
                xn = sb("xn", [P, NT, D], fp32, fi)
                ison = sb("ison", [P, NT], fp32, fi)
                hc = [sb(f"hcf{v}", [P, P], fp32, fi) for v in range(2)]
                ht = [sb(f"htf{v}", [P, P], fp32, fi) for v in range(2)]
                mean = sb("mean3", [P, NT], fp32, fi)
                var = sb("var3", [P, NT], fp32, fi)
                pt = [pb(f"ptf{v}", [P, 512], fp32, fi) for v in range(2)]
                pm = [pb(f"pmf{v}", [P, 512], fp32, fi) for v in range(2)]
                xn_in = sem("xn_in")
                q_in = sem("sums_in")
                q_used = sem("sums_used")
                mroot = sem("root_f")
                agg_ok = sem("aggregate_ready")
                fetched = sem("fetched_f")
                turned = sem("turned_f")
                stored = sem("stored_f")
                mult = sem("mult_f")
                relud = sem("relu_f")
                out_ok = sem("out_ready")
                out_out = sem("out_stored")
                sq = h[:, 0:NT, :]
                agg = q[0]

                with nc.Block() as block:
                    @block.sync
                    def _(sp):
                        def rows(t):
                            return t[0:NT * P, :].rearrange("(j p) c -> p j c", p=P)
                        sp.dma_start(xn[:, :, :], rows(x3_d)).then_inc(xn_in, 16)
                        sp.dma_start(q[0][:, :, :], rows(sum_d[0])).then_inc(q_in, 16)
                        for s in range(1, S):
                            if s > 1:
                                sp.wait_ge(q_used, s - 1)
                            sp.dma_start(q[1][:, :, :], rows(sum_d[s])).then_inc(q_in, 16)
                        sp.wait_ge(xn_in, 16)

                    @block.scalar
                    def _(act):
                        A.activation(ison[:, :], degOn[:, :], ACT.Sqrt).then_inc(mroot, 1)

                    @block.vector
                    def _(dve):
                        for s in range(1, S):
                            dve.wait_ge(q_in, 16 * (s + 1))
                            V.tensor_tensor(agg[:, :, :], agg[:, :, :], q[1][:, :, :], ALU.add).then_inc(q_used, 1)
                            dve.drain()
                        dve.wait_ge(mroot, 1)
                        V.reciprocal(ison[:, :], ison[:, :])
                        dve.drain()
                        V.tensor_tensor(agg[:, :, :], agg[:, :, :], bc(ison[:, :], 2, D), ALU.mult)

                def per_tile(eng, body):
                    with eng.Fori(0, NT // 2) as i:
                        body(i, range(2))
                    body(NT // 2, range(1))

                with nc.Block() as block:
                    @block.scalar
                    def _(act):
                        act.sem_inc(stored, 1)
                        def body(i, vs):
                            for v in vs:
                                act.wait_ge(turned, i * 2 + 1)
                                A.activation(hc[v][:, :], flat(agg[:, ds(i * 2 + v, 1), :]), ACT.Copy).then_inc(fetched, 1)
                            for v in vs:
                                act.wait_ge(turned, i * 2 + v + 2)
                                act.wait_ge(mult, i * 2 + 1)
                                A.activation(ht[v][:, :], pt[v][:, 0:P], ACT.Copy).then_inc(stored, 1)
                        per_tile(act, body)

                    @block.tensor
                    def _(pe):
                        pe.sem_inc(turned, 1)
                        pe.sem_inc(mult, 1)
                        def body(i, vs):
                            for v in vs:
                                pe.wait_ge(fetched, i * 2 + v + 1)
                                pe.wait_ge(stored, i * 2 + 1)
                                PE.transpose(pt[v][:, 0:P], hc[v][:, :], ident[:, :]).then_inc(turned, 1)
                            for v in vs:
                                pe.wait_ge(stored, i * 2 + v + 2)
                                pe.wait_ge(relud, i * 2 + 1)
                                PE.matmul(pm[v][:, 0:D], ht[v][:, :], w3[:, :], start=True, stop=True).then_inc(mult, 1)
                        per_tile(pe, body)

                    @block.vector
                    def _(dve):
                        dve.sem_inc(relud, 1)
                        def body(i, vs):
                            for v in vs:
                                dve.wait_ge(mult, i * 2 + v + 2)
                                x_ = flat(xn[:, ds(i * 2 + v, 1), :])
                                V.scalar_tensor_tensor(x_, pm[v][:, 0:D], 0.0, x_, ALU.max, ALU.add).then_inc(relud, 1)
                        per_tile(dve, body)

                ln_v, ln_s = normalised(xn[:, :, :], sq, mean[:, :], var[:, :], "L3")
                with nc.Block() as block:
                    @block.vector
                    def _(dve):
                        ln_v(dve)
                        V.drain().then_inc(out_ok, 1)

                    @block.scalar
                    def _(act):
                        ln_s(act)

                    @block.sync
                    def _(sp):
                        sp.wait_ge(out_ok, 1)
                        full = N // P
                        sp.dma_start(out[0:full * P, :].rearrange("(j p) c -> p j c", p=P),
                                     xn[:, 0:full, :]).then_inc(out_out, 16)
                        sp.dma_start(out[full * P:N, :], xn[0:N - full * P, full, :]).then_inc(out_out, 16)
                        sp.wait_ge(out_out, 32)


def lay_out(inputs):
    import numpy as np
    g = {k: np.asarray(v) for k, v in inputs.items()}

    def padded(a, rows, value=0):
        return np.concatenate([a, np.full((rows - a.shape[0],) + a.shape[1:], value, a.dtype)])

    arrays = {"x": padded(g["x"], NPAD)}
    for name in ("src", "dst"):
        arrays[name] = padded(g[name], EPAD, NT * P).reshape(P, EC)
    s, t = padded(g["src"], E + S + 1), padded(g["edge_type_4"], E + S + 1)
    arrays["windows"] = np.stack([a[k:k + E + 1] for a in (s, t) for k in range(S)], axis=1)
    a = padded(g["edge_attr_128"], E + S + 1)
    arrays["edge_windows"] = np.stack([a[k:k + E + 1] for k in range(S)], axis=1).reshape(E + 1, S * D)
    W0 = g["L0_gnn_W"]
    arrays["W0"] = W0.transpose(1, 0, 2)
    arrays["W0T"] = W0.transpose(2, 0, 1)
    att = g["L0_gnn_att_vectors"]
    for name, part in (("attI", att[:, :, :C]), ("attJ", att[:, :, C:])):
        a = np.zeros((H, C, H, K5), np.float32)
        for h in range(H):
            a[h, :, h, :] = part[:, h, :].T
        arrays[name] = a.reshape(D, H * K5)
    arrays["probs"] = g["L0_gnn_confounder_probs"]
    arrays["importance"] = g["L0_gnn_edge_importance"]
    arrays["bias0"] = g["L0_gnn_bias"]
    for name in ("Ws", "Wd"):
        arrays[name] = g["L1_gnn_" + name].transpose(1, 0, 2)
        arrays[name + "T"] = g["L1_gnn_" + name].transpose(2, 0, 1)
    for name, part in (("attS", g["L1_gnn_att_s"]), ("attD", g["L1_gnn_att_d"])):
        a = np.zeros((H, C, 3, H), np.float32)
        for h in range(H):
            a[h, :, :, h] = part[:, h, :].T
        arrays[name] = a.reshape(D, 3, H)
    arrays["bias1"] = g["L1_gnn_b"]
    arrays["w1a"] = g["L2_gnn_w1a"].reshape(2, P, HID).transpose(1, 0, 2)
    arrays["b1a"] = g["L2_gnn_b1a"].reshape(2, P).T
    arrays["w1b"] = g["L2_gnn_w1b"].reshape(2, P, HID).transpose(1, 0, 2)
    arrays["b1b"] = g["L2_gnn_b1b"].reshape(2, P).T
    arrays["w1c"] = g["L2_gnn_w1c"].reshape(2, P, HID).transpose(1, 0, 2)
    arrays["b1c"] = g["L2_gnn_b1c"]
    arrays["w2a"] = g["L2_gnn_w2a"].reshape(3, P, HID).transpose(1, 0, 2)
    arrays["b2a"] = g["L2_gnn_b2a"]
    arrays["w2b"] = g["L2_gnn_w2b"].reshape(2, P, D).transpose(1, 0, 2)
    arrays["b2b"] = g["L2_gnn_b2b"]
    arrays["w3T"] = g["L3_gnn_weight"].T
    arrays = {f"in_{k}": np.ascontiguousarray(v) for k, v in arrays.items()}
    return arrays, None


def kernel(**inputs):
    import numpy as np
    import concourse.bacc as bacc
    from concourse.bass_utils import run_bass_kernel_spmd

    nc = bacc.Bacc("TRN2", target_bir_lowering=False, num_devices=1)
    arrays, _ = lay_out(inputs)
    args = [nc.dram_tensor(k, a.shape, mybir.dt.from_np(a.dtype), kind="ExternalInput").ap()
            for k, a in arrays.items()]
    out = nc.dram_tensor("out", [N, D], mybir.dt.float32, kind="ExternalOutput").ap()
    gnn(nc, *args, out)
    r = run_bass_kernel_spmd(nc, [arrays], core_ids=[0])
    return r.results[0]["out"]
```
